# Optimizing a Trainium2 kernel written in Bass

```python
import numpy as np
import jax
import jax.numpy as jnp

def _softmax(x, axis=-1):
    return jax.nn.softmax(x, axis=axis)

def _gelu(x):
    return jax.nn.gelu(x, approximate=True)

def _silu(x):
    return jax.nn.silu(x)

def _sigmoid(x):
    return jax.nn.sigmoid(x)

def _layernorm(x, axis=-1, eps=1e-05):
    m = jnp.mean(x, axis=axis, keepdims=True)
    v = jnp.var(x, axis=axis, keepdims=True)
    return (x - m) / jnp.sqrt(v + eps)

def _scatter_add(tgt, idx, src, axis=0):
    return tgt.at[idx].add(src)

def _segment_sum(src, seg, n):
    return jax.ops.segment_sum(src, seg, n)
kernel_name = 'mk_gnn_ffn_d1_gnn_r32_6dbdd2'

def setup_inputs(seed: int=0):
    np.random.seed(seed)
    _w = jnp.asarray

    def _rec_inputs():
        import jax
        import jax.numpy as jnp
        _gk = jax.random.key(seed)
        x = -6.415e-05 + 1 * jax.random.normal(jax.random.fold_in(_gk, 1), (625, 512), jnp.float32)
        src = jax.random.randint(jax.random.fold_in(_gk, 2), (20000,), 0, 625, jnp.int32)
        dst = jax.random.randint(jax.random.fold_in(_gk, 3), (20000,), 0, 625, jnp.int32)
        _o = jnp.argsort(dst, stable=True)
        src = src[_o]
        dst = dst[_o]
        edge_attr_8 = -0.000521468 + 0.999954 * jax.random.normal(jax.random.fold_in(_gk, 12), (20000, 8), jnp.float32)
        edge_attr_8_n2 = -0.000521468 + 0.999954 * jax.random.normal(jax.random.fold_in(_gk, 13), (20000, 8), jnp.float32)
        return (x, src, dst, edge_attr_8, edge_attr_8_n2)
    x, src, dst, edge_attr_8, edge_attr_8_n2 = _rec_inputs()

    def _L0_gnn_setup():
        import jax, jax.numpy as jnp
        import numpy as np
        N = 625
        E = 20000
        D = 512
        H = 8
        DH = D // H
        EPS = 1e-05

        def layer_norm(x, g, b):
            mu = x.mean(-1, keepdims=True)
            var = ((x - mu) ** 2).mean(-1, keepdims=True)
            return (x - mu) * jax.lax.rsqrt(var + EPS) * g + b
        key = jax.random.key(seed)
        ks = jax.random.split(key, 12)
        return dict(node_feature=jax.random.normal(ks[0], (N, D), jnp.float32), src=jax.random.randint(ks[1], (E,), 0, N, dtype=jnp.int32), dst=jax.random.randint(ks[2], (E,), 0, N, dtype=jnp.int32), dist_attn=jax.random.normal(ks[3], (E, H), jnp.float32), path_attn=jax.random.normal(ks[4], (E, H), jnp.float32), Wqkv=jax.random.normal(ks[5], (D, 3 * D), jnp.float32) / np.float32(np.sqrt(D)), bqkv=jnp.zeros((3 * D,), jnp.float32), Wo=jax.random.normal(ks[6], (D, D), jnp.float32) / np.float32(np.sqrt(D)), bo=jnp.zeros((D,), jnp.float32), ln1_g=jnp.ones((D,), jnp.float32), ln1_b=jnp.zeros((D,), jnp.float32), W1=jax.random.normal(ks[7], (D, 4 * D), jnp.float32) / np.float32(np.sqrt(D)), b1=jnp.zeros((4 * D,), jnp.float32), W2=jax.random.normal(ks[8], (4 * D, D), jnp.float32) / np.float32(np.sqrt(4 * D)), b2=jnp.zeros((D,), jnp.float32), ln2_g=jnp.ones((D,), jnp.float32), ln2_b=jnp.zeros((D,), jnp.float32))
    _L0_gnn_all = _L0_gnn_setup()
    _L0_gnn_in = {k: v for k, v in _L0_gnn_all.items() if k in ('Wqkv', 'bqkv', 'Wo', 'bo', 'ln1_g', 'ln1_b', 'W1', 'b1', 'W2', 'b2', 'ln2_g', 'ln2_b')}
    del _L0_gnn_all

    def _L0_ffn_setup():
        import jax, jax.numpy as jnp
        import numpy as np
        DIM = 512
        HID = 1024
        E = 8
        K = 2
        B, S = (4, 64)
        key = jax.random.key(seed)
        ks = jax.random.split(key, 10)
        sd = DIM ** (-0.5)
        sh = HID ** (-0.5)
        return {'x': jax.random.normal(ks[0], (B, S, DIM), dtype=jnp.float32), 'gate_w': jax.random.normal(ks[1], (E, DIM), dtype=jnp.float32) * sd, 'biases': jnp.zeros((E,), dtype=jnp.float32), 'w1': jax.random.normal(ks[2], (E, DIM, HID), dtype=jnp.float32) * sd, 'w3': jax.random.normal(ks[3], (E, DIM, HID), dtype=jnp.float32) * sd, 'w2': jax.random.normal(ks[4], (E, HID, DIM), dtype=jnp.float32) * sh, 'sw1': jax.random.normal(ks[5], (DIM, HID), dtype=jnp.float32) * sd, 'sw3': jax.random.normal(ks[6], (DIM, HID), dtype=jnp.float32) * sd, 'sw2': jax.random.normal(ks[7], (HID, DIM), dtype=jnp.float32) * sh}
    _L0_ffn_all = _L0_ffn_setup()
    _L0_ffn_in = {k: v for k, v in _L0_ffn_all.items() if k in ('gate_w', 'biases', 'w1', 'w3', 'w2', 'sw1', 'sw3', 'sw2')}
    del _L0_ffn_all
    return {'x': x, 'src': src, 'dst': dst, 'edge_attr_8': edge_attr_8, 'edge_attr_8_n2': edge_attr_8_n2, 'L0_gnn_Wqkv': _L0_gnn_in['Wqkv'], 'L0_gnn_bqkv': _L0_gnn_in['bqkv'], 'L0_gnn_Wo': _L0_gnn_in['Wo'], 'L0_gnn_bo': _L0_gnn_in['bo'], 'L0_gnn_ln1_g': _L0_gnn_in['ln1_g'], 'L0_gnn_ln1_b': _L0_gnn_in['ln1_b'], 'L0_gnn_W1': _L0_gnn_in['W1'], 'L0_gnn_b1': _L0_gnn_in['b1'], 'L0_gnn_W2': _L0_gnn_in['W2'], 'L0_gnn_b2': _L0_gnn_in['b2'], 'L0_gnn_ln2_g': _L0_gnn_in['ln2_g'], 'L0_gnn_ln2_b': _L0_gnn_in['ln2_b'], 'L0_ffn_gate_w': _L0_ffn_in['gate_w'], 'L0_ffn_biases': _L0_ffn_in['biases'], 'L0_ffn_w1': _L0_ffn_in['w1'], 'L0_ffn_w3': _L0_ffn_in['w3'], 'L0_ffn_w2': _L0_ffn_in['w2'], 'L0_ffn_sw1': _L0_ffn_in['sw1'], 'L0_ffn_sw3': _L0_ffn_in['sw3'], 'L0_ffn_sw2': _L0_ffn_in['sw2']}

def reference(x, src, dst, edge_attr_8, edge_attr_8_n2, L0_gnn_Wqkv, L0_gnn_bqkv, L0_gnn_Wo, L0_gnn_bo, L0_gnn_ln1_g, L0_gnn_ln1_b, L0_gnn_W1, L0_gnn_b1, L0_gnn_W2, L0_gnn_b2, L0_gnn_ln2_g, L0_gnn_ln2_b, L0_ffn_gate_w, L0_ffn_biases, L0_ffn_w1, L0_ffn_w3, L0_ffn_w2, L0_ffn_sw1, L0_ffn_sw3, L0_ffn_sw2):
    import jax
    import jax.numpy as jnp

    def _L0_gnn_ref(node_feature, src, dst, dist_attn, path_attn, Wqkv, bqkv, Wo, bo, ln1_g, ln1_b, W1, b1, W2, b2, ln2_g, ln2_b):
        import jax, jax.numpy as jnp
        import numpy as np
        N = 625
        E = 20000
        D = 512
        H = 8
        DH = D // H
        EPS = 1e-05

        def layer_norm(x, g, b):
            mu = x.mean(-1, keepdims=True)
            var = ((x - mu) ** 2).mean(-1, keepdims=True)
            return (x - mu) * jax.lax.rsqrt(var + EPS) * g + b
        h = layer_norm(node_feature, ln1_g, ln1_b)
        qkv = (h @ Wqkv + bqkv).reshape(N, 3, H, DH)
        q = qkv[:, 0] * D ** (-0.5)
        k = qkv[:, 1]
        v = qkv[:, 2]
        logits = jnp.einsum('ehd,ehd->eh', q[src], k[dst])
        a = logits + dist_attn + path_attn
        mx = jax.ops.segment_max(a, dst, num_segments=N)
        e = jnp.exp(a - mx[dst])
        s = jax.ops.segment_sum(e, dst, num_segments=N)
        sa = e / s[dst]
        msg = v[src] * sa[:, :, None]
        agg = jax.ops.segment_sum(msg, dst, num_segments=N).reshape(N, D)
        x = agg @ Wo + bo
        h1 = node_feature + x
        h2 = layer_norm(h1, ln2_g, ln2_b)
        h2 = jax.nn.gelu(h2 @ W1 + b1, approximate=False) @ W2 + b2
        return h1 + h2

    def _L0_ffn_ref(x, gate_w, biases, w1, w3, w2, sw1, sw3, sw2):
        import jax, jax.numpy as jnp
        import numpy as np
        DIM = 512
        HID = 1024
        E = 8
        K = 2
        B, S = (4, 64)
        Bb, Ss, D = x.shape
        xt = x.reshape(Bb * Ss, D)
        shared = jax.nn.silu(xt @ sw1) * (xt @ sw3) @ sw2
        scores = xt @ gate_w.T
        _, idx = jax.lax.top_k(scores + biases, K)
        topv, _ = jax.lax.top_k(scores, K)
        p = jax.nn.sigmoid(topv)
        p = p / jnp.sum(p, axis=-1, keepdims=True)
        h = jax.nn.silu(jnp.einsum('td,edh->eth', xt, w1)) * jnp.einsum('td,edh->eth', xt, w3)
        y = jnp.einsum('eth,ehd->etd', h, w2)
        onehot = jax.nn.one_hot(idx, E, dtype=xt.dtype)
        comb = jnp.einsum('tk,tke->te', p, onehot)
        out = jnp.einsum('te,etd->td', comb, y) + shared
        return out.reshape(Bb, Ss, D)
    x = x + _L0_gnn_ref(_layernorm(x, axis=-1), src, dst, edge_attr_8, edge_attr_8_n2, L0_gnn_Wqkv, L0_gnn_bqkv, L0_gnn_Wo, L0_gnn_bo, L0_gnn_ln1_g, L0_gnn_ln1_b, L0_gnn_W1, L0_gnn_b1, L0_gnn_W2, L0_gnn_b2, L0_gnn_ln2_g, L0_gnn_ln2_b)
    x = x + _L0_ffn_ref(_layernorm(x, axis=-1)[None], L0_ffn_gate_w, L0_ffn_biases, L0_ffn_w1, L0_ffn_w3, L0_ffn_w2, L0_ffn_sw1, L0_ffn_sw3, L0_ffn_sw2)[0]
    return x

_drawn_inputs = setup_inputs


def setup_inputs(seed=0):
    import zlib

    import numpy as np

    out = dict(_drawn_inputs(seed))
    spreads = {'L0_gnn_bqkv': (0.0, 0.1),
     'L0_gnn_bo': (0.0, 0.1),
     'L0_gnn_ln1_g': (1.0, 0.2),
     'L0_gnn_ln1_b': (0.0, 0.1),
     'L0_gnn_b1': (0.0, 0.1),
     'L0_gnn_b2': (0.0, 0.1),
     'L0_gnn_ln2_g': (1.0, 0.2),
     'L0_gnn_ln2_b': (0.0, 0.1),
     'L0_ffn_biases': (0.0, 0.1)}
    factors = {}
    for name, (base, spread) in spreads.items():
        noise = np.random.default_rng([zlib.crc32(name.encode()), seed]).standard_normal(out[name].shape)
        drawn = base * np.exp(spread * noise) if base else spread * noise
        out[name] = jnp.asarray(drawn.astype(out[name].dtype))
    for name, factor in factors.items():
        out[name] = (out[name] * factor).astype(out[name].dtype)
    return out
```

```python
from contextlib import ExitStack

import concourse.bass as bass
from concourse import mybir

P = 128
F32 = mybir.dt.float32
I32 = mybir.dt.int32
U32 = mybir.dt.uint32
ALU = mybir.AluOpType
ACT = mybir.ActivationFunctionType
AX = mybir.AxisListType

N = 625
D = 512
DC = D // P
H = 8
DH = D // H
NE = 20000
FF = 4 * D
HID = 1024
HC = HID // P
EX = 8
NT = -(-N // P)
NP = NT * P
HALF = NP // 2
LAST = N - (NT - 1) * P
EPS = 1e-5
BN = P // H
NB = NP // BN
BPT = P // BN
CT = 5
CHUNK = CT * P
EP, EJ = 125, NE // 125
REC = 2 + H
BIG = 1e30
TINY = 2.0 ** -64
SLOT = 4096


def node_tiles(ap):
    full = ap[0:(NT - 1) * P, :].rearrange("(t p) n -> p t n", p=P)
    return full, ap[(NT - 1) * P:N, :]


def wait_past(eng, sem, value):
    if not isinstance(value, int) or value > 0:
        eng.wait_ge(sem, value)


def program(nc, x, src, dst, edge_attr_8, edge_attr_8_n2, Wqkv, bqkv, Wo, bo, ln1_g, ln1_b, W1, b1, W2, b2,
            ln2_g, ln2_b, gate_w, biases, w1, w3, w2, sw1, sw3, sw2, out):
    with ExitStack() as ctx:
        def sb(name, shape, dt=F32):
            return ctx.enter_context(nc.sbuf_tensor(name, shape, dt))

        def sem(name):
            return ctx.enter_context(nc.semaphore(name))

        wts = sb("wts", [P, 6 * SLOT])
        big = sb("big", [P, 16, NP])
        xs = sb("xs", [P, NT, D])
        hT = sb("hT", [P, DC, NP])
        vs = sb("vs", [P, NT, D])
        work = sb("work", [P, 12 * NP])
        iota_n = sb("iota_n", [P, NP])
        ident = sb("ident", [P, P])
        ones = sb("ones", [P, P])
        XM = sb("XM", [P, 2, P])
        small = sb("small", [P, 64])
        tab_f = sb("tab_f", [1, 3 * NB + 1])
        tab = sb("tab", [1, 2 * NB + 1], I32)
        psum = [ctx.enter_context(nc.psum_tensor(f"ps{i}", [P, 512], F32)) for i in range(8)]
        logits_d = nc.dram_tensor("logits_scratch", [NB, H, BN, NP], F32, kind="Internal").ap()
        rec_d = nc.dram_tensor("record_scratch", [NE + CHUNK, REC], F32, kind="Internal").ap()

        edge_records(nc, sem, src, dst, edge_attr_8, edge_attr_8_n2, rec_d, wts, iota_n, ident, ones, psum,
                     tab_f, tab, small)
        projections(nc, sem, x, Wqkv, bqkv, Wo, W1, W2, ln1_g, ln1_b, logits_d, wts, big, xs, hT, vs, work, small,
                    ident, psum)
        attention(nc, sem, rec_d, logits_d, big, hT, vs, work, iota_n, ident, ones, XM, tab, small, psum)
        attention_any(nc, sem, rec_d, logits_d, big, hT, vs, work, iota_n, ident, ones, XM, tab, small, psum)
        feed_forward(nc, sem, x, bo, ln2_g, ln2_b, b1, b2, wts, big, xs, hT, vs, work, small, ident, psum)
        experts(nc, sem, gate_w, biases, w1, w3, w2, sw1, sw3, sw2, out, wts, big, xs, hT, vs, work, iota_n, small,
                ident, psum)


class Order:

    def __init__(self, eng, sem, base=0):
        self.eng, self.sem, self.base, self.n = eng, sem, base, 0

    def done(self, ins):
        ins.then_inc(self.sem, 1)
        self.n += 1

    def wait(self):
        self.eng.wait_ge(self.sem, self.base + self.n)

    def link(self, ins):
        self.done(ins)
        self.wait()


def edge_records(nc, sem, src, dst, edge_attr_8, edge_attr_8_n2, rec_d, wts, iota_n, ident, ones, psum, tab_f, tab,
                 small):
    ints = wts[0:EP, 0:2 * EJ].bitcast(I32).rearrange("p (a j) -> p a j", a=2)
    blk_i = wts[0:EP, 320:320 + EJ].bitcast(I32)
    blk = wts[0:EP, 480:480 + EJ]
    near = wts[0:EP, 640:640 + EJ * H]
    path = wts[0:EP, 1920:1920 + EJ * H]
    rec = wts[0:EP, 3200:3200 + EJ * REC].rearrange("p (j c) -> p j c", c=REC)
    eq = wts[0:EP, 4800:4800 + EJ * NB].rearrange("p (j b) -> p j b", b=NB)
    pos = wts[0:EP, 11200:11200 + EJ * NB].rearrange("p (j b) -> p j b", b=NB)
    e_up = wts[0:EP, 17600:17600 + EJ]
    e_down = wts[0:EP, 17760:17760 + EJ]
    ends = wts[0:EP, 17920:17920 + 2 * NB]
    pad = wts[:, 18000:18000 + CT * REC]
    ends_t = small[0:2 * NB, 0:1]
    loaded, consts, own, turned, stored, tabled, poolown = map(
        sem, ("edge_loaded", "edge_consts", "edge_own", "edge_turned", "edge_stored", "edge_tabled", "edge_poolown"))

    with nc.Block() as block:
        @block.sync
        def _(sp):
            sp.dma_start(ints[:, 0, :], src.rearrange("(p j) -> p j", j=EJ)).then_inc(loaded, 16)
            sp.dma_start(ints[:, 1, :], dst.rearrange("(p j) -> p j", j=EJ)).then_inc(loaded, 16)
            sp.dma_start(near, edge_attr_8.rearrange("(p j) h -> p (j h)", j=EJ)).then_inc(loaded, 16)
            sp.dma_start(path, edge_attr_8_n2.rearrange("(p j) h -> p (j h)", j=EJ)).then_inc(loaded, 16)
            sp.wait_ge(consts, 7)
            sp.dma_start(rec_d[NE:NE + CHUNK, :].rearrange("(p t) c -> p (t c)", t=CT), pad).then_inc(stored, 16)
            sp.wait_ge(own, 3)
            sp.dma_start(rec_d[0:NE, :].rearrange("(p j) c -> p (j c)", j=EJ),
                         rec.rearrange("p j c -> p (j c)")).then_inc(stored, 16)
            sp.wait_ge(stored, 32)

        @block.gpsimd
        def _(pool):
            exact = dict(allow_small_or_imprecise_dtypes=True)
            pool.memset(ident[:, :], 0.0).then_inc(poolown, 1)
            pool.iota(iota_n[:, :], [[1, NP]], base=0, channel_multiplier=0, **exact).then_inc(consts, 1)
            pool.iota(e_up, [[1, EJ]], base=1, channel_multiplier=EJ, **exact).then_inc(consts, 1)
            pool.iota(e_down, [[-1, EJ]], base=NE, channel_multiplier=-EJ, **exact).then_inc(consts, 1)
            pool.memset(ones[:, :], 1.0).then_inc(consts, 1)
            pool.memset(pad, 0.0).then_inc(poolown, 1)
            pool.wait_ge(poolown, 2)
            pool.affine_select(out=ident[:, :], in_=ident[:, :], compare_op=ALU.not_equal, fill=1.0, base=0,
                               pattern=[[-1, P]], channel_multiplier=1).then_inc(consts, 1)
            pool.memset(pad.rearrange("p (t c) -> p t c", c=REC)[:, :, 1:2], -1.0).then_inc(consts, 2)

        @block.vector
        def _(dve):
            o = Order(dve, own)
            dve.wait_ge(loaded, 64)
            o.done(dve.tensor_copy(rec[:, :, 0], ints[:, 0, :]))
            o.done(dve.tensor_copy(rec[:, :, 1], ints[:, 1, :]))
            o.done(dve.tensor_tensor(rec[:, :, 2:REC], near.rearrange("p (j h) -> p j h", h=H),
                                     path.rearrange("p (j h) -> p j h", h=H), ALU.add))
            o.link(dve.tensor_scalar(blk_i, ints[:, 1, :], BN.bit_length() - 1, None, ALU.arith_shift_right))
            o.link(dve.tensor_copy(blk, blk_i))
            dve.wait_ge(consts, 7)
            o.link(dve.tensor_tensor(eq, blk.unsqueeze(2).broadcast_to([EP, EJ, NB]),
                                     iota_n[0:EP, 0:NB].unsqueeze(1).broadcast_to([EP, EJ, NB]), ALU.is_equal))
            for k, e in enumerate((e_up, e_down)):
                o.link(dve.tensor_tensor(pos, eq, e.unsqueeze(2).broadcast_to([EP, EJ, NB]), ALU.mult))
                o.link(dve.tensor_reduce(ends[:, k * NB:(k + 1) * NB], pos.rearrange("p j b -> p b j"), AX.X,
                                         ALU.max))
            dve.wait_ge(turned, 1)
            o.link(dve.tensor_reduce(ends_t, psum[0][0:2 * NB, 0:EP], AX.X, ALU.max))
            dve.wait_ge(turned, 2)
            o.link(dve.tensor_scalar(tab_f[0:1, 0:NB], psum[1][0:1, NB:2 * NB], -1.0, float(NE), ALU.mult, ALU.add))
            o.link(dve.tensor_copy(tab_f[0:1, NB:2 * NB], psum[1][0:1, 0:NB]))
            o.link(dve.tensor_tensor(tab_f[0:1, 2 * NB + 1:3 * NB + 1], tab_f[0:1, NB:2 * NB], tab_f[0:1, 0:NB],
                                     ALU.subtract))
            o.link(dve.tensor_reduce(tab_f[0:1, 2 * NB:2 * NB + 1], tab_f[0:1, 2 * NB + 1:3 * NB + 1], AX.X, ALU.max))
            dve.tensor_copy(tab[0:1, :], tab_f[0:1, 0:2 * NB + 1]).then_inc(tabled, 1)

        @block.tensor
        def _(pe):
            pe.wait_ge(consts, 7)
            pe.wait_ge(own, 10)
            pe.transpose(psum[0][0:2 * NB, 0:EP], ends, ident[0:EP, 0:EP]).then_inc(turned, 1)
            pe.wait_ge(own, 11)
            pe.matmul(psum[1][0:1, 0:2 * NB], ends_t, ident[0:2 * NB, 0:2 * NB], start=True,
                      stop=True).then_inc(turned, 1)


def projections(nc, sem, x, Wqkv, bqkv, Wo, W1, W2, ln1_g, ln1_b, logits_d, wts, big, xs, hT, vs, work, small, ident,
                psum):
    wqkv = wts[:, 0:DC * 3 * D].rearrange("p (c n) -> p c n", c=DC)
    wo = wts[:, 3 * DC * D:4 * DC * D].rearrange("p (c n) -> p c n", c=DC)
    w1 = wts[:, 2 * SLOT:2 * SLOT + DC * FF].rearrange("p (c n) -> p c n", c=DC)
    w2 = wts[:, 4 * SLOT:4 * SLOT + DC * FF].rearrange("p (c n) -> p c n", n=D)
    g1 = work[:, 0:D]
    s1 = work[:, D:2 * D]
    bv = work[:, 2 * D:3 * D]
    hrow = [work[:, (3 + i) * D:(4 + i) * D] for i in range(2)]
    stage = [work[:, 6 * NP + i * NP:6 * NP + (i + 1) * NP] for i in range(2)]
    eps = small[:, 0:1]
    bqk_row = work[0:2 * DC, 5 * D:5 * D + P]
    bqk = small[:, 1:9]
    std = small[:, 10:15]
    rstd = small[:, 15:20]
    mv = small[:, 20:30].rearrange("p (t c) -> p t c", c=2)
    stats = small[:, 30:60].rearrange("p (t c) -> p t c", c=6)
    pairs = [(h, t) for t in range(NT) for h in range(H)]
    (x_in, vec_in, wqkv_in, later_in, zeroed, own, stds, rows, turned, moved, qk_ps, qk_sb, v_ps, v_sb, s_ps, s_act,
     s_dve, s_out, bqk_ready) = map(sem, (
        "x_in", "vec_in", "wqkv_in", "later_in", "tail_zeroed", "ln_own", "ln_stds", "h_rows", "h_turned", "h_moved",
        "qk_ps", "qk_sb", "v_ps", "v_sb", "s_ps", "s_act", "s_dve", "s_out", "bqk_ready"))
    s_out = [s_out, sem("s_out1")]
    bqk_turned = sem("bqk_turned")
    scale = float(D) ** -0.5

    with nc.Block() as block:
        @block.sync
        def _(sp):
            full, rest = node_tiles(x)
            sp.wait_ge(zeroed, 1)
            sp.dma_start(xs[:, 0:NT - 1, :], full).then_inc(x_in, 16)
            sp.dma_start(xs[0:LAST, NT - 1, :], rest).then_inc(x_in, 16)
            sp.dma_start(wqkv, Wqkv.rearrange("(c p) n -> p c n", p=P)).then_inc(wqkv_in, 16)
            sp.dma_start(bqk_row, bqkv[0:2 * D].rearrange("(m p) -> m p", p=P)).then_inc(vec_in, 16)
            for to, vec in ((g1, ln1_g), (s1, ln1_b), (bv, bqkv[2 * D:3 * D])):
                sp.dma_start(to, vec.rearrange("(a n) -> a n", a=1).broadcast_to([P, D])).then_inc(vec_in, 16)
            sp.dma_start(wo, Wo.rearrange("(c p) n -> p c n", p=P)).then_inc(later_in, 16)
            sp.dma_start(w1, W1.rearrange("(c p) n -> p c n", p=P)).then_inc(later_in, 16)
            sp.dma_start(w2, W2.rearrange("(c p) n -> p c n", p=P)).then_inc(later_in, 16)
            for i, (h, t) in enumerate(pairs):
                done = s_act if i % 2 == 0 else s_dve
                sp.wait_ge(done, i // 2 + 1)
                sp.dma_start(logits_d[t * BPT:(t + 1) * BPT, h, :, :].rearrange("b l s -> b l s"),
                             stage[i % 2]).then_inc(s_out[i % 2], 16)
            sp.wait_ge(s_out[0], 16 * 20)
            sp.wait_ge(s_out[1], 16 * 20)
            sp.wait_ge(later_in, 48)

        @block.gpsimd
        def _(pool):
            pool.memset(xs[:, NT - 1, :], 0.0).then_inc(zeroed, 1)

        @block.vector
        def _(dve):
            o = Order(dve, own)
            dve.memset(eps, EPS).then_inc(own, 1)
            o.n += 1
            dve.wait_ge(x_in, 32)
            for norm in range(2):
                for t in range(NT):
                    o.done(dve.bn_stats(stats[:, t, :], xs[:, t, :]))
                o.wait()
                for t in range(NT):
                    o.done(dve.bn_aggr(mv[:, t, :], stats[:, t, :]))
                o.wait()
                dve.wait_ge(stds, norm + 1)
                o.link(dve.reciprocal(rstd, std))
                if norm == 0:
                    for t in range(NT):
                        o.done(dve.tensor_scalar(xs[:, t, :], xs[:, t, :], mv[:, t, 0:1], rstd[:, t:t + 1],
                                                 ALU.subtract, ALU.mult))
                    o.wait()
            dve.wait_ge(vec_in, 64)
            dve.wait_ge(bqk_turned, 1)
            dve.tensor_scalar(bqk[:, 0:DC], psum[7][:, 0:DC], scale, None, ALU.mult).then_inc(bqk_ready, 1)
            dve.tensor_copy(bqk[:, DC:2 * DC], psum[7][:, DC:2 * DC]).then_inc(bqk_ready, 1)
            for t in range(NT):
                r = hrow[t % 2]
                if t >= 2:
                    dve.wait_ge(turned, t - 1)
                o.link(dve.tensor_scalar(r, xs[:, t, :], mv[:, t, 0:1], rstd[:, t:t + 1], ALU.subtract, ALU.mult))
                o.link(dve.tensor_tensor(r, r, g1, ALU.mult))
                dve.tensor_tensor(r, r, s1, ALU.add).then_inc(rows, 1)
            for t in range(NT):
                dve.wait_ge(v_ps, t + 1)
                dve.tensor_tensor(vs[:, t, :], psum[4 + t % 2][:, :], bv, ALU.add).then_inc(v_sb, 1)
            for i in range(1, len(pairs), 2):
                dve.wait_ge(s_ps, i + 1)
                if i >= 2:
                    dve.wait_ge(s_out[1], 16 * (i // 2))
                a, b = (psum[2 * (i % 4)], psum[2 * (i % 4) + 1])
                dve.tensor_copy(stage[1][:, 0:HALF], a[:, 0:HALF])
                dve.tensor_copy(stage[1][:, HALF:NP], b[:, 0:HALF]).then_inc(s_dve, 1)

        @block.scalar
        def _(act):
            for norm in range(2):
                act.wait_ge(own, 1 + 10 + 16 * norm)
                act.activation(std, mv[:, :, 1], ACT.Sqrt, bias=eps).then_inc(stds, 1)
            for t in range(NT):
                act.wait_ge(turned, t + 1)
                act.activation(hT[:, :, t * P:(t + 1) * P], psum[t % 2][:, :].rearrange("p (c n) -> p c n", c=DC),
                               ACT.Copy).then_inc(moved, 1)
            act.wait_ge(bqk_ready, 2)
            for m in range(2 * DC):
                for half in range(2):
                    i = 2 * m + half
                    act.wait_ge(qk_ps, i + 1)
                    act.activation(big[:, m, half * HALF:(half + 1) * HALF], psum[i % 4][:, 0:HALF], ACT.Identity,
                                   bias=bqk[:, m:m + 1], scale=scale if m < DC else 1.0).then_inc(qk_sb, 1)
            for i in range(0, len(pairs), 2):
                act.wait_ge(s_ps, i + 1)
                if i >= 2:
                    act.wait_ge(s_out[0], 16 * (i // 2))
                a, b = (psum[2 * (i % 4)], psum[2 * (i % 4) + 1])
                act.activation(stage[0][:, 0:HALF], a[:, 0:HALF], ACT.Copy)
                act.activation(stage[0][:, HALF:NP], b[:, 0:HALF], ACT.Copy).then_inc(s_act, 1)

        @block.tensor
        def _(pe):
            pe.wait_ge(vec_in, 64)
            pe.transpose(psum[7][:, 0:2 * DC], bqk_row, ident[0:2 * DC, 0:2 * DC]).then_inc(bqk_turned, 1)
            for t in range(NT):
                pe.wait_ge(rows, t + 1)
                if t >= 2:
                    pe.wait_ge(moved, t - 1)
                for c in range(DC):
                    last = pe.transpose(psum[t % 2][:, c * P:(c + 1) * P], hrow[t % 2][:, c * P:(c + 1) * P],
                                        ident[:, :])
                last.then_inc(turned, 1)
            pe.wait_ge(moved, NT)
            pe.wait_ge(wqkv_in, 16)
            for m in range(2 * DC):
                for half in range(2):
                    i = 2 * m + half
                    if i >= 4:
                        pe.wait_ge(qk_sb, i - 3)
                    for c in range(DC):
                        last = pe.matmul(psum[i % 4][:, 0:HALF], wqkv[:, c, m * P:(m + 1) * P],
                                         hT[:, c, half * HALF:(half + 1) * HALF], start=c == 0, stop=c == DC - 1)
                    last.then_inc(qk_ps, 1)
            for t in range(NT):
                if t >= 2:
                    pe.wait_ge(v_sb, t - 1)
                for c in range(DC):
                    last = pe.matmul(psum[4 + t % 2][:, :], hT[:, c, t * P:(t + 1) * P], wqkv[:, c, 2 * D:3 * D],
                                     start=c == 0, stop=c == DC - 1)
                last.then_inc(v_ps, 1)
            pe.wait_ge(qk_sb, 4 * DC)
            pe.wait_ge(v_sb, NT)
            for i, (h, t) in enumerate(pairs):
                r = slice(DH * (h % 2), DH * (h % 2 + 1))
                if i >= 4:
                    pe.wait_ge(s_act if i % 2 == 0 else s_dve, i // 2 - 1)
                for half in range(2):
                    last = pe.matmul(psum[2 * (i % 4) + half][:, 0:HALF],
                                     big[r, DC + h // 2, t * P:(t + 1) * P],
                                     big[r, h // 2, half * HALF:(half + 1) * HALF], start=True, stop=True)
                last.then_inc(s_ps, 1)


def attention(nc, sem, rec_d, logits_d, big, hT, vs, work, iota_n, ident, ones, XM, tab, small, psum):
    X = [work[:, i * CT * P:(i + 1) * CT * P].rearrange("p (t m) -> p t m", t=CT) for i in range(2)]
    R = work[:, 2 * NP:3 * NP].rearrange("p (t m) -> p t m", t=CT)
    onehot = work[:, 3 * NP:8 * NP].rearrange("p (t s) -> p t s", t=CT)
    S = [work[:, (8 + i) * NP:(9 + i) * NP] for i in range(2)]
    L = work[:, 10 * NP:11 * NP]
    PR = work[:, 11 * NP:12 * NP]
    PT = big[:, 8:16, :].rearrange("p a n -> p (a n)").rearrange("p (t h d) -> p t h d", t=NT, h=H)
    rec = [big[:, i, 0:CT * REC].rearrange("p (t c) -> p t c", t=CT) for i in range(2)]
    miss = [big[:, 2 + i, 0:CT * BN].rearrange("p (t d) -> p t d", t=CT) for i in range(2)]
    minus_big = big[:, 4, 0:1]
    diag = big[:, 4, P:2 * P]
    tiny = small[:, 0:1]
    guard, nguard, total, inv, worst = (small[:, k:k + 1] for k in range(1, 6))
    psT, psM = psum[0][:, 0:P], psum[0][:, P:2 * P]
    psW = [(psum[1], psum[2]), (psum[3], psum[4])]
    psP = (psum[5], psum[6])
    psO = psum[7]

    (consts, poolown, x_ready, xm_ready, xm_turned, own, diag_ready, rep_ready, d_done, r_ready, oh_ready,
     l_ready, g_ready, e_ready, p_made, inv_ready, p_ready, p_turned, pt_ready, o_ready, o_moved, oh_used) = map(sem, (
         "at_consts", "at_poolown", "x_ready", "xm_ready", "xm_turned", "at_own", "diag_ready", "rep_ready", "d_done",
         "r_ready", "oh_ready", "l_ready", "g_ready", "e_ready", "p_made", "inv_ready", "p_ready",
         "p_turned", "pt_ready", "o_ready", "o_moved", "oh_used"))
    worst_ready = sem("worst_ready")
    rec_in = [sem(f"rec_in{i}") for i in range(2)]
    s_in = [sem(f"s_in{i}") for i in range(2)]
    half = BPT // 2

    with nc.Block() as block:
        @block.sync
        def _(sp):
            longest = sp.value_load(tab[0:1, 2 * NB:2 * NB + 1], min_val=-NE, max_val=NE)
            with sp.If(longest < CHUNK + 1):
                def tile(j):
                    for k in range(BPT):
                        b = j * BPT + k
                        start = sp.value_load(tab[0:1, bass.ds(b, 1)], min_val=0, max_val=NE)
                        at = sp.snap(start * REC)
                        row = b * (P * NP) if isinstance(b, int) else sp.snap(b * (P * NP))
                        free = b - 1
                        free = free if isinstance(free, int) else sp.snap(free)
                        hot = free * CT if isinstance(free, int) else sp.snap(free * CT)
                        wait_past(sp, oh_ready, hot)
                        wait_past(sp, x_ready, free)
                        sp.dma_start(rec[k % 2].rearrange("p t c -> p (t c)"),
                                     rec_d.rearrange("e c -> (e c)")[bass.ds(at, CHUNK * REC)].rearrange("(p n) -> p n", p=P))\
                          .then_inc(rec_in[k % 2], 16)
                        wait_past(sp, e_ready, free)
                        sp.dma_start(S[k % 2], logits_d.rearrange("b h l s -> (b h l s)")[bass.ds(row, P * NP)].rearrange("(p n) -> p n", p=P))\
                          .then_inc(s_in[k % 2], 16)

                tile(0)
                with sp.Fori(1, NT) as j:
                    tile(j)

        @block.gpsimd
        def _(pool):
            longest = pool.value_load(tab[0:1, 2 * NB:2 * NB + 1], min_val=-NE, max_val=NE)
            with pool.If(longest < CHUNK + 1):
                pool.memset(minus_big, -BIG).then_inc(consts, 1)
                pool.memset(tiny, TINY).then_inc(consts, 1)
                pool.wait_ge(consts, 2)
                def tile(j):
                    for k in range(BPT):
                        b = j * BPT + k
                        m = miss[k % 2]
                        wait_past(pool, rec_in[k % 2], 16 * half * j + 16 * (k // 2 + 1))
                        pool.tensor_tensor(m, rec[k % 2][:, :, 1:2].broadcast_to([P, CT, BN]),
                                           iota_n[:, bass.ds(b * BN, BN)].unsqueeze(1).broadcast_to([P, CT, BN]),
                                           ALU.subtract).then_inc(poolown, 1)
                        wait_past(pool, poolown, 3 * b + 1)
                        pool.tensor_tensor(m, m, m, ALU.mult).then_inc(poolown, 1)
                        wait_past(pool, poolown, 3 * b + 2)
                        pool.tensor_tensor(m, m, minus_big.unsqueeze(1).broadcast_to([P, CT, BN]), ALU.mult)\
                            .then_inc(poolown, 1)
                        wait_past(pool, poolown, 3 * b + 3)
                        wait_past(pool, r_ready, b - 1)
                        pool.tensor_tensor(X[k % 2].rearrange("p t (h d) -> p t h d", h=H),
                                           rec[k % 2][:, :, 2:REC].unsqueeze(3).broadcast_to([P, CT, H, BN]),
                                           m.unsqueeze(2).broadcast_to([P, CT, H, BN]), ALU.add).then_inc(x_ready, 1)

                tile(0)
                with pool.Fori(1, NT) as j:
                    tile(j)

        @block.vector
        def _(dve):
            longest = dve.value_load(tab[0:1, 2 * NB:2 * NB + 1], min_val=-NE, max_val=NE)
            with dve.If(longest < CHUNK + 1):
                dve.wait_ge(consts, 2)

                def onehots(b, k, tiles):
                    for t in tiles:
                        wait_past(dve, oh_used, CT * (b - 1) + t + 1)
                        dve.tensor_scalar(onehot[:, t, :], iota_n[:, :], rec[k % 2][:, t, 0:1], None, ALU.is_equal)\
                           .then_inc(oh_ready, 1)

                def front(j, k):
                    b = j * BPT + k
                    wait_past(dve, x_ready, b + 1)
                    dve.tensor_reduce(XM[:, k % 2, :], X[k % 2].rearrange("p t m -> p m t"), AX.X, ALU.max)\
                       .then_inc(xm_ready, 1)
                    onehots(b, k, (0, 1))
                    wait_past(dve, xm_turned, b + 1)
                    dve.tensor_reduce(worst, psT, AX.X, ALU.max).then_inc(worst_ready, 1)
                    wait_past(dve, worst_ready, b + 1)
                    dve.tensor_scalar(diag, ident[:, :], worst, -BIG / 10, ALU.mult, ALU.max).then_inc(diag_ready, 1)
                    onehots(b, k, (2, 3, 4))
                    wait_past(dve, rep_ready, b + 1)
                    dve.tensor_tensor(X[k % 2], X[k % 2], psM.unsqueeze(1).broadcast_to([P, CT, P]), ALU.subtract)\
                       .then_inc(d_done, 1)

                def back(j, k):
                    b = j * BPT + k
                    lo, hi = psW[k % 2]
                    wait_past(dve, l_ready, b + 1)
                    wait_past(dve, s_in[k % 2], 16 * half * j + 16 * (k // 2 + 1))
                    dve.tensor_tensor(L, L, S[k % 2], ALU.add).then_inc(own, 1)
                    wait_past(dve, own, 3 * b + 1)
                    dve.tensor_reduce(nguard, L, AX.X, ALU.max, negate=True).then_inc(g_ready, 1)
                    wait_past(dve, e_ready, b + 1)
                    wait_past(dve, p_turned, b)
                    dve.tensor_tensor_reduce(PR[:, 0:HALF], lo[:, 0:HALF], L[:, 0:HALF], 1.0, 0.0, ALU.mult, ALU.add,
                                             total).then_inc(own, 1)
                    wait_past(dve, own, 3 * b + 2)
                    dve.tensor_tensor_reduce(PR[:, HALF:NP], hi[:, 0:HALF], L[:, HALF:NP], 1.0, total, ALU.mult, ALU.add,
                                             guard).then_inc(own, 1)
                    wait_past(dve, own, 3 * b + 3)
                    dve.tensor_scalar(total, guard, 1e-37, None, ALU.max).then_inc(p_made, 1)
                    wait_past(dve, p_made, b + 1)
                    dve.reciprocal(inv, total).then_inc(inv_ready, 1)

                def tile(j):
                    for k in range(BPT):
                        front(j, k)
                        if k:
                            back(j, k - 1)
                    back(j, BPT - 1)
                    wait_past(dve, o_ready, j + 1)
                    dve.tensor_copy(hT[:, :, bass.ds(j * P, P)], psO[:, :].rearrange("p (c d) -> p c d", c=DC))\
                       .then_inc(o_moved, 1)

                tile(0)
                with dve.Fori(1, NT) as j:
                    tile(j)

        @block.scalar
        def _(act):
            longest = act.value_load(tab[0:1, 2 * NB:2 * NB + 1], min_val=-NE, max_val=NE)
            with act.If(longest < CHUNK + 1):
                act.preload_act_table_set("natural_log_exp_and_others")
                act.wait_ge(consts, 2)

                def weigh(j, k):
                    b = j * BPT + k
                    wait_past(act, d_done, b + 1)
                    wait_past(act, oh_used, CT * b)
                    act.activation(R, X[k % 2], ACT.Exp).then_inc(r_ready, 1)

                def guards(j, k):
                    b = j * BPT + k
                    wait_past(act, oh_used, CT * (b + 1))
                    wait_past(act, inv_ready, b)
                    lo, hi = psW[k % 2]
                    act.activation(L[:, 0:HALF], lo[:, 0:HALF], ACT.Ln, bias=tiny)
                    act.activation(L[:, HALF:NP], hi[:, 0:HALF], ACT.Ln, bias=tiny).then_inc(l_ready, 1)

                def exps(j, k):
                    b = j * BPT + k
                    wait_past(act, g_ready, b + 1)
                    act.activation(L, S[k % 2], ACT.Exp, bias=nguard).then_inc(e_ready, 1)

                def norm(j, k):
                    b = j * BPT + k
                    wait_past(act, inv_ready, b + 1)
                    act.activation(PR, PR, ACT.Copy, scale=inv).then_inc(p_ready, 1)

                def keep(j, k):
                    b = j * BPT + k
                    wait_past(act, p_turned, b + 1)
                    if k == 0:
                        wait_past(act, o_ready, j)
                    lo = psP[0][:, :].rearrange("s (t h d) -> s t h d", t=4, h=H)
                    for t in range(4):
                        act.activation(PT[:, t, :, k * BN:(k + 1) * BN], lo[:, t], ACT.Copy)
                    act.activation(PT[:, 4, :, k * BN:(k + 1) * BN], psP[1][:, 0:P].rearrange("s (h d) -> s h d", h=H),
                                   ACT.Copy).then_inc(pt_ready, 1)

                def tile(j):
                    for k in range(BPT):
                        weigh(j, k)
                        if k:
                            exps(j, k - 1)
                            norm(j, k - 1)
                            keep(j, k - 1)
                        guards(j, k)
                    exps(j, BPT - 1)
                    norm(j, BPT - 1)
                    keep(j, BPT - 1)

                tile(0)
                with act.Fori(1, NT) as j:
                    tile(j)

        @block.tensor
        def _(pe):
            longest = pe.value_load(tab[0:1, 2 * NB:2 * NB + 1], min_val=-NE, max_val=NE)
            with pe.If(longest < CHUNK + 1):
                def front(j, k):
                    b = j * BPT + k
                    wait_past(pe, xm_ready, b + 1)
                    wait_past(pe, d_done, b)
                    pe.transpose(psT, XM[:, k % 2, :], ident[:, :]).then_inc(xm_turned, 1)
                    wait_past(pe, diag_ready, b + 1)
                    pe.matmul(psM, ones[:, :], diag, start=True, stop=True).then_inc(rep_ready, 1)

                def sums(j, k):
                    b = j * BPT + k
                    lo, hi = psW[k % 2]
                    wait_past(pe, r_ready, b + 1)
                    wait_past(pe, inv_ready, b - 1)
                    for t in range(CT):
                        wait_past(pe, oh_ready, CT * b + t + 1)
                        pe.matmul(lo[:, 0:HALF], R[:, t, :], onehot[:, t, 0:HALF], start=t == 0, stop=t == CT - 1)
                        last = pe.matmul(hi[:, 0:HALF], R[:, t, :], onehot[:, t, HALF:NP], start=t == 0,
                                         stop=t == CT - 1)
                        last.then_inc(oh_used, 1)

                def turn(j, k):
                    b = j * BPT + k
                    wait_past(pe, p_ready, b + 1)
                    wait_past(pe, pt_ready, b)
                    for t in range(NT):
                        to = psP[t // 4][:, (t % 4) * P:(t % 4 + 1) * P]
                        last = pe.transpose(to, PR[:, t * P:(t + 1) * P], ident[:, :])
                    last.then_inc(p_turned, 1)

                def tile(j):
                    for k in range(BPT):
                        front(j, k)
                        sums(j, k)
                        if k:
                            turn(j, k - 1)
                    turn(j, BPT - 1)
                    wait_past(pe, pt_ready, BPT * (j + 1))
                    wait_past(pe, o_moved, j)
                    for h in range(H):
                        r = slice(DH * (h % 2), DH * (h % 2 + 1))
                        for t in range(NT):
                            last = pe.matmul(psO[r, (h // 2) * P:(h // 2 + 1) * P], vs[:, t, h * DH:(h + 1) * DH],
                                             PT[:, t, h, :], start=t == 0, stop=t == NT - 1)
                    last.then_inc(o_ready, 1)

                tile(0)
                with pe.Fori(1, NT) as j:
                    tile(j)


def feed_forward(nc, sem, x, bo, ln2_g, ln2_b, b1, b2, wts, big, xs, hT, vs, work, small, ident, psum):
    wo = wts[:, 3 * DC * D:4 * DC * D].rearrange("p (c n) -> p c n", c=DC)
    w1 = wts[:, 2 * SLOT:2 * SLOT + DC * FF].rearrange("p (c n) -> p c n", c=DC)
    w2 = wts[:, 4 * SLOT:4 * SLOT + DC * FF].rearrange("p (c n) -> p c n", n=D)
    g2, s2, bo_r, b2_r = (work[:, i * D:(i + 1) * D] for i in range(4))
    xin = work[:, 5 * D:10 * D].rearrange("p (t n) -> p t n", t=NT)
    hrow = [work[:, (10 + i) * D:(11 + i) * D] for i in range(2)]
    b1_row = work[0:FF // P, 12 * D:12 * D + P]
    b1c = vs[:, 0, 0:FF // P]
    eps = small[:, 0:1]
    std = small[:, 10:15]
    rstd = small[:, 15:20]
    mv = small[:, 20:30].rearrange("p (t c) -> p t c", c=2)
    stats = small[:, 30:60].rearrange("p (t c) -> p t c", c=6)
    MC = FF // P
    (vec_in, x_in, zeroed, own, stds, rows, turned, moved, o_ps, b1_turned, b1_ready, u_ps, u_sb, y_ps, y_sb,
     eps_set) = map(sem, (
         "ff_vec_in", "ff_x_in", "ff_zeroed", "ff_own", "ff_stds", "ff_rows", "ff_turned", "ff_moved", "o_ps",
         "b1_turned", "b1_ready", "u_ps", "u_sb", "y_ps", "y_sb", "ff_eps"))

    with nc.Block() as block:
        @block.sync
        def _(sp):
            for to, vec in ((g2, ln2_g), (s2, ln2_b), (bo_r, bo), (b2_r, b2)):
                sp.dma_start(to, vec.rearrange("(a n) -> a n", a=1).broadcast_to([P, D])).then_inc(vec_in, 16)
            sp.dma_start(b1_row, b1.rearrange("(m p) -> m p", p=P)).then_inc(vec_in, 16)
            full, rest = node_tiles(x)
            sp.wait_ge(zeroed, 1)
            sp.dma_start(xin[:, 0:NT - 1, :], full).then_inc(x_in, 16)
            sp.dma_start(xin[0:LAST, NT - 1, :], rest).then_inc(x_in, 16)

        @block.gpsimd
        def _(pool):
            pool.memset(xin[:, NT - 1, :], 0.0).then_inc(zeroed, 1)

        @block.vector
        def _(dve):
            o = Order(dve, own)
            dve.memset(eps, EPS).then_inc(eps_set, 1)
            dve.wait_ge(vec_in, 80)
            for t in range(NT):
                dve.wait_ge(o_ps, t + 1)
                o.link(dve.tensor_tensor(xs[:, t, :], xs[:, t, :], psum[t % 2][:, :], ALU.add))
                o.link(dve.tensor_tensor(xs[:, t, :], xs[:, t, :], bo_r, ALU.add))
                o.link(dve.bn_stats(stats[:, t, :], xs[:, t, :]))
                o.link(dve.bn_aggr(mv[:, t, :], stats[:, t, :]))
            dve.wait_ge(stds, 1)
            o.link(dve.reciprocal(rstd, std))
            for t in range(NT):
                r = hrow[t % 2]
                if t >= 2:
                    dve.wait_ge(turned, t - 1)
                o.link(dve.tensor_scalar(r, xs[:, t, :], mv[:, t, 0:1], rstd[:, t:t + 1], ALU.subtract, ALU.mult))
                o.link(dve.tensor_tensor(r, r, g2, ALU.mult))
                dve.tensor_tensor(r, r, s2, ALU.add).then_inc(rows, 1)
            dve.wait_ge(b1_turned, 1)
            dve.tensor_copy(b1c, psum[7][:, 0:MC]).then_inc(b1_ready, 1)
            dve.wait_ge(x_in, 32)
            for t in range(NT):
                o.link(dve.tensor_tensor(xin[:, t, :], xin[:, t, :], b2_r, ALU.add))
                o.link(dve.tensor_tensor(xs[:, t, :], xs[:, t, :], xin[:, t, :], ALU.add))
            for t in range(NT):
                dve.wait_ge(y_ps, t + 1)
                dve.tensor_tensor(xs[:, t, :], xs[:, t, :], psum[4 + t % 2][:, :], ALU.add).then_inc(y_sb, 1)

        @block.scalar
        def _(act):
            act.wait_ge(eps_set, 1)
            act.wait_ge(own, 4 * NT)
            act.activation(std, mv[:, :, 1], ACT.Sqrt, bias=eps).then_inc(stds, 1)
            for t in range(NT):
                act.wait_ge(turned, t + 1)
                act.activation(hT[:, :, t * P:(t + 1) * P], psum[2 + t % 2][:, :].rearrange("p (c n) -> p c n", c=DC),
                               ACT.Copy).then_inc(moved, 1)
            act.wait_ge(b1_ready, 1)
            for m in range(MC):
                for half in range(2):
                    i = 2 * m + half
                    act.wait_ge(u_ps, i + 1)
                    act.activation(big[:, m, half * HALF:(half + 1) * HALF], psum[i % 4][:, 0:HALF], ACT.Gelu,
                                   bias=b1c[:, m:m + 1]).then_inc(u_sb, 1)

        @block.tensor
        def _(pe):
            for t in range(NT):
                if t >= 2:
                    pe.wait_ge(own, 4 * (t - 2) + 1)
                for c in range(DC):
                    last = pe.matmul(psum[t % 2][:, :], hT[:, c, t * P:(t + 1) * P], wo[:, c, :], start=c == 0,
                                     stop=c == DC - 1)
                last.then_inc(o_ps, 1)
            pe.wait_ge(vec_in, 80)
            pe.transpose(psum[7][:, 0:MC], b1_row, ident[0:MC, 0:MC]).then_inc(b1_turned, 1)
            for t in range(NT):
                pe.wait_ge(rows, t + 1)
                if t >= 2:
                    pe.wait_ge(moved, t - 1)
                for c in range(DC):
                    last = pe.transpose(psum[2 + t % 2][:, c * P:(c + 1) * P], hrow[t % 2][:, c * P:(c + 1) * P],
                                        ident[:, :])
                last.then_inc(turned, 1)
            pe.wait_ge(moved, NT)
            for m in range(MC):
                for half in range(2):
                    i = 2 * m + half
                    if i >= 4:
                        pe.wait_ge(u_sb, i - 3)
                    for c in range(DC):
                        last = pe.matmul(psum[i % 4][:, 0:HALF], w1[:, c, m * P:(m + 1) * P],
                                         hT[:, c, half * HALF:(half + 1) * HALF], start=c == 0, stop=c == DC - 1)
                    last.then_inc(u_ps, 1)
            pe.wait_ge(u_sb, 2 * MC)
            for t in range(NT):
                if t >= 2:
                    pe.wait_ge(y_sb, t - 1)
                for m in range(MC):
                    last = pe.matmul(psum[4 + t % 2][:, :], big[:, m, t * P:(t + 1) * P], w2[:, m, :], start=m == 0,
                                     stop=m == MC - 1)
                last.then_inc(y_ps, 1)


def experts(nc, sem, gate_w, biases, w1, w3, w2, sw1, sw3, sw2, out, wts, big, xs, hT, vs, work, iota_n, small,
            ident, psum):
    slots = [wts[:, i * SLOT:(i + 1) * SLOT] for i in range(6)]
    hrow = [work[:, i * D:(i + 1) * D] for i in range(2)]
    gate_row = work[0:EX, 2 * D:3 * D]
    bias_r = work[:, 3 * D:3 * D + EX]
    gate_t = work[:, 3 * D + 8:3 * D + 8 + DC * EX].rearrange("p (c e) -> p c e", c=DC)
    gates = work[:, 4 * D:4 * D + NT * EX].rearrange("p (t e) -> p t e", t=NT)
    sc, sbias, top, topb = (work[:, 4 * D + 40 + 40 * i:4 * D + 80 + 40 * i].rearrange("p (t e) -> p t e", t=NT)
                            for i in range(4))
    idx = work[:, 4 * D + 240:4 * D + 280].bitcast(U32).rearrange("p (t e) -> p t e", t=NT)
    idx_f = work[:, 4 * D + 280:4 * D + 320].rearrange("p (t e) -> p t e", t=NT)
    prob = work[:, 4 * D + 320:4 * D + 330].rearrange("p (t k) -> p t k", t=NT)
    psums = work[:, 4 * D + 330:4 * D + 335]
    pick = work[:, 4 * D + 340:4 * D + 380].rearrange("p (t e) -> p t e", t=NT)
    gated = [work[:, 5 * D + i * HALF:5 * D + (i + 1) * HALF] for i in range(2)]
    eps = small[:, 0:1]
    std = small[:, 10:15]
    rstd = small[:, 15:20]
    mv = small[:, 20:30].rearrange("p (t c) -> p t c", c=2)
    stats = small[:, 30:60].rearrange("p (t c) -> p t c", c=6)
    (vec_in, own, stds, rows, turned, moved, gate_turned, sc_ps, exp_in, exp_out, a_ps, a_sb, b_sb, y_ps, y_sb,
     sh_in, stored, gate_ready) = map(sem, (
         "ex_vec_in", "ex_own", "ex_stds", "ex_rows", "ex_turned", "ex_moved", "gate_turned", "sc_ps", "exp_in",
         "exp_out", "a_ps", "a_sb", "b_sb", "ey_ps", "ey_sb", "sh_in", "ex_stored", "gate_ready"))
    w_in = [sem(f"w_in{i}") for i in range(2)]

    def parts(s, a, b, c):
        return ((slots[s].rearrange("p (c n) -> p c n", c=DC), a.rearrange("(c p) n -> p c n", p=P)),
                (slots[s + 1].rearrange("p (c n) -> p c n", c=DC), b.rearrange("(c p) n -> p c n", p=P)),
                (slots[s + 2].rearrange("p (c n) -> p c n", n=D), c.rearrange("(c p) n -> p c n", p=P)))

    def of(w, e):
        return w[bass.ds(e, 1), :, :].rearrange("a k n -> (a k) n")

    with nc.Block() as block:
        @block.sync
        def _(sp):
            sp.dma_start(gate_row, gate_w).then_inc(vec_in, 16)
            sp.dma_start(bias_r, biases.rearrange("(a n) -> a n", a=1).broadcast_to([P, EX])).then_inc(vec_in, 16)
            for to, frm in parts(0, sw1, sw3, sw2):
                sp.dma_start(to, frm).then_inc(sh_in, 16)

            def load(j, k):
                e = j * 2 + k
                wait_past(sp, y_ps, e * NT if isinstance(e, int) else sp.snap(e * NT))
                for to, frm in parts(3 - 3 * k, of(w1, e), of(w3, e), of(w2, e)):
                    sp.dma_start(to, frm).then_inc(w_in[k], 16)

            load(0, 0)
            load(0, 1)
            with sp.Fori(1, EX // 2) as j:
                load(j, 0)
                load(j, 1)
            sp.wait_ge(y_sb, NT * (EX + 1))
            full, rest = node_tiles(out)
            sp.dma_start(full, xs[:, 0:NT - 1, :]).then_inc(stored, 16)
            sp.dma_start(rest, xs[0:LAST, NT - 1, :]).then_inc(stored, 16)
            sp.wait_ge(stored, 32)

        @block.vector
        def _(dve):
            o = Order(dve, own)
            for t in range(NT):
                o.done(dve.bn_stats(stats[:, t, :], xs[:, t, :]))
            o.wait()
            for t in range(NT):
                o.done(dve.bn_aggr(mv[:, t, :], stats[:, t, :]))
            dve.wait_ge(stds, 1)
            o.link(dve.reciprocal(rstd, std))
            for t in range(NT):
                if t >= 2:
                    dve.wait_ge(turned, t - 1)
                dve.tensor_scalar(hrow[t % 2], xs[:, t, :], mv[:, t, 0:1], rstd[:, t:t + 1], ALU.subtract,
                                  ALU.mult).then_inc(rows, 1)
            dve.wait_ge(gate_turned, 1)
            o.link(dve.tensor_copy(gate_t, psum[7][:, 0:DC * EX].rearrange("p (c e) -> p c e", c=DC)))
            dve.wait_ge(sc_ps, 1)
            o.link(dve.tensor_copy(sc, psum[6][:, 0:NT * EX].rearrange("p (t e) -> p t e", t=NT)))
            o.link(dve.tensor_tensor(sbias, sc, bias_r.unsqueeze(1).broadcast_to([P, NT, EX]), ALU.add))
            for t in range(NT):
                o.done(dve.max(top[:, t, :], sc[:, t, :]))
                o.done(dve.max(topb[:, t, :], sbias[:, t, :]))
            o.wait()
            for t in range(NT):
                o.done(dve.max_index(idx[:, t, :], topb[:, t, :], sbias[:, t, :]))
            o.wait()
            dve.tensor_copy(idx_f, idx).then_inc(exp_in, 1)
            dve.wait_ge(exp_in, 1)
            dve.wait_ge(exp_out, 1)
            o.link(dve.tensor_scalar(prob, prob, 1.0, None, ALU.add))
            o.link(dve.reciprocal(prob, prob))
            o.link(dve.tensor_reduce(psums, prob, AX.X, ALU.add))
            o.link(dve.reciprocal(psums, psums))
            o.link(dve.tensor_tensor(prob, prob, psums.unsqueeze(2).broadcast_to([P, NT, 2]), ALU.mult))
            for k in range(2):
                o.link(dve.tensor_tensor(pick, iota_n[:, 0:EX].unsqueeze(1).broadcast_to([P, NT, EX]),
                                         idx_f[:, :, k:k + 1].broadcast_to([P, NT, EX]), ALU.is_equal))
                o.link(dve.tensor_tensor(pick if k else gates, pick,
                                         prob[:, :, k:k + 1].broadcast_to([P, NT, EX]), ALU.mult))
            dve.tensor_tensor(gates, gates, pick, ALU.add).then_inc(gate_ready, 1)
            dve.wait_ge(gate_ready, 1)

            def hidden(e, k):
                for m in range(HC):
                    for half in range(2):
                        i = 2 * m + half
                        dve.wait_ge(a_sb, e * (2 * HC) + (i + 1))
                        dve.wait_ge(a_ps, e * (2 * HC) + (i + 1))
                        dve.tensor_tensor(big[:, HC * k + m, half * HALF:(half + 1) * HALF], gated[i % 2],
                                          psum[2 * (i % 2) + 1][:, 0:HALF], ALU.mult).then_inc(b_sb, 1)

            hidden(0, 0)
            for t in range(NT):
                dve.wait_ge(y_ps, t + 1)
                dve.tensor_tensor(xs[:, t, :], xs[:, t, :], psum[4 + t % 2][:, :], ALU.add).then_inc(y_sb, 1)
            with dve.Fori(0, EX // 2) as j:
                for k in range(2):
                    e = j * 2 + (k + 1)
                    hidden(e, 1 - k)
                    for t in range(NT):
                        dve.wait_ge(y_ps, e * NT + (t + 1))
                        dve.wait_ge(y_sb, e * NT + (t + 1 - NT))
                        dve.scalar_tensor_tensor(out=xs[:, t, :], in0=psum[4 + t % 2][:, :],
                                                 scalar=gates[:, t, bass.ds(e - 1, 1)], in1=xs[:, t, :],
                                                 op0=ALU.mult, op1=ALU.add).then_inc(y_sb, 1)

        @block.scalar
        def _(act):
            act.wait_ge(own, 2 * NT)
            act.activation(std, mv[:, :, 1], ACT.Sqrt, bias=eps).then_inc(stds, 1)
            for t in range(NT):
                act.wait_ge(turned, t + 1)
                act.activation(hT[:, :, t * P:(t + 1) * P], psum[2 + t % 2][:, :].rearrange("p (c n) -> p c n", c=DC),
                               ACT.Copy).then_inc(moved, 1)
            act.wait_ge(exp_in, 1)
            act.activation(prob, top[:, :, 0:2], ACT.Exp, scale=-1.0).then_inc(exp_out, 1)

            def hidden(e):
                for i in range(2 * HC):
                    act.wait_ge(a_ps, e * (2 * HC) + (i + 1))
                    if isinstance(e, int) and i < 2:
                        pass
                    else:
                        act.wait_ge(b_sb, e * (2 * HC) + (i - 1))
                    act.activation(gated[i % 2], psum[2 * (i % 2)][:, 0:HALF], ACT.Silu).then_inc(a_sb, 1)

            hidden(0)
            with act.Fori(0, EX // 2) as j:
                for k in range(2):
                    hidden(j * 2 + (k + 1))

        @block.tensor
        def _(pe):
            for t in range(NT):
                pe.wait_ge(rows, t + 1)
                if t >= 2:
                    pe.wait_ge(moved, t - 1)
                for c in range(DC):
                    last = pe.transpose(psum[2 + t % 2][:, c * P:(c + 1) * P], hrow[t % 2][:, c * P:(c + 1) * P],
                                        ident[:, :])
                last.then_inc(turned, 1)
            pe.wait_ge(vec_in, 32)
            for c in range(DC):
                last = pe.transpose(psum[7][:, c * EX:(c + 1) * EX], gate_row[:, c * P:(c + 1) * P],
                                    ident[0:EX, 0:EX])
            last.then_inc(gate_turned, 1)
            pe.wait_ge(moved, NT)
            pe.wait_ge(own, 2 * NT + 2)
            for t in range(NT):
                for c in range(DC):
                    last = pe.matmul(psum[6][:, t * EX:(t + 1) * EX], hT[:, c, t * P:(t + 1) * P], gate_t[:, c, :],
                                     start=c == 0, stop=c == DC - 1)
            last.then_inc(sc_ps, 1)

            def expert(e, s, k):
                a, b, c3 = (p[0] for p in parts(s, sw1, sw3, sw2))
                for m in range(HC):
                    for half in range(2):
                        i = 2 * m + half
                        if not (isinstance(e, int) and i < 2):
                            pe.wait_ge(b_sb, e * (2 * HC) + (i - 1))
                        for w, bank in ((a, 2 * (i % 2)), (b, 2 * (i % 2) + 1)):
                            for c in range(DC):
                                last = pe.matmul(psum[bank][:, 0:HALF], w[:, c, m * P:(m + 1) * P],
                                                 hT[:, c, half * HALF:(half + 1) * HALF], start=c == 0,
                                                 stop=c == DC - 1)
                        last.then_inc(a_ps, 1)
                pe.wait_ge(b_sb, e * (2 * HC) + 2 * HC)
                for t in range(NT):
                    if not (isinstance(e, int) and t < 2):
                        pe.wait_ge(y_sb, e * NT + (t - 1))
                    for m in range(HC):
                        last = pe.matmul(psum[4 + t % 2][:, :], big[:, HC * k + m, t * P:(t + 1) * P], c3[:, m, :],
                                         start=m == 0, stop=m == HC - 1)
                    last.then_inc(y_ps, 1)

            pe.wait_ge(sh_in, 48)
            expert(0, 0, 0)
            with pe.Fori(0, EX // 2) as j:
                for k in range(2):
                    pe.wait_ge(w_in[k], j * 48 + 48)
                    expert(j * 2 + (k + 1), 3 - 3 * k, 1 - k)


def attention_any(nc, sem, rec_d, logits_d, big, hT, vs, work, iota_n, ident, ones, XM, tab, small, psum):
    NCH = -(-NE // CHUNK)
    X = work[:, 0:CT * P].rearrange("p (t m) -> p t m", t=CT)
    R = work[:, 2 * NP:3 * NP].rearrange("p (t m) -> p t m", t=CT)
    onehot = work[:, 3 * NP:8 * NP].rearrange("p (t s) -> p t s", t=CT)
    S = work[:, 8 * NP:9 * NP]
    L = work[:, 10 * NP:11 * NP]
    PR = work[:, 11 * NP:12 * NP]
    PT = big[:, 8:16, :].rearrange("p a n -> p (a n)").rearrange("p (t h d) -> p t h d", t=NT, h=H)
    rec = big[:, 0, 0:CT * REC].rearrange("p (t c) -> p t c", t=CT)
    miss = big[:, 2, 0:CT * BN].rearrange("p (t d) -> p t d", t=CT)
    minus_big = big[:, 4, 0:1]
    diag = big[:, 4, P:2 * P]
    zeros = big[:, 4, 2 * P:3 * P]
    tiny = small[:, 0:1]
    guard, nguard, total, inv, worst = (small[:, k:k + 1] for k in range(1, 6))
    psT, psM = psum[0][:, 0:P], psum[0][:, P:2 * P]
    lo, hi = psum[1], psum[2]
    psP = (psum[5], psum[6])
    psO = psum[7]
    names = ("consts poolown rec_in x_made chunk_used xm_ready xm_turned own worst_ready diag_ready rep_ready "
             "d_done oh_ready r_ready w_ready s_in l_ready g_ready e_ready p_made inv_ready p_ready p_turned pt_ready "
             "o_ready o_moved w_closed").split()
    (consts, poolown, rec_in, x_made, chunk_used, xm_ready, xm_turned, own, worst_ready, diag_ready,
     rep_ready, d_done, oh_ready, r_ready, w_ready, s_in, l_ready, g_ready, e_ready, p_made, inv_ready, p_ready,
     p_turned, pt_ready, o_ready, o_moved, w_closed) = (sem("any_" + n) for n in names)

    with nc.Block() as block:
        @block.sync
        def _(sp):
            longest = sp.value_load(tab[0:1, 2 * NB:2 * NB + 1], min_val=-NE, max_val=NE)
            with sp.If(longest > CHUNK):
                with sp.Fori(0, NB) as b:
                    row = sp.snap(b * (P * NP))
                    blocks_done = sp.snap(b + 1)
                    sp.wait_ge(e_ready, blocks_done)
                    sp.dma_start(S, logits_d.rearrange("b h l s -> (b h l s)")[bass.ds(row, P * NP)]
                                 .rearrange("(p n) -> p n", p=P)).then_inc(s_in, 16)
                    for sweep in range(2):
                        with sp.Fori(0, NCH) as c:
                            at = sp.snap(c * (CHUNK * REC))
                            used = sp.snap(b * (2 * NCH) + (c + (sweep * NCH + 1)))
                            sp.wait_ge(chunk_used, used)
                            sp.dma_start(rec.rearrange("p t c -> p (t c)"),
                                         rec_d.rearrange("e c -> (e c)")[bass.ds(at, CHUNK * REC)]
                                         .rearrange("(p n) -> p n", p=P)).then_inc(rec_in, 16)

        @block.gpsimd
        def _(pool):
            longest = pool.value_load(tab[0:1, 2 * NB:2 * NB + 1], min_val=-NE, max_val=NE)
            with pool.If(longest > CHUNK):
                pool.memset(minus_big, -BIG).then_inc(consts, 1)
                pool.memset(zeros, 0.0).then_inc(consts, 1)
                pool.memset(tiny, TINY).then_inc(consts, 1)
                pool.wait_ge(consts, 3)
                with pool.Fori(0, NB) as b:
                    for sweep in range(2):
                        with pool.Fori(0, NCH) as c:
                            v = b * (2 * NCH) + (c + sweep * NCH)
                            pool.wait_ge(rec_in, v * 16 + 16)
                            pool.tensor_tensor(miss, rec[:, :, 1:2].broadcast_to([P, CT, BN]),
                                               iota_n[:, bass.ds(b * BN, BN)].unsqueeze(1).broadcast_to([P, CT, BN]),
                                               ALU.subtract).then_inc(poolown, 1)
                            pool.wait_ge(poolown, v * 3 + 1)
                            pool.tensor_tensor(miss, miss, miss, ALU.mult).then_inc(poolown, 1)
                            pool.wait_ge(poolown, v * 3 + 2)
                            pool.tensor_tensor(miss, miss, minus_big.unsqueeze(1).broadcast_to([P, CT, BN]),
                                               ALU.mult).then_inc(poolown, 1)
                            pool.wait_ge(poolown, v * 3 + 3)
                            pool.tensor_tensor(X.rearrange("p t (h d) -> p t h d", h=H),
                                               rec[:, :, 2:REC].unsqueeze(3).broadcast_to([P, CT, H, BN]),
                                               miss.unsqueeze(2).broadcast_to([P, CT, H, BN]), ALU.add)\
                                .then_inc(x_made, 1)

        @block.vector
        def _(dve):
            longest = dve.value_load(tab[0:1, 2 * NB:2 * NB + 1], min_val=-NE, max_val=NE)
            with dve.If(longest > CHUNK):
                for s in (chunk_used, inv_ready):
                    dve.sem_inc(s, 1)
                dve.wait_ge(consts, 3)
                with dve.Fori(0, NB) as b:
                    dve.wait_ge(xm_turned, b + 1)
                    dve.memset(XM[:, 0, :], -BIG).then_inc(own, 1)
                    with dve.Fori(0, NCH) as c:
                        v = b * (2 * NCH) + c
                        u = b * (2 * NCH + 4) + c * 2
                        dve.wait_ge(x_made, v + 1)
                        dve.wait_ge(own, u + 1)
                        dve.tensor_reduce(XM[:, 1, :], X.rearrange("p t m -> p m t"), AX.X, ALU.max).then_inc(own, 1)
                        dve.wait_ge(own, u + 2)
                        dve.tensor_tensor(XM[:, 0, :], XM[:, 0, :], XM[:, 1, :], ALU.max).then_inc(own, 1)
                        dve.wait_ge(own, u + 3)
                        dve.sem_inc(chunk_used, 1)
                    dve.sem_inc(xm_ready, 1)
                    dve.wait_ge(xm_turned, b + 2)
                    dve.tensor_reduce(worst, psT, AX.X, ALU.max).then_inc(worst_ready, 1)
                    dve.wait_ge(worst_ready, b + 1)
                    dve.tensor_scalar(diag, ident[:, :], worst, -BIG / 10, ALU.mult, ALU.max).then_inc(diag_ready, 1)
                    with dve.Fori(0, NCH) as c:
                        v = b * (2 * NCH) + (c + NCH)
                        dve.wait_ge(rep_ready, b + 1)
                        dve.wait_ge(x_made, v + 1)
                        dve.tensor_tensor(X, X, psM.unsqueeze(1).broadcast_to([P, CT, P]), ALU.subtract)\
                           .then_inc(d_done, 1)
                        dve.wait_ge(w_ready, b * NCH + (c + 1))
                        for t in range(CT):
                            dve.tensor_scalar(onehot[:, t, :], iota_n[:, :], rec[:, t, 0:1], None, ALU.is_equal)\
                               .then_inc(oh_ready, 1)
                        dve.wait_ge(w_ready, b * NCH + (c + 2))
                        dve.sem_inc(chunk_used, 1)
                    dve.wait_ge(l_ready, b + 1)
                    dve.wait_ge(s_in, b * 16 + 16)
                    dve.tensor_tensor(L, L, S, ALU.add).then_inc(own, 1)
                    dve.wait_ge(own, b * (2 * NCH + 4) + (2 * NCH + 2))
                    dve.tensor_reduce(nguard, L, AX.X, ALU.max, negate=True).then_inc(g_ready, 1)
                    dve.wait_ge(e_ready, b + 2)
                    dve.wait_ge(p_turned, b + 1)
                    dve.tensor_tensor_reduce(PR[:, 0:HALF], lo[:, 0:HALF], L[:, 0:HALF], 1.0, 0.0, ALU.mult, ALU.add,
                                             total).then_inc(own, 1)
                    dve.wait_ge(own, b * (2 * NCH + 4) + (2 * NCH + 3))
                    dve.tensor_tensor_reduce(PR[:, HALF:NP], hi[:, 0:HALF], L[:, HALF:NP], 1.0, total, ALU.mult,
                                             ALU.add, guard).then_inc(own, 1)
                    dve.wait_ge(own, b * (2 * NCH + 4) + (2 * NCH + 4))
                    dve.tensor_scalar(total, guard, 1e-37, None, ALU.max).then_inc(p_made, 1)
                    dve.wait_ge(p_made, b + 1)
                    dve.reciprocal(inv, total).then_inc(inv_ready, 1)

        @block.scalar
        def _(act):
            longest = act.value_load(tab[0:1, 2 * NB:2 * NB + 1], min_val=-NE, max_val=NE)
            with act.If(longest > CHUNK):
                for s in (e_ready, pt_ready, o_moved):
                    act.sem_inc(s, 1)
                act.preload_act_table_set("natural_log_exp_and_others")
                act.wait_ge(consts, 3)
                with act.Fori(0, NT) as j:
                    with act.Fori(0, BPT) as k:
                        b = j * BPT + k
                        with act.Fori(0, NCH) as c:
                            act.wait_ge(d_done, b * NCH + (c + 1))
                            act.wait_ge(w_ready, b * NCH + (c + 1))
                            act.activation(R, X, ACT.Exp).then_inc(r_ready, 1)
                        act.wait_ge(w_closed, b + 1)
                        act.wait_ge(inv_ready, b + 1)
                        act.activation(L[:, 0:HALF], lo[:, 0:HALF], ACT.Ln, bias=tiny)
                        act.activation(L[:, HALF:NP], hi[:, 0:HALF], ACT.Ln, bias=tiny).then_inc(l_ready, 1)
                        act.wait_ge(g_ready, b + 1)
                        act.activation(L, S, ACT.Exp, bias=nguard).then_inc(e_ready, 1)
                        act.wait_ge(inv_ready, b + 2)
                        act.activation(PR, PR, ACT.Copy, scale=inv).then_inc(p_ready, 1)
                        act.wait_ge(p_turned, b + 2)
                        act.wait_ge(o_ready, j + 1)
                        first = psP[0][:, :].rearrange("s (t h d) -> s t h d", t=4, h=H)
                        for t in range(4):
                            act.activation(PT[:, t, :, bass.ds(k * BN, BN)], first[:, t], ACT.Copy)
                        act.activation(PT[:, 4, :, bass.ds(k * BN, BN)],
                                       psP[1][:, 0:P].rearrange("s (h d) -> s h d", h=H), ACT.Copy)\
                           .then_inc(pt_ready, 1)
                    act.wait_ge(o_ready, j + 2)
                    act.activation(hT[:, :, bass.ds(j * P, P)], psO[:, :].rearrange("p (c d) -> p c d", c=DC),
                                   ACT.Copy).then_inc(o_moved, 1)

        @block.tensor
        def _(pe):
            longest = pe.value_load(tab[0:1, 2 * NB:2 * NB + 1], min_val=-NE, max_val=NE)
            with pe.If(longest > CHUNK):
                for s in (w_ready, xm_turned, p_turned, o_ready):
                    pe.sem_inc(s, 1)
                pe.wait_ge(consts, 3)
                with pe.Fori(0, NT) as j:
                    with pe.Fori(0, BPT) as k:
                        b = j * BPT + k
                        pe.wait_ge(xm_ready, b + 1)
                        pe.transpose(psT, XM[:, 0, :], ident[:, :]).then_inc(xm_turned, 1)
                        pe.wait_ge(diag_ready, b + 1)
                        pe.matmul(psM, ones[:, :], diag, start=True, stop=True).then_inc(rep_ready, 1)
                        pe.wait_ge(inv_ready, b + 1)
                        pe.matmul(lo[:, 0:HALF], zeros, iota_n[:, 0:HALF], start=True, stop=False)
                        pe.matmul(hi[:, 0:HALF], zeros, iota_n[:, 0:HALF], start=True, stop=False)
                        with pe.Fori(0, NCH) as c:
                            v = b * NCH + c
                            pe.wait_ge(r_ready, v + 1)
                            pe.wait_ge(oh_ready, v * CT + CT)
                            for t in range(CT):
                                pe.matmul(lo[:, 0:HALF], R[:, t, :], onehot[:, t, 0:HALF], start=False, stop=False)
                                last = pe.matmul(hi[:, 0:HALF], R[:, t, :], onehot[:, t, HALF:NP], start=False,
                                                 stop=False)
                            last.then_inc(w_ready, 1)
                        pe.matmul(lo[:, 0:HALF], zeros, iota_n[:, 0:HALF], start=False, stop=True)
                        pe.matmul(hi[:, 0:HALF], zeros, iota_n[:, 0:HALF], start=False, stop=True)\
                          .then_inc(w_closed, 1)
                        pe.wait_ge(p_ready, b + 1)
                        pe.wait_ge(pt_ready, b + 1)
                        for t in range(NT):
                            to = psP[t // 4][:, (t % 4) * P:(t % 4 + 1) * P]
                            last = pe.transpose(to, PR[:, t * P:(t + 1) * P], ident[:, :])
                        last.then_inc(p_turned, 1)
                    pe.wait_ge(pt_ready, j * BPT + (BPT + 1))
                    pe.wait_ge(o_moved, j + 1)
                    for h in range(H):
                        r = slice(DH * (h % 2), DH * (h % 2 + 1))
                        for t in range(NT):
                            last = pe.matmul(psO[r, (h // 2) * P:(h // 2 + 1) * P], vs[:, t, h * DH:(h + 1) * DH],
                                             PT[:, t, h, :], start=t == 0, stop=t == NT - 1)
                    last.then_inc(o_ready, 1)


_INS = ['x', 'src', 'dst', 'edge_attr_8', 'edge_attr_8_n2', 'L0_gnn_Wqkv', 'L0_gnn_bqkv', 'L0_gnn_Wo', 'L0_gnn_bo',
        'L0_gnn_ln1_g', 'L0_gnn_ln1_b', 'L0_gnn_W1', 'L0_gnn_b1', 'L0_gnn_W2', 'L0_gnn_b2', 'L0_gnn_ln2_g',
        'L0_gnn_ln2_b', 'L0_ffn_gate_w', 'L0_ffn_biases', 'L0_ffn_w1', 'L0_ffn_w3', 'L0_ffn_w2', 'L0_ffn_sw1',
        'L0_ffn_sw3', 'L0_ffn_sw2']


def kernel(**inputs):
    import numpy as _np
    import concourse.bacc as _bacc
    from concourse import mybir as _mybir
    from concourse.bass_utils import run_bass_kernel_spmd as _run

    nc = _bacc.Bacc("TRN2", target_bir_lowering=False, num_devices=1)
    arrays, args = {}, []
    for name in _INS:
        a = _np.ascontiguousarray(inputs[name])
        arrays[f"in_{name}"] = a
        args.append(nc.dram_tensor(f"in_{name}", a.shape, _mybir.dt.from_np(a.dtype), kind="ExternalInput").ap())
    out = nc.dram_tensor("out", (N, D), F32, kind="ExternalOutput").ap()
    program(nc, *args, out)
    r = _run(nc, [arrays], core_ids=[0])
    return r.results[0]["out"]
```

```python
from contextlib import ExitStack

import concourse.bass as bass
from concourse import mybir

P = 128
F32 = mybir.dt.float32
I32 = mybir.dt.int32
U32 = mybir.dt.uint32
ALU = mybir.AluOpType
ACT = mybir.ActivationFunctionType
AX = mybir.AxisListType

N = 625
D = 512
DC = D // P
H = 8
DH = D // H
NE = 20000
FF = 4 * D
HID = 1024
HC = HID // P
EX = 8
NT = -(-N // P)
NP = NT * P
HALF = NP // 2
LAST = N - (NT - 1) * P
EPS = 1e-5
BN = P // H
NB = NP // BN
BPT = P // BN
CT = 5
CHUNK = CT * P
EP, EJ = 125, NE // 125
REC = 2 + H
BIG = 1e30
TINY = 2.0 ** -64
SLOT = 4096
CB = 2
CAP = CB * P


def node_tiles(ap):
    full = ap[0:(NT - 1) * P, :].rearrange("(t p) n -> p t n", p=P)
    return full, ap[(NT - 1) * P:N, :]


def wait_past(eng, sem, value):
    if not isinstance(value, int) or value > 0:
        eng.wait_ge(sem, value)


def program(nc, x, src, dst, edge_attr_8, edge_attr_8_n2, Wqkv, bqkv, Wo, bo, ln1_g, ln1_b, W1, b1, W2, b2,
            ln2_g, ln2_b, gate_w, biases, w1, w3, w2, sw1, sw3, sw2, out):
    with ExitStack() as ctx:
        def sb(name, shape, dt=F32):
            return ctx.enter_context(nc.sbuf_tensor(name, shape, dt))

        def sem(name):
            return ctx.enter_context(nc.semaphore(name))

        wts = sb("wts", [P, 6 * SLOT])
        big = sb("big", [P, 16, NP])
        xs = sb("xs", [P, NT, D])
        hT = sb("hT", [P, DC, NP])
        vs = sb("vs", [P, NT, D])
        work = sb("work", [P, 12 * NP])
        iota_n = sb("iota_n", [P, NP])
        ident = sb("ident", [P, P])
        ones = sb("ones", [P, P])
        below = sb("below", [P, P])
        XM = sb("XM", [P, 2, P])
        small = sb("small", [P, 64])
        tab_f = sb("tab_f", [1, 3 * NB + 1])
        tab = sb("tab", [1, 2 * NB + 1], I32)
        most = sb("most", [1, 1], I32)
        psum = [ctx.enter_context(nc.psum_tensor(f"ps{i}", [P, 512], F32)) for i in range(8)]
        logits_d = nc.dram_tensor("logits_scratch", [NB, H, BN, NP], F32, kind="Internal").ap()
        rec_d = nc.dram_tensor("record_scratch", [NE + CHUNK, REC], F32, kind="Internal").ap()
        rows_d = nc.dram_tensor("slot_rows", [EX * CAP, D], F32, kind="Internal").ap()
        y_d = nc.dram_tensor("slot_results", [EX * CAP, D], F32, kind="Internal").ap()
        w_in = [sem(f"w_in{i}") for i in range(2)]

        edge_records(nc, sem, src, dst, edge_attr_8, edge_attr_8_n2, rec_d, rows_d, wts, iota_n, ident, ones, below,
                     psum, tab_f, tab, small)
        projections(nc, sem, x, Wqkv, bqkv, Wo, W1, W2, ln1_g, ln1_b, logits_d, wts, big, xs, hT, vs, work, small,
                    ident, psum)
        attention(nc, sem, rec_d, logits_d, big, hT, vs, work, iota_n, ident, ones, XM, tab, small, psum)
        attention_any(nc, sem, rec_d, logits_d, big, hT, vs, work, iota_n, ident, ones, XM, tab, small, psum)
        feed_forward(nc, sem, x, bo, ln2_g, ln2_b, b1, b2, wts, big, xs, hT, vs, work, small, ident, psum)
        routing(nc, sem, w_in, gate_w, biases, w1, w3, w2, sw1, sw3, sw2, rows_d, wts, big, xs, hT, vs, work, iota_n,
                below, ones, most, small, ident, psum)
        experts_routed(nc, sem, w_in, w1, w3, w2, rows_d, y_d, out, wts, big, xs, hT, vs, work, most, ident, psum)
        experts_all(nc, sem, w_in, w1, w3, w2, out, wts, big, xs, hT, work, most, psum)


class Order:

    def __init__(self, eng, sem, base=0):
        self.eng, self.sem, self.base, self.n = eng, sem, base, 0

    def done(self, ins):
        ins.then_inc(self.sem, 1)
        self.n += 1

    def wait(self):
        self.eng.wait_ge(self.sem, self.base + self.n)

    def link(self, ins):
        self.done(ins)
        self.wait()


def edge_records(nc, sem, src, dst, edge_attr_8, edge_attr_8_n2, rec_d, rows_d, wts, iota_n, ident, ones, below, psum,
                 tab_f, tab, small):
    ints = wts[0:EP, 0:2 * EJ].bitcast(I32).rearrange("p (a j) -> p a j", a=2)
    blk_i = wts[0:EP, 320:320 + EJ].bitcast(I32)
    blk = wts[0:EP, 480:480 + EJ]
    near = wts[0:EP, 640:640 + EJ * H]
    path = wts[0:EP, 1920:1920 + EJ * H]
    rec = wts[0:EP, 3200:3200 + EJ * REC].rearrange("p (j c) -> p j c", c=REC)
    eq = wts[0:EP, 4800:4800 + EJ * NB].rearrange("p (j b) -> p j b", b=NB)
    pos = wts[0:EP, 11200:11200 + EJ * NB].rearrange("p (j b) -> p j b", b=NB)
    e_up = wts[0:EP, 17600:17600 + EJ]
    e_down = wts[0:EP, 17760:17760 + EJ]
    ends = wts[0:EP, 17920:17920 + 2 * NB]
    pad = wts[:, 18000:18000 + CT * REC]
    zeros = wts[:, 18432:18432 + D]
    ends_t = small[0:2 * NB, 0:1]
    loaded, consts, own, turned, stored, tabled, poolown = map(
        sem, ("edge_loaded", "edge_consts", "edge_own", "edge_turned", "edge_stored", "edge_tabled", "edge_poolown"))

    with nc.Block() as block:
        @block.sync
        def _(sp):
            sp.dma_start(ints[:, 0, :], src.rearrange("(p j) -> p j", j=EJ)).then_inc(loaded, 16)
            sp.dma_start(ints[:, 1, :], dst.rearrange("(p j) -> p j", j=EJ)).then_inc(loaded, 16)
            sp.dma_start(near, edge_attr_8.rearrange("(p j) h -> p (j h)", j=EJ)).then_inc(loaded, 16)
            sp.dma_start(path, edge_attr_8_n2.rearrange("(p j) h -> p (j h)", j=EJ)).then_inc(loaded, 16)
            sp.wait_ge(consts, 9)
            sp.dma_start(rows_d.rearrange("(a p) n -> p a n", p=P),
                         zeros.unsqueeze(1).broadcast_to([P, EX * CB, D])).then_inc(stored, 16)
            sp.dma_start(rec_d[NE:NE + CHUNK, :].rearrange("(p t) c -> p (t c)", t=CT), pad).then_inc(stored, 16)
            sp.wait_ge(own, 3)
            sp.dma_start(rec_d[0:NE, :].rearrange("(p j) c -> p (j c)", j=EJ),
                         rec.rearrange("p j c -> p (j c)")).then_inc(stored, 16)
            sp.wait_ge(stored, 48)

        @block.gpsimd
        def _(pool):
            exact = dict(allow_small_or_imprecise_dtypes=True)
            pool.memset(ident[:, :], 0.0).then_inc(poolown, 1)
            pool.iota(iota_n[:, :], [[1, NP]], base=0, channel_multiplier=0, **exact).then_inc(consts, 1)
            pool.iota(e_up, [[1, EJ]], base=1, channel_multiplier=EJ, **exact).then_inc(consts, 1)
            pool.iota(e_down, [[-1, EJ]], base=NE, channel_multiplier=-EJ, **exact).then_inc(consts, 1)
            pool.memset(ones[:, :], 1.0).then_inc(consts, 1)
            pool.memset(pad, 0.0).then_inc(poolown, 1)
            pool.memset(below[:, :], 1.0).then_inc(poolown, 1)
            pool.wait_ge(poolown, 3)
            pool.affine_select(out=ident[:, :], in_=ident[:, :], compare_op=ALU.not_equal, fill=1.0, base=0,
                               pattern=[[-1, P]], channel_multiplier=1).then_inc(consts, 1)
            pool.memset(pad.rearrange("p (t c) -> p t c", c=REC)[:, :, 1:2], -1.0).then_inc(consts, 2)
            pool.memset(zeros, 0.0).then_inc(consts, 1)
            pool.affine_select(out=below[:, :], in_=below[:, :], compare_op=ALU.is_gt, fill=0.0, base=0,
                               pattern=[[1, P]], channel_multiplier=-1).then_inc(consts, 1)

        @block.vector
        def _(dve):
            o = Order(dve, own)
            dve.wait_ge(loaded, 64)
            o.done(dve.tensor_copy(rec[:, :, 0], ints[:, 0, :]))
            o.done(dve.tensor_copy(rec[:, :, 1], ints[:, 1, :]))
            o.done(dve.tensor_tensor(rec[:, :, 2:REC], near.rearrange("p (j h) -> p j h", h=H),
                                     path.rearrange("p (j h) -> p j h", h=H), ALU.add))
            o.link(dve.tensor_scalar(blk_i, ints[:, 1, :], BN.bit_length() - 1, None, ALU.arith_shift_right))
            o.link(dve.tensor_copy(blk, blk_i))
            dve.wait_ge(consts, 9)
            o.link(dve.tensor_tensor(eq, blk.unsqueeze(2).broadcast_to([EP, EJ, NB]),
                                     iota_n[0:EP, 0:NB].unsqueeze(1).broadcast_to([EP, EJ, NB]), ALU.is_equal))
            for k, e in enumerate((e_up, e_down)):
                o.link(dve.tensor_tensor(pos, eq, e.unsqueeze(2).broadcast_to([EP, EJ, NB]), ALU.mult))
                o.link(dve.tensor_reduce(ends[:, k * NB:(k + 1) * NB], pos.rearrange("p j b -> p b j"), AX.X,
                                         ALU.max))
            dve.wait_ge(turned, 1)
            o.link(dve.tensor_reduce(ends_t, psum[0][0:2 * NB, 0:EP], AX.X, ALU.max))
            dve.wait_ge(turned, 2)
            o.link(dve.tensor_scalar(tab_f[0:1, 0:NB], psum[1][0:1, NB:2 * NB], -1.0, float(NE), ALU.mult, ALU.add))
            o.link(dve.tensor_copy(tab_f[0:1, NB:2 * NB], psum[1][0:1, 0:NB]))
            o.link(dve.tensor_tensor(tab_f[0:1, 2 * NB + 1:3 * NB + 1], tab_f[0:1, NB:2 * NB], tab_f[0:1, 0:NB],
                                     ALU.subtract))
            o.link(dve.tensor_reduce(tab_f[0:1, 2 * NB:2 * NB + 1], tab_f[0:1, 2 * NB + 1:3 * NB + 1], AX.X, ALU.max))
            dve.tensor_copy(tab[0:1, :], tab_f[0:1, 0:2 * NB + 1]).then_inc(tabled, 1)

        @block.tensor
        def _(pe):
            pe.wait_ge(consts, 9)
            pe.wait_ge(own, 10)
            pe.transpose(psum[0][0:2 * NB, 0:EP], ends, ident[0:EP, 0:EP]).then_inc(turned, 1)
            pe.wait_ge(own, 11)
            pe.matmul(psum[1][0:1, 0:2 * NB], ends_t, ident[0:2 * NB, 0:2 * NB], start=True,
                      stop=True).then_inc(turned, 1)


def projections(nc, sem, x, Wqkv, bqkv, Wo, W1, W2, ln1_g, ln1_b, logits_d, wts, big, xs, hT, vs, work, small, ident,
                psum):
    wqkv = wts[:, 0:DC * 3 * D].rearrange("p (c n) -> p c n", c=DC)
    wo = wts[:, 3 * DC * D:4 * DC * D].rearrange("p (c n) -> p c n", c=DC)
    w1 = wts[:, 2 * SLOT:2 * SLOT + DC * FF].rearrange("p (c n) -> p c n", c=DC)
    w2 = wts[:, 4 * SLOT:4 * SLOT + DC * FF].rearrange("p (c n) -> p c n", n=D)
    g1 = work[:, 0:D]
    s1 = work[:, D:2 * D]
    bv = work[:, 2 * D:3 * D]
    hrow = [work[:, (3 + i) * D:(4 + i) * D] for i in range(2)]
    stage = [work[:, 6 * NP + i * NP:6 * NP + (i + 1) * NP] for i in range(2)]
    eps = small[:, 0:1]
    bqk_row = work[0:2 * DC, 5 * D:5 * D + P]
    bqk = small[:, 1:9]
    std = small[:, 10:15]
    rstd = small[:, 15:20]
    mv = small[:, 20:30].rearrange("p (t c) -> p t c", c=2)
    stats = small[:, 30:60].rearrange("p (t c) -> p t c", c=6)
    pairs = [(h, t) for t in range(NT) for h in range(H)]
    (x_in, vec_in, wqkv_in, later_in, zeroed, own, stds, rows, turned, moved, qk_ps, qk_sb, v_ps, v_sb, s_ps, s_act,
     s_dve, s_out, bqk_ready) = map(sem, (
        "x_in", "vec_in", "wqkv_in", "later_in", "tail_zeroed", "ln_own", "ln_stds", "h_rows", "h_turned", "h_moved",
        "qk_ps", "qk_sb", "v_ps", "v_sb", "s_ps", "s_act", "s_dve", "s_out", "bqk_ready"))
    s_out = [s_out, sem("s_out1")]
    bqk_turned = sem("bqk_turned")
    scale = float(D) ** -0.5

    with nc.Block() as block:
        @block.sync
        def _(sp):
            full, rest = node_tiles(x)
            sp.wait_ge(zeroed, 1)
            sp.dma_start(xs[:, 0:NT - 1, :], full).then_inc(x_in, 16)
            sp.dma_start(xs[0:LAST, NT - 1, :], rest).then_inc(x_in, 16)
            sp.dma_start(wqkv, Wqkv.rearrange("(c p) n -> p c n", p=P)).then_inc(wqkv_in, 16)
            sp.dma_start(bqk_row, bqkv[0:2 * D].rearrange("(m p) -> m p", p=P)).then_inc(vec_in, 16)
            for to, vec in ((g1, ln1_g), (s1, ln1_b), (bv, bqkv[2 * D:3 * D])):
                sp.dma_start(to, vec.rearrange("(a n) -> a n", a=1).broadcast_to([P, D])).then_inc(vec_in, 16)
            sp.dma_start(wo, Wo.rearrange("(c p) n -> p c n", p=P)).then_inc(later_in, 16)
            sp.dma_start(w1, W1.rearrange("(c p) n -> p c n", p=P)).then_inc(later_in, 16)
            sp.dma_start(w2, W2.rearrange("(c p) n -> p c n", p=P)).then_inc(later_in, 16)
            for i, (h, t) in enumerate(pairs):
                done = s_act if i % 2 == 0 else s_dve
                sp.wait_ge(done, i // 2 + 1)
                sp.dma_start(logits_d[t * BPT:(t + 1) * BPT, h, :, :].rearrange("b l s -> b l s"),
                             stage[i % 2]).then_inc(s_out[i % 2], 16)
            sp.wait_ge(s_out[0], 16 * 20)
            sp.wait_ge(s_out[1], 16 * 20)
            sp.wait_ge(later_in, 48)

        @block.gpsimd
        def _(pool):
            pool.memset(xs[:, NT - 1, :], 0.0).then_inc(zeroed, 1)

        @block.vector
        def _(dve):
            o = Order(dve, own)
            dve.memset(eps, EPS).then_inc(own, 1)
            o.n += 1
            dve.wait_ge(x_in, 32)
            for norm in range(2):
                for t in range(NT):
                    o.done(dve.bn_stats(stats[:, t, :], xs[:, t, :]))
                o.wait()
                for t in range(NT):
                    o.done(dve.bn_aggr(mv[:, t, :], stats[:, t, :]))
                o.wait()
                dve.wait_ge(stds, norm + 1)
                o.link(dve.reciprocal(rstd, std))
                if norm == 0:
                    for t in range(NT):
                        o.done(dve.tensor_scalar(xs[:, t, :], xs[:, t, :], mv[:, t, 0:1], rstd[:, t:t + 1],
                                                 ALU.subtract, ALU.mult))
                    o.wait()
            dve.wait_ge(vec_in, 64)
            dve.wait_ge(bqk_turned, 1)
            dve.tensor_scalar(bqk[:, 0:DC], psum[7][:, 0:DC], scale, None, ALU.mult).then_inc(bqk_ready, 1)
            dve.tensor_copy(bqk[:, DC:2 * DC], psum[7][:, DC:2 * DC]).then_inc(bqk_ready, 1)
            for t in range(NT):
                r = hrow[t % 2]
                if t >= 2:
                    dve.wait_ge(turned, t - 1)
                o.link(dve.tensor_scalar(r, xs[:, t, :], mv[:, t, 0:1], rstd[:, t:t + 1], ALU.subtract, ALU.mult))
                o.link(dve.tensor_tensor(r, r, g1, ALU.mult))
                dve.tensor_tensor(r, r, s1, ALU.add).then_inc(rows, 1)
            for t in range(NT):
                dve.wait_ge(v_ps, t + 1)
                dve.tensor_tensor(vs[:, t, :], psum[4 + t % 2][:, :], bv, ALU.add).then_inc(v_sb, 1)
            for i in range(1, len(pairs), 2):
                dve.wait_ge(s_ps, i + 1)
                if i >= 2:
                    dve.wait_ge(s_out[1], 16 * (i // 2))
                a, b = (psum[2 * (i % 4)], psum[2 * (i % 4) + 1])
                dve.tensor_copy(stage[1][:, 0:HALF], a[:, 0:HALF])
                dve.tensor_copy(stage[1][:, HALF:NP], b[:, 0:HALF]).then_inc(s_dve, 1)

        @block.scalar
        def _(act):
            for norm in range(2):
                act.wait_ge(own, 1 + 10 + 16 * norm)
                act.activation(std, mv[:, :, 1], ACT.Sqrt, bias=eps).then_inc(stds, 1)
            for t in range(NT):
                act.wait_ge(turned, t + 1)
                act.activation(hT[:, :, t * P:(t + 1) * P], psum[t % 2][:, :].rearrange("p (c n) -> p c n", c=DC),
                               ACT.Copy).then_inc(moved, 1)
            act.wait_ge(bqk_ready, 2)
            for m in range(2 * DC):
                for half in range(2):
                    i = 2 * m + half
                    act.wait_ge(qk_ps, i + 1)
                    act.activation(big[:, m, half * HALF:(half + 1) * HALF], psum[i % 4][:, 0:HALF], ACT.Identity,
                                   bias=bqk[:, m:m + 1], scale=scale if m < DC else 1.0).then_inc(qk_sb, 1)
            for i in range(0, len(pairs), 2):
                act.wait_ge(s_ps, i + 1)
                if i >= 2:
                    act.wait_ge(s_out[0], 16 * (i // 2))
                a, b = (psum[2 * (i % 4)], psum[2 * (i % 4) + 1])
                act.activation(stage[0][:, 0:HALF], a[:, 0:HALF], ACT.Copy)
                act.activation(stage[0][:, HALF:NP], b[:, 0:HALF], ACT.Copy).then_inc(s_act, 1)

        @block.tensor
        def _(pe):
            pe.wait_ge(vec_in, 64)
            pe.transpose(psum[7][:, 0:2 * DC], bqk_row, ident[0:2 * DC, 0:2 * DC]).then_inc(bqk_turned, 1)
            for t in range(NT):
                pe.wait_ge(rows, t + 1)
                if t >= 2:
                    pe.wait_ge(moved, t - 1)
                for c in range(DC):
                    last = pe.transpose(psum[t % 2][:, c * P:(c + 1) * P], hrow[t % 2][:, c * P:(c + 1) * P],
                                        ident[:, :])
                last.then_inc(turned, 1)
            pe.wait_ge(moved, NT)
            pe.wait_ge(wqkv_in, 16)
            for m in range(2 * DC):
                for half in range(2):
                    i = 2 * m + half
                    if i >= 4:
                        pe.wait_ge(qk_sb, i - 3)
                    for c in range(DC):
                        last = pe.matmul(psum[i % 4][:, 0:HALF], wqkv[:, c, m * P:(m + 1) * P],
                                         hT[:, c, half * HALF:(half + 1) * HALF], start=c == 0, stop=c == DC - 1)
                    last.then_inc(qk_ps, 1)
            for t in range(NT):
                if t >= 2:
                    pe.wait_ge(v_sb, t - 1)
                for c in range(DC):
                    last = pe.matmul(psum[4 + t % 2][:, :], hT[:, c, t * P:(t + 1) * P], wqkv[:, c, 2 * D:3 * D],
                                     start=c == 0, stop=c == DC - 1)
                last.then_inc(v_ps, 1)
            pe.wait_ge(qk_sb, 4 * DC)
            pe.wait_ge(v_sb, NT)
            for i, (h, t) in enumerate(pairs):
                r = slice(DH * (h % 2), DH * (h % 2 + 1))
                if i >= 4:
                    pe.wait_ge(s_act if i % 2 == 0 else s_dve, i // 2 - 1)
                for half in range(2):
                    last = pe.matmul(psum[2 * (i % 4) + half][:, 0:HALF],
                                     big[r, DC + h // 2, t * P:(t + 1) * P],
                                     big[r, h // 2, half * HALF:(half + 1) * HALF], start=True, stop=True)
                last.then_inc(s_ps, 1)


def attention(nc, sem, rec_d, logits_d, big, hT, vs, work, iota_n, ident, ones, XM, tab, small, psum):
    X = [work[:, i * CT * P:(i + 1) * CT * P].rearrange("p (t m) -> p t m", t=CT) for i in range(2)]
    R = work[:, 2 * NP:3 * NP].rearrange("p (t m) -> p t m", t=CT)
    onehot = work[:, 3 * NP:8 * NP].rearrange("p (t s) -> p t s", t=CT)
    S = [work[:, (8 + i) * NP:(9 + i) * NP] for i in range(2)]
    L = work[:, 10 * NP:11 * NP]
    PR = work[:, 11 * NP:12 * NP]
    PT = big[:, 8:16, :].rearrange("p a n -> p (a n)").rearrange("p (t h d) -> p t h d", t=NT, h=H)
    rec = [big[:, i, 0:CT * REC].rearrange("p (t c) -> p t c", t=CT) for i in range(2)]
    miss = [big[:, 2 + i, 0:CT * BN].rearrange("p (t d) -> p t d", t=CT) for i in range(2)]
    minus_big = big[:, 4, 0:1]
    diag = big[:, 4, P:2 * P]
    tiny = small[:, 0:1]
    guard, nguard, total, inv, worst = (small[:, k:k + 1] for k in range(1, 6))
    psT, psM = psum[0][:, 0:P], psum[0][:, P:2 * P]
    psW = [(psum[1], psum[2]), (psum[3], psum[4])]
    psP = (psum[5], psum[6])
    psO = psum[7]

    (consts, poolown, x_ready, xm_ready, xm_turned, own, diag_ready, rep_ready, d_done, r_ready, oh_ready,
     l_ready, g_ready, e_ready, p_made, inv_ready, p_ready, p_turned, pt_ready, o_ready, o_moved, oh_used) = map(sem, (
         "at_consts", "at_poolown", "x_ready", "xm_ready", "xm_turned", "at_own", "diag_ready", "rep_ready", "d_done",
         "r_ready", "oh_ready", "l_ready", "g_ready", "e_ready", "p_made", "inv_ready", "p_ready",
         "p_turned", "pt_ready", "o_ready", "o_moved", "oh_used"))
    worst_ready = sem("worst_ready")
    rec_in = [sem(f"rec_in{i}") for i in range(2)]
    s_in = [sem(f"s_in{i}") for i in range(2)]
    half = BPT // 2

    with nc.Block() as block:
        @block.sync
        def _(sp):
            longest = sp.value_load(tab[0:1, 2 * NB:2 * NB + 1], min_val=-NE, max_val=NE)
            with sp.If(longest < CHUNK + 1):
                def tile(j):
                    for k in range(BPT):
                        b = j * BPT + k
                        start = sp.value_load(tab[0:1, bass.ds(b, 1)], min_val=0, max_val=NE)
                        at = sp.snap(start * REC)
                        row = b * (P * NP) if isinstance(b, int) else sp.snap(b * (P * NP))
                        free = b - 1
                        free = free if isinstance(free, int) else sp.snap(free)
                        hot = free * CT if isinstance(free, int) else sp.snap(free * CT)
                        wait_past(sp, oh_ready, hot)
                        wait_past(sp, x_ready, free)
                        sp.dma_start(rec[k % 2].rearrange("p t c -> p (t c)"),
                                     rec_d.rearrange("e c -> (e c)")[bass.ds(at, CHUNK * REC)].rearrange("(p n) -> p n", p=P))\
                          .then_inc(rec_in[k % 2], 16)
                        wait_past(sp, e_ready, free)
                        sp.dma_start(S[k % 2], logits_d.rearrange("b h l s -> (b h l s)")[bass.ds(row, P * NP)].rearrange("(p n) -> p n", p=P))\
                          .then_inc(s_in[k % 2], 16)

                tile(0)
                with sp.Fori(1, NT) as j:
                    tile(j)

        @block.gpsimd
        def _(pool):
            longest = pool.value_load(tab[0:1, 2 * NB:2 * NB + 1], min_val=-NE, max_val=NE)
            with pool.If(longest < CHUNK + 1):
                pool.memset(minus_big, -BIG).then_inc(consts, 1)
                pool.memset(tiny, TINY).then_inc(consts, 1)
                pool.wait_ge(consts, 2)
                def tile(j):
                    for k in range(BPT):
                        b = j * BPT + k
                        m = miss[k % 2]
                        wait_past(pool, rec_in[k % 2], 16 * half * j + 16 * (k // 2 + 1))
                        pool.tensor_tensor(m, rec[k % 2][:, :, 1:2].broadcast_to([P, CT, BN]),
                                           iota_n[:, bass.ds(b * BN, BN)].unsqueeze(1).broadcast_to([P, CT, BN]),
                                           ALU.subtract).then_inc(poolown, 1)
                        wait_past(pool, poolown, 3 * b + 1)
                        pool.tensor_tensor(m, m, m, ALU.mult).then_inc(poolown, 1)
                        wait_past(pool, poolown, 3 * b + 2)
                        pool.tensor_tensor(m, m, minus_big.unsqueeze(1).broadcast_to([P, CT, BN]), ALU.mult)\
                            .then_inc(poolown, 1)
                        wait_past(pool, poolown, 3 * b + 3)
                        wait_past(pool, r_ready, b - 1)
                        pool.tensor_tensor(X[k % 2].rearrange("p t (h d) -> p t h d", h=H),
                                           rec[k % 2][:, :, 2:REC].unsqueeze(3).broadcast_to([P, CT, H, BN]),
                                           m.unsqueeze(2).broadcast_to([P, CT, H, BN]), ALU.add).then_inc(x_ready, 1)

                tile(0)
                with pool.Fori(1, NT) as j:
                    tile(j)

        @block.vector
        def _(dve):
            longest = dve.value_load(tab[0:1, 2 * NB:2 * NB + 1], min_val=-NE, max_val=NE)
            with dve.If(longest < CHUNK + 1):
                dve.wait_ge(consts, 2)

                def onehots(b, k, tiles):
                    for t in tiles:
                        wait_past(dve, oh_used, CT * (b - 1) + t + 1)
                        dve.tensor_scalar(onehot[:, t, :], iota_n[:, :], rec[k % 2][:, t, 0:1], None, ALU.is_equal)\
                           .then_inc(oh_ready, 1)

                def front(j, k):
                    b = j * BPT + k
                    wait_past(dve, x_ready, b + 1)
                    dve.tensor_reduce(XM[:, k % 2, :], X[k % 2].rearrange("p t m -> p m t"), AX.X, ALU.max)\
                       .then_inc(xm_ready, 1)
                    onehots(b, k, (0, 1))
                    wait_past(dve, xm_turned, b + 1)
                    dve.tensor_reduce(worst, psT, AX.X, ALU.max).then_inc(worst_ready, 1)
                    wait_past(dve, worst_ready, b + 1)
                    dve.tensor_scalar(diag, ident[:, :], worst, -BIG / 10, ALU.mult, ALU.max).then_inc(diag_ready, 1)
                    onehots(b, k, (2, 3, 4))
                    wait_past(dve, rep_ready, b + 1)
                    dve.tensor_tensor(X[k % 2], X[k % 2], psM.unsqueeze(1).broadcast_to([P, CT, P]), ALU.subtract)\
                       .then_inc(d_done, 1)

                def back(j, k):
                    b = j * BPT + k
                    lo, hi = psW[k % 2]
                    wait_past(dve, l_ready, b + 1)
                    wait_past(dve, s_in[k % 2], 16 * half * j + 16 * (k // 2 + 1))
                    dve.tensor_tensor(L, L, S[k % 2], ALU.add).then_inc(own, 1)
                    wait_past(dve, own, 3 * b + 1)
                    dve.tensor_reduce(nguard, L, AX.X, ALU.max, negate=True).then_inc(g_ready, 1)
                    wait_past(dve, e_ready, b + 1)
                    wait_past(dve, p_turned, b)
                    dve.tensor_tensor_reduce(PR[:, 0:HALF], lo[:, 0:HALF], L[:, 0:HALF], 1.0, 0.0, ALU.mult, ALU.add,
                                             total).then_inc(own, 1)
                    wait_past(dve, own, 3 * b + 2)
                    dve.tensor_tensor_reduce(PR[:, HALF:NP], hi[:, 0:HALF], L[:, HALF:NP], 1.0, total, ALU.mult, ALU.add,
                                             guard).then_inc(own, 1)
                    wait_past(dve, own, 3 * b + 3)
                    dve.tensor_scalar(total, guard, 1e-37, None, ALU.max).then_inc(p_made, 1)
                    wait_past(dve, p_made, b + 1)
                    dve.reciprocal(inv, total).then_inc(inv_ready, 1)

                def tile(j):
                    for k in range(BPT):
                        front(j, k)
                        if k:
                            back(j, k - 1)
                    back(j, BPT - 1)
                    wait_past(dve, o_ready, j + 1)
                    dve.tensor_copy(hT[:, :, bass.ds(j * P, P)], psO[:, :].rearrange("p (c d) -> p c d", c=DC))\
                       .then_inc(o_moved, 1)

                tile(0)
                with dve.Fori(1, NT) as j:
                    tile(j)

        @block.scalar
        def _(act):
            longest = act.value_load(tab[0:1, 2 * NB:2 * NB + 1], min_val=-NE, max_val=NE)
            with act.If(longest < CHUNK + 1):
                act.preload_act_table_set("natural_log_exp_and_others")
                act.wait_ge(consts, 2)

                def weigh(j, k):
                    b = j * BPT + k
                    wait_past(act, d_done, b + 1)
                    wait_past(act, oh_used, CT * b)
                    act.activation(R, X[k % 2], ACT.Exp).then_inc(r_ready, 1)

                def guards(j, k):
                    b = j * BPT + k
                    wait_past(act, oh_used, CT * (b + 1))
                    wait_past(act, inv_ready, b)
                    lo, hi = psW[k % 2]
                    act.activation(L[:, 0:HALF], lo[:, 0:HALF], ACT.Ln, bias=tiny)
                    act.activation(L[:, HALF:NP], hi[:, 0:HALF], ACT.Ln, bias=tiny).then_inc(l_ready, 1)

                def exps(j, k):
                    b = j * BPT + k
                    wait_past(act, g_ready, b + 1)
                    act.activation(L, S[k % 2], ACT.Exp, bias=nguard).then_inc(e_ready, 1)

                def norm(j, k):
                    b = j * BPT + k
                    wait_past(act, inv_ready, b + 1)
                    act.activation(PR, PR, ACT.Copy, scale=inv).then_inc(p_ready, 1)

                def keep(j, k):
                    b = j * BPT + k
                    wait_past(act, p_turned, b + 1)
                    if k == 0:
                        wait_past(act, o_ready, j)
                    lo = psP[0][:, :].rearrange("s (t h d) -> s t h d", t=4, h=H)
                    for t in range(4):
                        act.activation(PT[:, t, :, k * BN:(k + 1) * BN], lo[:, t], ACT.Copy)
                    act.activation(PT[:, 4, :, k * BN:(k + 1) * BN], psP[1][:, 0:P].rearrange("s (h d) -> s h d", h=H),
                                   ACT.Copy).then_inc(pt_ready, 1)

                def tile(j):
                    for k in range(BPT):
                        weigh(j, k)
                        if k:
                            exps(j, k - 1)
                            norm(j, k - 1)
                            keep(j, k - 1)
                        guards(j, k)
                    exps(j, BPT - 1)
                    norm(j, BPT - 1)
                    keep(j, BPT - 1)

                tile(0)
                with act.Fori(1, NT) as j:
                    tile(j)

        @block.tensor
        def _(pe):
            longest = pe.value_load(tab[0:1, 2 * NB:2 * NB + 1], min_val=-NE, max_val=NE)
            with pe.If(longest < CHUNK + 1):
                def front(j, k):
                    b = j * BPT + k
                    wait_past(pe, xm_ready, b + 1)
                    wait_past(pe, d_done, b)
                    pe.transpose(psT, XM[:, k % 2, :], ident[:, :]).then_inc(xm_turned, 1)
                    wait_past(pe, diag_ready, b + 1)
                    pe.matmul(psM, ones[:, :], diag, start=True, stop=True).then_inc(rep_ready, 1)

                def sums(j, k):
                    b = j * BPT + k
                    lo, hi = psW[k % 2]
                    wait_past(pe, r_ready, b + 1)
                    wait_past(pe, inv_ready, b - 1)
                    for t in range(CT):
                        wait_past(pe, oh_ready, CT * b + t + 1)
                        pe.matmul(lo[:, 0:HALF], R[:, t, :], onehot[:, t, 0:HALF], start=t == 0, stop=t == CT - 1)
                        last = pe.matmul(hi[:, 0:HALF], R[:, t, :], onehot[:, t, HALF:NP], start=t == 0,
                                         stop=t == CT - 1)
                        last.then_inc(oh_used, 1)

                def turn(j, k):
                    b = j * BPT + k
                    wait_past(pe, p_ready, b + 1)
                    wait_past(pe, pt_ready, b)
                    for t in range(NT):
                        to = psP[t // 4][:, (t % 4) * P:(t % 4 + 1) * P]
                        last = pe.transpose(to, PR[:, t * P:(t + 1) * P], ident[:, :])
                    last.then_inc(p_turned, 1)

                def tile(j):
                    for k in range(BPT):
                        front(j, k)
                        sums(j, k)
                        if k:
                            turn(j, k - 1)
                    turn(j, BPT - 1)
                    wait_past(pe, pt_ready, BPT * (j + 1))
                    wait_past(pe, o_moved, j)
                    for h in range(H):
                        r = slice(DH * (h % 2), DH * (h % 2 + 1))
                        for t in range(NT):
                            last = pe.matmul(psO[r, (h // 2) * P:(h // 2 + 1) * P], vs[:, t, h * DH:(h + 1) * DH],
                                             PT[:, t, h, :], start=t == 0, stop=t == NT - 1)
                    last.then_inc(o_ready, 1)

                tile(0)
                with pe.Fori(1, NT) as j:
                    tile(j)


def feed_forward(nc, sem, x, bo, ln2_g, ln2_b, b1, b2, wts, big, xs, hT, vs, work, small, ident, psum):
    wo = wts[:, 3 * DC * D:4 * DC * D].rearrange("p (c n) -> p c n", c=DC)
    w1 = wts[:, 2 * SLOT:2 * SLOT + DC * FF].rearrange("p (c n) -> p c n", c=DC)
    w2 = wts[:, 4 * SLOT:4 * SLOT + DC * FF].rearrange("p (c n) -> p c n", n=D)
    g2, s2, bo_r, b2_r = (work[:, i * D:(i + 1) * D] for i in range(4))
    xin = work[:, 5 * D:10 * D].rearrange("p (t n) -> p t n", t=NT)
    hrow = [work[:, (10 + i) * D:(11 + i) * D] for i in range(2)]
    b1_row = work[0:FF // P, 12 * D:12 * D + P]
    b1c = vs[:, 0, 0:FF // P]
    eps = small[:, 0:1]
    std = small[:, 10:15]
    rstd = small[:, 15:20]
    mv = small[:, 20:30].rearrange("p (t c) -> p t c", c=2)
    stats = small[:, 30:60].rearrange("p (t c) -> p t c", c=6)
    MC = FF // P
    (vec_in, x_in, zeroed, own, stds, rows, turned, moved, o_ps, b1_turned, b1_ready, u_ps, u_sb, y_ps, y_sb,
     eps_set) = map(sem, (
         "ff_vec_in", "ff_x_in", "ff_zeroed", "ff_own", "ff_stds", "ff_rows", "ff_turned", "ff_moved", "o_ps",
         "b1_turned", "b1_ready", "u_ps", "u_sb", "y_ps", "y_sb", "ff_eps"))

    with nc.Block() as block:
        @block.sync
        def _(sp):
            for to, vec in ((g2, ln2_g), (s2, ln2_b), (bo_r, bo), (b2_r, b2)):
                sp.dma_start(to, vec.rearrange("(a n) -> a n", a=1).broadcast_to([P, D])).then_inc(vec_in, 16)
            sp.dma_start(b1_row, b1.rearrange("(m p) -> m p", p=P)).then_inc(vec_in, 16)
            full, rest = node_tiles(x)
            sp.wait_ge(zeroed, 1)
            sp.dma_start(xin[:, 0:NT - 1, :], full).then_inc(x_in, 16)
            sp.dma_start(xin[0:LAST, NT - 1, :], rest).then_inc(x_in, 16)

        @block.gpsimd
        def _(pool):
            pool.memset(xin[:, NT - 1, :], 0.0).then_inc(zeroed, 1)

        @block.vector
        def _(dve):
            o = Order(dve, own)
            dve.memset(eps, EPS).then_inc(eps_set, 1)
            dve.wait_ge(vec_in, 80)
            for t in range(NT):
                dve.wait_ge(o_ps, t + 1)
                o.link(dve.tensor_tensor(xs[:, t, :], xs[:, t, :], psum[t % 2][:, :], ALU.add))
                o.link(dve.tensor_tensor(xs[:, t, :], xs[:, t, :], bo_r, ALU.add))
                o.link(dve.bn_stats(stats[:, t, :], xs[:, t, :]))
                o.link(dve.bn_aggr(mv[:, t, :], stats[:, t, :]))
            dve.wait_ge(stds, 1)
            o.link(dve.reciprocal(rstd, std))
            for t in range(NT):
                r = hrow[t % 2]
                if t >= 2:
                    dve.wait_ge(turned, t - 1)
                o.link(dve.tensor_scalar(r, xs[:, t, :], mv[:, t, 0:1], rstd[:, t:t + 1], ALU.subtract, ALU.mult))
                o.link(dve.tensor_tensor(r, r, g2, ALU.mult))
                dve.tensor_tensor(r, r, s2, ALU.add).then_inc(rows, 1)
            dve.wait_ge(b1_turned, 1)
            dve.tensor_copy(b1c, psum[7][:, 0:MC]).then_inc(b1_ready, 1)
            dve.wait_ge(x_in, 32)
            for t in range(NT):
                o.link(dve.tensor_tensor(xin[:, t, :], xin[:, t, :], b2_r, ALU.add))
                o.link(dve.tensor_tensor(xs[:, t, :], xs[:, t, :], xin[:, t, :], ALU.add))
            for t in range(NT):
                dve.wait_ge(y_ps, t + 1)
                dve.tensor_tensor(xs[:, t, :], xs[:, t, :], psum[4 + t % 2][:, :], ALU.add).then_inc(y_sb, 1)

        @block.scalar
        def _(act):
            act.wait_ge(eps_set, 1)
            act.wait_ge(own, 4 * NT)
            act.activation(std, mv[:, :, 1], ACT.Sqrt, bias=eps).then_inc(stds, 1)
            for t in range(NT):
                act.wait_ge(turned, t + 1)
                act.activation(hT[:, :, t * P:(t + 1) * P], psum[2 + t % 2][:, :].rearrange("p (c n) -> p c n", c=DC),
                               ACT.Copy).then_inc(moved, 1)
            act.wait_ge(b1_ready, 1)
            for m in range(MC):
                for half in range(2):
                    i = 2 * m + half
                    act.wait_ge(u_ps, i + 1)
                    act.activation(big[:, m, half * HALF:(half + 1) * HALF], psum[i % 4][:, 0:HALF], ACT.Gelu,
                                   bias=b1c[:, m:m + 1]).then_inc(u_sb, 1)

        @block.tensor
        def _(pe):
            for t in range(NT):
                if t >= 2:
                    pe.wait_ge(own, 4 * (t - 2) + 1)
                for c in range(DC):
                    last = pe.matmul(psum[t % 2][:, :], hT[:, c, t * P:(t + 1) * P], wo[:, c, :], start=c == 0,
                                     stop=c == DC - 1)
                last.then_inc(o_ps, 1)
            pe.wait_ge(vec_in, 80)
            pe.transpose(psum[7][:, 0:MC], b1_row, ident[0:MC, 0:MC]).then_inc(b1_turned, 1)
            for t in range(NT):
                pe.wait_ge(rows, t + 1)
                if t >= 2:
                    pe.wait_ge(moved, t - 1)
                for c in range(DC):
                    last = pe.transpose(psum[2 + t % 2][:, c * P:(c + 1) * P], hrow[t % 2][:, c * P:(c + 1) * P],
                                        ident[:, :])
                last.then_inc(turned, 1)
            pe.wait_ge(moved, NT)
            for m in range(MC):
                for half in range(2):
                    i = 2 * m + half
                    if i >= 4:
                        pe.wait_ge(u_sb, i - 3)
                    for c in range(DC):
                        last = pe.matmul(psum[i % 4][:, 0:HALF], w1[:, c, m * P:(m + 1) * P],
                                         hT[:, c, half * HALF:(half + 1) * HALF], start=c == 0, stop=c == DC - 1)
                    last.then_inc(u_ps, 1)
            pe.wait_ge(u_sb, 2 * MC)
            for t in range(NT):
                if t >= 2:
                    pe.wait_ge(y_sb, t - 1)
                for m in range(MC):
                    last = pe.matmul(psum[4 + t % 2][:, :], big[:, m, t * P:(t + 1) * P], w2[:, m, :], start=m == 0,
                                     stop=m == MC - 1)
                last.then_inc(y_ps, 1)


def routing(nc, sem, w_in, gate_w, biases, w1, w3, w2, sw1, sw3, sw2, rows_d, wts, big, xs, hT, vs, work, iota_n, below,
            ones, most, small, ident, psum):
    hidden_T = big[:, 0:HC, :]
    gate_row = work[0:EX, 2 * D:3 * D]
    bias_r = work[:, 3 * D:3 * D + EX]
    gate_t = work[:, 3 * D + 8:3 * D + 8 + DC * EX].rearrange("p (c e) -> p c e", c=DC)
    names = gate_views(work)
    gates, prob, slot_i = names["gates"], names["prob"], names["slot_i"]
    sc, sbias, top, topb, pick0, pick1, cum, tot, base, picked = (
        work[:, 4 * D + 200 + 40 * i:4 * D + 240 + 40 * i].rearrange("p (t e) -> p t e", t=NT) for i in range(10))
    idx = work[:, 4 * D + 600:4 * D + 640].bitcast(U32).rearrange("p (t e) -> p t e", t=NT)
    idx_f = work[:, 4 * D + 640:4 * D + 680].rearrange("p (t e) -> p t e", t=NT)
    psums = work[:, 4 * D + 680:4 * D + 685]
    first_slot = work[:, 4 * D + 688:4 * D + 696]
    slot_f = work[:, 4 * D + 700:4 * D + 710].rearrange("p (k t) -> p k t", k=2)
    count = work[:, 4 * D + 712:4 * D + 720]
    most_f = work[:, 4 * D + 720:4 * D + 721]
    weighed = work[:, 4 * D + 740:4 * D + 780].rearrange("p (t e) -> p t e", t=NT)
    gated = [work[:, 6 * D + i * HALF:6 * D + (i + 1) * HALF] for i in range(2)]
    eps = small[:, 0:1]
    std = small[:, 10:15]
    rstd = small[:, 15:20]
    mv = small[:, 20:30].rearrange("p (t c) -> p t c", c=2)
    stats = small[:, 30:60].rearrange("p (t c) -> p t c", c=6)
    (vec_in, own, stds, rows, turned, moved, gate_turned, sc_ps, best, exp_out, a_ps, a_sb, b_sb, y_ps, y_sb, sh_in,
     picks_ready, cum_ps, slots_ready, scattered) = map(sem, (
         "ro_vec_in", "ro_own", "ro_stds", "ro_rows", "ro_turned", "ro_moved", "gate_turned", "sc_ps", "best",
         "ro_exp_out", "sh_a_ps", "sh_a_sb", "sh_b_sb", "sh_y_ps", "sh_y_sb", "sh_in", "picks_ready", "cum_ps",
         "slots_ready", "scattered"))
    sh1, sh3, sh2 = (p[0] for p in expert_parts(wts, 0, sw1, sw3, sw2))

    with nc.Block() as block:
        @block.sync
        def _(sp):
            sp.dma_start(gate_row, gate_w).then_inc(vec_in, 16)
            sp.dma_start(bias_r, biases.rearrange("(a n) -> a n", a=1).broadcast_to([P, EX])).then_inc(vec_in, 16)
            for to, frm in expert_parts(wts, 0, sw1, sw3, sw2):
                sp.dma_start(to, frm).then_inc(sh_in, 16)
            for to, frm in expert_parts(wts, 3, w1[0], w3[0], w2[0]):
                sp.dma_start(to, frm).then_inc(w_in[0], 16)

        @block.gpsimd
        def _(pool):
            pool.wait_ge(slots_ready, 1)
            fullest = pool.value_load(most[0:1, 0:1], min_val=0, max_val=NP)
            with pool.If(fullest < CAP + 1):
                for t in range(NT):
                    n = P if t < NT - 1 else LAST
                    for k in range(2):
                        pool.indirect_dma_start(
                            out=rows_d, out_offset=bass.IndirectOffsetOnAxis(ap=slot_i[0:n, k, t:t + 1], axis=0),
                            in_=vs[0:n, t, :], in_offset=None).then_inc(scattered, 16)
                pool.wait_ge(scattered, 16 * 2 * NT)

        @block.vector
        def _(dve):
            o = Order(dve, own)
            for t in range(NT):
                o.done(dve.bn_stats(stats[:, t, :], xs[:, t, :]))
            o.wait()
            for t in range(NT):
                o.done(dve.bn_aggr(mv[:, t, :], stats[:, t, :]))
            dve.wait_ge(stds, 1)
            o.link(dve.reciprocal(rstd, std))
            for t in range(NT):
                dve.tensor_scalar(vs[:, t, :], xs[:, t, :], mv[:, t, 0:1], rstd[:, t:t + 1], ALU.subtract,
                                  ALU.mult).then_inc(rows, 1)
            dve.wait_ge(gate_turned, 1)
            o.link(dve.tensor_copy(gate_t, psum[7][:, 0:DC * EX].rearrange("p (c e) -> p c e", c=DC)))
            dve.wait_ge(sc_ps, 1)
            o.link(dve.tensor_copy(sc, psum[6][:, 0:NT * EX].rearrange("p (t e) -> p t e", t=NT)))
            o.link(dve.tensor_tensor(sbias, sc, bias_r.unsqueeze(1).broadcast_to([P, NT, EX]), ALU.add))
            for t in range(NT):
                o.done(dve.max(top[:, t, :], sc[:, t, :]))
                o.done(dve.max(topb[:, t, :], sbias[:, t, :]))
            o.wait()
            for t in range(NT):
                o.done(dve.max_index(idx[:, t, :], topb[:, t, :], sbias[:, t, :]))
            o.wait()
            dve.tensor_copy(idx_f, idx).then_inc(best, 1)
            dve.wait_ge(best, 1)

            def hidden(i):
                m, half = i // 2, i % 2
                dve.wait_ge(a_sb, i + 1)
                dve.wait_ge(a_ps, i + 1)
                dve.tensor_tensor(hidden_T[:, m, half * HALF:(half + 1) * HALF], gated[i % 2],
                                  psum[2 * (i % 2) + 1][:, 0:HALF], ALU.mult).then_inc(b_sb, 1)

            hidden(0)
            hidden(1)
            for k, pick in enumerate((pick0, pick1)):
                o.done(dve.tensor_tensor(pick, iota_n[:, 0:EX].unsqueeze(1).broadcast_to([P, NT, EX]),
                                         idx_f[:, :, k:k + 1].broadcast_to([P, NT, EX]), ALU.is_equal))
            o.wait()
            dve.tensor_tensor(picked, pick0, pick1, ALU.add).then_inc(picks_ready, 1)
            dve.wait_ge(picks_ready, 1)
            hidden(2)
            dve.wait_ge(exp_out, 1)
            o.link(dve.tensor_scalar(prob, prob, 1.0, None, ALU.add))
            o.link(dve.reciprocal(prob, prob))
            o.link(dve.tensor_reduce(psums, prob, AX.X, ALU.add))
            o.link(dve.reciprocal(psums, psums))
            o.link(dve.tensor_tensor(prob, prob, psums.unsqueeze(2).broadcast_to([P, NT, 2]), ALU.mult))
            hidden(3)
            dve.wait_ge(cum_ps, 1)
            o.done(dve.memset(base[:, 0, :], 0.0))
            o.done(dve.tensor_scalar(first_slot, iota_n[:, 0:EX], float(CAP), None, ALU.mult))
            o.done(dve.tensor_copy(cum, psum[6][:, 0:NT * EX].rearrange("p (t e) -> p t e", t=NT)))
            o.link(dve.tensor_copy(tot, psum[7][:, 0:NT * EX].rearrange("p (t e) -> p t e", t=NT)))
            for t in range(1, NT):
                o.link(dve.tensor_tensor(base[:, t, :], base[:, t - 1, :], tot[:, t - 1, :], ALU.add))
            hidden(4)
            o.link(dve.tensor_tensor(count, base[:, NT - 1, :], tot[:, NT - 1, :], ALU.add))
            o.link(dve.tensor_reduce(most_f, count, AX.X, ALU.max))
            o.done(dve.tensor_copy(most[0:1, 0:1], most_f[0:1, :]))
            o.link(dve.tensor_tensor(cum, cum, base, ALU.add))
            o.link(dve.tensor_tensor(cum, cum, first_slot.unsqueeze(1).broadcast_to([P, NT, EX]), ALU.add))
            for k, pick in enumerate((pick0, pick1)):
                o.link(dve.tensor_tensor(weighed, pick, cum, ALU.mult))
                o.link(dve.tensor_reduce(slot_f[:, k, :], weighed, AX.X, ALU.add))
            dve.tensor_copy(slot_i, slot_f).then_inc(slots_ready, 1)
            hidden(5)
            o.link(dve.tensor_tensor(weighed, pick0, prob[:, :, 0:1].broadcast_to([P, NT, EX]), ALU.mult))
            o.link(dve.tensor_tensor(gates, pick1, prob[:, :, 1:2].broadcast_to([P, NT, EX]), ALU.mult))
            o.done(dve.tensor_tensor(gates, gates, weighed, ALU.add))
            for i in range(6, 2 * HC):
                hidden(i)
            for t in range(NT):
                dve.wait_ge(y_ps, t + 1)
                dve.tensor_tensor(xs[:, t, :], xs[:, t, :], psum[4 + t % 2][:, :], ALU.add).then_inc(y_sb, 1)

        @block.scalar
        def _(act):
            act.wait_ge(own, 2 * NT)
            act.activation(std, mv[:, :, 1], ACT.Sqrt, bias=eps).then_inc(stds, 1)
            for t in range(NT):
                act.wait_ge(turned, t + 1)
                act.activation(hT[:, :, t * P:(t + 1) * P], psum[2 + t % 2][:, :].rearrange("p (c n) -> p c n", c=DC),
                               ACT.Copy).then_inc(moved, 1)
            act.wait_ge(best, 1)
            act.activation(prob, top[:, :, 0:2], ACT.Exp, scale=-1.0).then_inc(exp_out, 1)
            for i in range(2 * HC):
                act.wait_ge(a_ps, i + 1)
                if i >= 2:
                    act.wait_ge(b_sb, i - 1)
                act.activation(gated[i % 2], psum[2 * (i % 2)][:, 0:HALF], ACT.Silu).then_inc(a_sb, 1)

        @block.tensor
        def _(pe):
            pe.wait_ge(vec_in, 32)
            for c in range(DC):
                last = pe.transpose(psum[7][:, c * EX:(c + 1) * EX], gate_row[:, c * P:(c + 1) * P],
                                    ident[0:EX, 0:EX])
            last.then_inc(gate_turned, 1)
            for t in range(NT):
                pe.wait_ge(rows, t + 1)
                if t >= 2:
                    pe.wait_ge(moved, t - 1)
                for c in range(DC):
                    last = pe.transpose(psum[2 + t % 2][:, c * P:(c + 1) * P], vs[:, t, c * P:(c + 1) * P],
                                        ident[:, :])
                last.then_inc(turned, 1)
            pe.wait_ge(moved, NT)
            pe.wait_ge(own, 2 * NT + 2)
            for t in range(NT):
                for c in range(DC):
                    last = pe.matmul(psum[6][:, t * EX:(t + 1) * EX], hT[:, c, t * P:(t + 1) * P], gate_t[:, c, :],
                                     start=c == 0, stop=c == DC - 1)
            last.then_inc(sc_ps, 1)
            pe.wait_ge(sh_in, 48)

            def hidden(i):
                m, half = i // 2, i % 2
                if i >= 2:
                    pe.wait_ge(b_sb, i - 1)
                for w, bank in ((sh1, 2 * (i % 2)), (sh3, 2 * (i % 2) + 1)):
                    for c in range(DC):
                        last = pe.matmul(psum[bank][:, 0:HALF], w[:, c, m * P:(m + 1) * P],
                                         hT[:, c, half * HALF:(half + 1) * HALF], start=c == 0, stop=c == DC - 1)
                last.then_inc(a_ps, 1)

            for i in range(4):
                hidden(i)
            pe.wait_ge(picks_ready, 1)
            for lhs, bank in ((below, 6), (ones, 7)):
                for t in range(NT):
                    n = P if t < NT - 1 else LAST
                    last = pe.matmul(psum[bank][:, t * EX:(t + 1) * EX], lhs[0:n, :], picked[0:n, t, :], start=True,
                                     stop=True)
            last.then_inc(cum_ps, 1)
            for i in range(4, 2 * HC):
                hidden(i)
            pe.wait_ge(b_sb, 2 * HC)
            for t in range(NT):
                if t >= 2:
                    pe.wait_ge(y_sb, t - 1)
                for m in range(HC):
                    last = pe.matmul(psum[4 + t % 2][:, :], hidden_T[:, m, t * P:(t + 1) * P], sh2[:, m, :],
                                     start=m == 0, stop=m == HC - 1)
                last.then_inc(y_ps, 1)


def gate_views(work):
    return dict(gates=work[:, 4 * D:4 * D + NT * EX].rearrange("p (t e) -> p t e", t=NT),
                prob=work[:, 4 * D + 40:4 * D + 50].rearrange("p (t k) -> p t k", t=NT),
                slot_i=work[:, 4 * D + 60:4 * D + 70].bitcast(I32).rearrange("p (k t) -> p k t", k=2))


def expert_parts(wts, s, a, b, c):
    slots = [wts[:, i * SLOT:(i + 1) * SLOT] for i in range(s, s + 3)]
    return ((slots[0].rearrange("p (c n) -> p c n", c=DC), a.rearrange("(c p) n -> p c n", p=P)),
            (slots[1].rearrange("p (c n) -> p c n", c=DC), b.rearrange("(c p) n -> p c n", p=P)),
            (slots[2].rearrange("p (c n) -> p c n", n=D), c.rearrange("(c p) n -> p c n", p=P)))


def one_expert(w, e):
    return w[bass.ds(e, 1), :, :].rearrange("a k n -> (a k) n")


def experts_routed(nc, sem, w_in, w1, w3, w2, rows_d, y_d, out, wts, big, xs, hT, vs, work, most, ident, psum):
    names = gate_views(work)
    prob, slot_i = names["prob"], names["slot_i"]
    flat = big.rearrange("p a n -> p (a n)")
    hidden_T = [flat[:, k * HC * CAP:(k + 1) * HC * CAP].rearrange("p (m n) -> p m n", m=HC) for k in range(2)]
    at = 2 * HC * CAP
    y_st = [flat[:, at + k * D:at + (k + 1) * D] for k in range(CB)]
    at += CB * D
    got = flat[:, at:at + 2 * NT * D].rearrange("p (k t n) -> p k t n", k=2, t=NT)
    xrow = [vs[:, 2 * k:2 * k + CB, :] for k in range(2)]
    xT = [hT.rearrange("p c n -> p (c n)")[:, k * DC * CAP:(k + 1) * DC * CAP].rearrange("p (c n) -> p c n", c=DC)
          for k in range(2)]
    gated = [work[:, 6 * D + i * CAP:6 * D + (i + 1) * CAP] for i in range(2)]
    (x_turned, x_moved, a_ps, a_sb, b_sb, y_ps, y_sb, sums, stored) = map(sem, (
        "xe_turned", "xe_moved", "re_a_ps", "re_a_sb", "re_b_sb", "re_y_ps", "re_y_sb", "re_sums", "re_stored"))
    x_in = [sem(f"xe_in{i}") for i in range(2)]
    y_out = [sem(f"y_out{i}") for i in range(CB)]
    got_in = [sem(f"got_in{i}") for i in range(NT)]
    PAIRS = EX // 2

    with nc.Block() as block:
        @block.sync
        def _(sp):
            fullest = sp.value_load(most[0:1, 0:1], min_val=0, max_val=NP)
            with sp.If(fullest < CAP + 1):
                def rows_of(d, first, n):
                    return d[bass.ds(first, n), :]

                for k in range(2):
                    sp.dma_start(xrow[k], rows_d[k * CAP:(k + 1) * CAP, :].rearrange("(b p) n -> p b n", p=P))\
                      .then_inc(x_in[k], 16)
                for to, frm in expert_parts(wts, 0, w1[1], w3[1], w2[1]):
                    sp.dma_start(to, frm).then_inc(w_in[1], 16)

                def store(first, e, blk):
                    sp.wait_ge(y_sb, CB * e + (blk + 1))
                    sp.dma_start(rows_of(y_d, first, P), y_st[blk]).then_inc(y_out[blk], 16)

                with sp.Fori(0, PAIRS - 1) as j:
                    for k in range(2):
                        e = j * 2 + k
                        at_x = sp.snap((e + 2) * CAP)
                        at_y = [sp.snap(e * CAP + blk * P) for blk in range(CB)]
                        next_e = sp.snap(e + 2)
                        used = sp.snap(e * CB + CB)
                        sp.wait_ge(x_turned, e + 1)
                        sp.dma_start(xrow[k], rows_of(rows_d, at_x, CAP).rearrange("(b p) n -> p b n", p=P))\
                          .then_inc(x_in[k], 16)
                        sp.wait_ge(y_ps, used)
                        for to, frm in expert_parts(wts, 3 - 3 * k, one_expert(w1, next_e), one_expert(w3, next_e),
                                                    one_expert(w2, next_e)):
                            sp.dma_start(to, frm).then_inc(w_in[k], 16)
                        for blk in range(CB):
                            store(at_y[blk], e, blk)
                for e in (EX - 2, EX - 1):
                    for blk in range(CB):
                        store(e * CAP + blk * P, e, blk)
                for t in range(NT):
                    n = P if t < NT - 1 else LAST
                    sp.wait_ge(sums, 2 * t + 2)
                    sp.dma_start(out[t * P:t * P + n, :], xs[0:n, t, :]).then_inc(stored, 16)
                sp.wait_ge(stored, 16 * NT)

        @block.gpsimd
        def _(pool):
            fullest = pool.value_load(most[0:1, 0:1], min_val=0, max_val=NP)
            with pool.If(fullest < CAP + 1):
                for blk in range(CB):
                    pool.wait_ge(y_out[blk], 16 * EX)
                for t in range(NT):
                    n = P if t < NT - 1 else LAST
                    for k in range(2):
                        pool.indirect_dma_start(
                            out=got[0:n, k, t, :], out_offset=None, in_=y_d,
                            in_offset=bass.IndirectOffsetOnAxis(ap=slot_i[0:n, k, t:t + 1], axis=0))\
                            .then_inc(got_in[t], 16)

        @block.vector
        def _(dve):
            fullest = dve.value_load(most[0:1, 0:1], min_val=0, max_val=NP)
            with dve.If(fullest < CAP + 1):
                def expert(e, k):
                    for m in range(HC):
                        wait_past(dve, a_sb, e * HC + (m + 1))
                        wait_past(dve, a_ps, e * HC + (m + 1))
                        dve.tensor_tensor(hidden_T[k][:, m, :], gated[m % 2], psum[2 * (m % 2) + 1][:, 0:CAP],
                                          ALU.mult).then_inc(b_sb, 1)
                    for blk in range(CB):
                        wait_past(dve, y_ps, e * CB + (blk + 1))
                        wait_past(dve, y_out[blk], e * 16)
                        dve.tensor_copy(y_st[blk], psum[4 + blk][:, :]).then_inc(y_sb, 1)

                def pair(j):
                    for k in range(2):
                        expert(j * 2 + k, k)

                pair(0)
                with dve.Fori(1, PAIRS) as j:
                    pair(j)
                for t in range(NT):
                    n = P if t < NT - 1 else LAST
                    dve.wait_ge(got_in[t], 32)
                    for k in range(2):
                        if k:
                            dve.wait_ge(sums, 2 * t + 1)
                        dve.scalar_tensor_tensor(out=xs[0:n, t, :], in0=got[0:n, k, t, :],
                                                 scalar=prob[0:n, t, k:k + 1], in1=xs[0:n, t, :], op0=ALU.mult,
                                                 op1=ALU.add).then_inc(sums, 1)

        @block.scalar
        def _(act):
            fullest = act.value_load(most[0:1, 0:1], min_val=0, max_val=NP)
            with act.If(fullest < CAP + 1):
                def move(e, k):
                    wait_past(act, x_turned, e + 1)
                    for blk in range(CB):
                        last = act.activation(xT[k][:, :, blk * P:(blk + 1) * P],
                                              psum[6 + blk][:, :].rearrange("p (c n) -> p c n", c=DC), ACT.Copy)
                    last.then_inc(x_moved, 1)

                def expert(e, k, more):
                    for m in range(HC):
                        wait_past(act, a_ps, e * HC + (m + 1))
                        wait_past(act, b_sb, e * HC + (m - 1))
                        act.activation(gated[m % 2], psum[2 * (m % 2)][:, 0:CAP], ACT.Silu).then_inc(a_sb, 1)
                    if more:
                        move(e + 1, 1 - k)

                move(0, 0)
                expert(0, 0, True)
                expert(1, 1, True)
                with act.Fori(1, PAIRS - 1) as j:
                    for k in range(2):
                        expert(j * 2 + k, k, True)
                expert(EX - 2, 0, True)
                expert(EX - 1, 1, False)

        @block.tensor
        def _(pe):
            fullest = pe.value_load(most[0:1, 0:1], min_val=0, max_val=NP)
            with pe.If(fullest < CAP + 1):
                def turn(e, k, j):
                    wait_past(pe, x_in[k], j * 16 + 16)
                    wait_past(pe, x_moved, e)
                    for blk in range(CB):
                        for c in range(DC):
                            last = pe.transpose(psum[6 + blk][:, c * P:(c + 1) * P],
                                                xrow[k][:, blk, c * P:(c + 1) * P], ident[:, :])
                    last.then_inc(x_turned, 1)

                def expert(e, k, j, more):
                    w1s, w3s, w2s = (p[0] for p in expert_parts(wts, 3 - 3 * k, w1[0], w3[0], w2[0]))
                    wait_past(pe, w_in[k], j * 48 + 48)
                    wait_past(pe, x_moved, e + 1)
                    for m in range(HC):
                        wait_past(pe, b_sb, e * HC + (m - 1))
                        for w, bank in ((w1s, 2 * (m % 2)), (w3s, 2 * (m % 2) + 1)):
                            for c in range(DC):
                                last = pe.matmul(psum[bank][:, 0:CAP], w[:, c, m * P:(m + 1) * P], xT[k][:, c, :],
                                                 start=c == 0, stop=c == DC - 1)
                        last.then_inc(a_ps, 1)
                    if more:
                        turn(e + 1, 1 - k, j + k)
                    wait_past(pe, b_sb, e * HC + HC)
                    for blk in range(CB):
                        wait_past(pe, y_sb, e * CB + (blk + 1 - CB))
                        for m in range(HC):
                            last = pe.matmul(psum[4 + blk][:, :], hidden_T[k][:, m, blk * P:(blk + 1) * P],
                                             w2s[:, m, :], start=m == 0, stop=m == HC - 1)
                        last.then_inc(y_ps, 1)

                turn(0, 0, 0)
                expert(0, 0, 0, True)
                expert(1, 1, 0, True)
                with pe.Fori(1, PAIRS - 1) as j:
                    for k in range(2):
                        expert(j * 2 + k, k, j, True)
                expert(EX - 2, 0, PAIRS - 1, True)
                expert(EX - 1, 1, PAIRS - 1, False)


def experts_all(nc, sem, w_in, w1, w3, w2, out, wts, big, xs, hT, work, most, psum):
    gates = gate_views(work)["gates"]
    gated = [work[:, 6 * D + i * HALF:6 * D + (i + 1) * HALF] for i in range(2)]
    (a_ps, a_sb, b_sb, y_ps, y_sb, stored) = map(sem, (
        "all_a_ps", "all_a_sb", "all_b_sb", "all_y_ps", "all_y_sb", "all_stored"))

    with nc.Block() as block:
        @block.sync
        def _(sp):
            fullest = sp.value_load(most[0:1, 0:1], min_val=0, max_val=NP)
            with sp.If(fullest > CAP):
                for to, frm in expert_parts(wts, 0, w1[1], w3[1], w2[1]):
                    sp.dma_start(to, frm).then_inc(w_in[1], 16)
                with sp.Fori(0, EX // 2 - 1) as j:
                    for k in range(2):
                        e = j * 2 + k
                        next_e = sp.snap(e + 2)
                        used = sp.snap(e * NT + NT)
                        sp.wait_ge(y_ps, used)
                        for to, frm in expert_parts(wts, 3 - 3 * k, one_expert(w1, next_e), one_expert(w3, next_e),
                                                    one_expert(w2, next_e)):
                            sp.dma_start(to, frm).then_inc(w_in[k], 16)
                full, rest = node_tiles(out)
                sp.wait_ge(y_sb, NT * EX)
                sp.dma_start(full, xs[:, 0:NT - 1, :]).then_inc(stored, 16)
                sp.dma_start(rest, xs[0:LAST, NT - 1, :]).then_inc(stored, 16)
                sp.wait_ge(stored, 32)

        @block.vector
        def _(dve):
            fullest = dve.value_load(most[0:1, 0:1], min_val=0, max_val=NP)
            with dve.If(fullest > CAP):
                def expert(e, k):
                    for m in range(HC):
                        for half in range(2):
                            i = 2 * m + half
                            wait_past(dve, a_sb, e * (2 * HC) + (i + 1))
                            wait_past(dve, a_ps, e * (2 * HC) + (i + 1))
                            dve.tensor_tensor(big[:, HC * k + m, half * HALF:(half + 1) * HALF], gated[i % 2],
                                              psum[2 * (i % 2) + 1][:, 0:HALF], ALU.mult).then_inc(b_sb, 1)
                    for t in range(NT):
                        wait_past(dve, y_ps, e * NT + (t + 1))
                        wait_past(dve, y_sb, e * NT + (t + 1 - NT))
                        dve.scalar_tensor_tensor(out=xs[:, t, :], in0=psum[4 + t % 2][:, :],
                                                 scalar=gates[:, t, bass.ds(e, 1)], in1=xs[:, t, :],
                                                 op0=ALU.mult, op1=ALU.add).then_inc(y_sb, 1)

                for k in range(2):
                    expert(k, k)
                with dve.Fori(1, EX // 2) as j:
                    for k in range(2):
                        expert(j * 2 + k, k)

        @block.scalar
        def _(act):
            fullest = act.value_load(most[0:1, 0:1], min_val=0, max_val=NP)
            with act.If(fullest > CAP):
                def expert(e):
                    for i in range(2 * HC):
                        wait_past(act, a_ps, e * (2 * HC) + (i + 1))
                        wait_past(act, b_sb, e * (2 * HC) + (i - 1))
                        act.activation(gated[i % 2], psum[2 * (i % 2)][:, 0:HALF], ACT.Silu).then_inc(a_sb, 1)

                for k in range(2):
                    expert(k)
                with act.Fori(1, EX // 2) as j:
                    for k in range(2):
                        expert(j * 2 + k)

        @block.tensor
        def _(pe):
            fullest = pe.value_load(most[0:1, 0:1], min_val=0, max_val=NP)
            with pe.If(fullest > CAP):
                def expert(e, k, j):
                    a, b, c3 = (p[0] for p in expert_parts(wts, 3 - 3 * k, w1[0], w3[0], w2[0]))
                    wait_past(pe, w_in[k], j * 48 + 48)
                    for m in range(HC):
                        for half in range(2):
                            i = 2 * m + half
                            wait_past(pe, b_sb, e * (2 * HC) + (i - 1))
                            for w, bank in ((a, 2 * (i % 2)), (b, 2 * (i % 2) + 1)):
                                for c in range(DC):
                                    last = pe.matmul(psum[bank][:, 0:HALF], w[:, c, m * P:(m + 1) * P],
                                                     hT[:, c, half * HALF:(half + 1) * HALF], start=c == 0,
                                                     stop=c == DC - 1)
                            last.then_inc(a_ps, 1)
                    wait_past(pe, b_sb, e * (2 * HC) + 2 * HC)
                    for t in range(NT):
                        wait_past(pe, y_sb, e * NT + (t - 1))
                        for m in range(HC):
                            last = pe.matmul(psum[4 + t % 2][:, :], big[:, HC * k + m, t * P:(t + 1) * P],
                                             c3[:, m, :], start=m == 0, stop=m == HC - 1)
                        last.then_inc(y_ps, 1)

                for k in range(2):
                    expert(k, k, 0)
                with pe.Fori(1, EX // 2) as j:
                    for k in range(2):
                        expert(j * 2 + k, k, j)


def attention_any(nc, sem, rec_d, logits_d, big, hT, vs, work, iota_n, ident, ones, XM, tab, small, psum):
    NCH = -(-NE // CHUNK)
    X = work[:, 0:CT * P].rearrange("p (t m) -> p t m", t=CT)
    R = work[:, 2 * NP:3 * NP].rearrange("p (t m) -> p t m", t=CT)
    onehot = work[:, 3 * NP:8 * NP].rearrange("p (t s) -> p t s", t=CT)
    S = work[:, 8 * NP:9 * NP]
    L = work[:, 10 * NP:11 * NP]
    PR = work[:, 11 * NP:12 * NP]
    PT = big[:, 8:16, :].rearrange("p a n -> p (a n)").rearrange("p (t h d) -> p t h d", t=NT, h=H)
    rec = big[:, 0, 0:CT * REC].rearrange("p (t c) -> p t c", t=CT)
    miss = big[:, 2, 0:CT * BN].rearrange("p (t d) -> p t d", t=CT)
    minus_big = big[:, 4, 0:1]
    diag = big[:, 4, P:2 * P]
    zeros = big[:, 4, 2 * P:3 * P]
    tiny = small[:, 0:1]
    guard, nguard, total, inv, worst = (small[:, k:k + 1] for k in range(1, 6))
    psT, psM = psum[0][:, 0:P], psum[0][:, P:2 * P]
    lo, hi = psum[1], psum[2]
    psP = (psum[5], psum[6])
    psO = psum[7]
    names = ("consts poolown rec_in x_made chunk_used xm_ready xm_turned own worst_ready diag_ready rep_ready "
             "d_done oh_ready r_ready w_ready s_in l_ready g_ready e_ready p_made inv_ready p_ready p_turned pt_ready "
             "o_ready o_moved w_closed").split()
    (consts, poolown, rec_in, x_made, chunk_used, xm_ready, xm_turned, own, worst_ready, diag_ready,
     rep_ready, d_done, oh_ready, r_ready, w_ready, s_in, l_ready, g_ready, e_ready, p_made, inv_ready, p_ready,
     p_turned, pt_ready, o_ready, o_moved, w_closed) = (sem("any_" + n) for n in names)

    with nc.Block() as block:
        @block.sync
        def _(sp):
            longest = sp.value_load(tab[0:1, 2 * NB:2 * NB + 1], min_val=-NE, max_val=NE)
            with sp.If(longest > CHUNK):
                with sp.Fori(0, NB) as b:
                    row = sp.snap(b * (P * NP))
                    blocks_done = sp.snap(b + 1)
                    sp.wait_ge(e_ready, blocks_done)
                    sp.dma_start(S, logits_d.rearrange("b h l s -> (b h l s)")[bass.ds(row, P * NP)]
                                 .rearrange("(p n) -> p n", p=P)).then_inc(s_in, 16)
                    for sweep in range(2):
                        with sp.Fori(0, NCH) as c:
                            at = sp.snap(c * (CHUNK * REC))
                            used = sp.snap(b * (2 * NCH) + (c + (sweep * NCH + 1)))
                            sp.wait_ge(chunk_used, used)
                            sp.dma_start(rec.rearrange("p t c -> p (t c)"),
                                         rec_d.rearrange("e c -> (e c)")[bass.ds(at, CHUNK * REC)]
                                         .rearrange("(p n) -> p n", p=P)).then_inc(rec_in, 16)

        @block.gpsimd
        def _(pool):
            longest = pool.value_load(tab[0:1, 2 * NB:2 * NB + 1], min_val=-NE, max_val=NE)
            with pool.If(longest > CHUNK):
                pool.memset(minus_big, -BIG).then_inc(consts, 1)
                pool.memset(zeros, 0.0).then_inc(consts, 1)
                pool.memset(tiny, TINY).then_inc(consts, 1)
                pool.wait_ge(consts, 3)
                with pool.Fori(0, NB) as b:
                    for sweep in range(2):
                        with pool.Fori(0, NCH) as c:
                            v = b * (2 * NCH) + (c + sweep * NCH)
                            pool.wait_ge(rec_in, v * 16 + 16)
                            pool.tensor_tensor(miss, rec[:, :, 1:2].broadcast_to([P, CT, BN]),
                                               iota_n[:, bass.ds(b * BN, BN)].unsqueeze(1).broadcast_to([P, CT, BN]),
                                               ALU.subtract).then_inc(poolown, 1)
                            pool.wait_ge(poolown, v * 3 + 1)
                            pool.tensor_tensor(miss, miss, miss, ALU.mult).then_inc(poolown, 1)
                            pool.wait_ge(poolown, v * 3 + 2)
                            pool.tensor_tensor(miss, miss, minus_big.unsqueeze(1).broadcast_to([P, CT, BN]),
                                               ALU.mult).then_inc(poolown, 1)
                            pool.wait_ge(poolown, v * 3 + 3)
                            pool.tensor_tensor(X.rearrange("p t (h d) -> p t h d", h=H),
                                               rec[:, :, 2:REC].unsqueeze(3).broadcast_to([P, CT, H, BN]),
                                               miss.unsqueeze(2).broadcast_to([P, CT, H, BN]), ALU.add)\
                                .then_inc(x_made, 1)

        @block.vector
        def _(dve):
            longest = dve.value_load(tab[0:1, 2 * NB:2 * NB + 1], min_val=-NE, max_val=NE)
            with dve.If(longest > CHUNK):
                for s in (chunk_used, inv_ready):
                    dve.sem_inc(s, 1)
                dve.wait_ge(consts, 3)
                with dve.Fori(0, NB) as b:
                    dve.wait_ge(xm_turned, b + 1)
                    dve.memset(XM[:, 0, :], -BIG).then_inc(own, 1)
                    with dve.Fori(0, NCH) as c:
                        v = b * (2 * NCH) + c
                        u = b * (2 * NCH + 4) + c * 2
                        dve.wait_ge(x_made, v + 1)
                        dve.wait_ge(own, u + 1)
                        dve.tensor_reduce(XM[:, 1, :], X.rearrange("p t m -> p m t"), AX.X, ALU.max).then_inc(own, 1)
                        dve.wait_ge(own, u + 2)
                        dve.tensor_tensor(XM[:, 0, :], XM[:, 0, :], XM[:, 1, :], ALU.max).then_inc(own, 1)
                        dve.wait_ge(own, u + 3)
                        dve.sem_inc(chunk_used, 1)
                    dve.sem_inc(xm_ready, 1)
                    dve.wait_ge(xm_turned, b + 2)
                    dve.tensor_reduce(worst, psT, AX.X, ALU.max).then_inc(worst_ready, 1)
                    dve.wait_ge(worst_ready, b + 1)
                    dve.tensor_scalar(diag, ident[:, :], worst, -BIG / 10, ALU.mult, ALU.max).then_inc(diag_ready, 1)
                    with dve.Fori(0, NCH) as c:
                        v = b * (2 * NCH) + (c + NCH)
                        dve.wait_ge(rep_ready, b + 1)
                        dve.wait_ge(x_made, v + 1)
                        dve.tensor_tensor(X, X, psM.unsqueeze(1).broadcast_to([P, CT, P]), ALU.subtract)\
                           .then_inc(d_done, 1)
                        dve.wait_ge(w_ready, b * NCH + (c + 1))
                        for t in range(CT):
                            dve.tensor_scalar(onehot[:, t, :], iota_n[:, :], rec[:, t, 0:1], None, ALU.is_equal)\
                               .then_inc(oh_ready, 1)
                        dve.wait_ge(w_ready, b * NCH + (c + 2))
                        dve.sem_inc(chunk_used, 1)
                    dve.wait_ge(l_ready, b + 1)
                    dve.wait_ge(s_in, b * 16 + 16)
                    dve.tensor_tensor(L, L, S, ALU.add).then_inc(own, 1)
                    dve.wait_ge(own, b * (2 * NCH + 4) + (2 * NCH + 2))
                    dve.tensor_reduce(nguard, L, AX.X, ALU.max, negate=True).then_inc(g_ready, 1)
                    dve.wait_ge(e_ready, b + 2)
                    dve.wait_ge(p_turned, b + 1)
                    dve.tensor_tensor_reduce(PR[:, 0:HALF], lo[:, 0:HALF], L[:, 0:HALF], 1.0, 0.0, ALU.mult, ALU.add,
                                             total).then_inc(own, 1)
                    dve.wait_ge(own, b * (2 * NCH + 4) + (2 * NCH + 3))
                    dve.tensor_tensor_reduce(PR[:, HALF:NP], hi[:, 0:HALF], L[:, HALF:NP], 1.0, total, ALU.mult,
                                             ALU.add, guard).then_inc(own, 1)
                    dve.wait_ge(own, b * (2 * NCH + 4) + (2 * NCH + 4))
                    dve.tensor_scalar(total, guard, 1e-37, None, ALU.max).then_inc(p_made, 1)
                    dve.wait_ge(p_made, b + 1)
                    dve.reciprocal(inv, total).then_inc(inv_ready, 1)

        @block.scalar
        def _(act):
            longest = act.value_load(tab[0:1, 2 * NB:2 * NB + 1], min_val=-NE, max_val=NE)
            with act.If(longest > CHUNK):
                for s in (e_ready, pt_ready, o_moved):
                    act.sem_inc(s, 1)
                act.preload_act_table_set("natural_log_exp_and_others")
                act.wait_ge(consts, 3)
                with act.Fori(0, NT) as j:
                    with act.Fori(0, BPT) as k:
                        b = j * BPT + k
                        with act.Fori(0, NCH) as c:
                            act.wait_ge(d_done, b * NCH + (c + 1))
                            act.wait_ge(w_ready, b * NCH + (c + 1))
                            act.activation(R, X, ACT.Exp).then_inc(r_ready, 1)
                        act.wait_ge(w_closed, b + 1)
                        act.wait_ge(inv_ready, b + 1)
                        act.activation(L[:, 0:HALF], lo[:, 0:HALF], ACT.Ln, bias=tiny)
                        act.activation(L[:, HALF:NP], hi[:, 0:HALF], ACT.Ln, bias=tiny).then_inc(l_ready, 1)
                        act.wait_ge(g_ready, b + 1)
                        act.activation(L, S, ACT.Exp, bias=nguard).then_inc(e_ready, 1)
                        act.wait_ge(inv_ready, b + 2)
                        act.activation(PR, PR, ACT.Copy, scale=inv).then_inc(p_ready, 1)
                        act.wait_ge(p_turned, b + 2)
                        act.wait_ge(o_ready, j + 1)
                        first = psP[0][:, :].rearrange("s (t h d) -> s t h d", t=4, h=H)
                        for t in range(4):
                            act.activation(PT[:, t, :, bass.ds(k * BN, BN)], first[:, t], ACT.Copy)
                        act.activation(PT[:, 4, :, bass.ds(k * BN, BN)],
                                       psP[1][:, 0:P].rearrange("s (h d) -> s h d", h=H), ACT.Copy)\
                           .then_inc(pt_ready, 1)
                    act.wait_ge(o_ready, j + 2)
                    act.activation(hT[:, :, bass.ds(j * P, P)], psO[:, :].rearrange("p (c d) -> p c d", c=DC),
                                   ACT.Copy).then_inc(o_moved, 1)

        @block.tensor
        def _(pe):
            longest = pe.value_load(tab[0:1, 2 * NB:2 * NB + 1], min_val=-NE, max_val=NE)
            with pe.If(longest > CHUNK):
                for s in (w_ready, xm_turned, p_turned, o_ready):
                    pe.sem_inc(s, 1)
                pe.wait_ge(consts, 3)
                with pe.Fori(0, NT) as j:
                    with pe.Fori(0, BPT) as k:
                        b = j * BPT + k
                        pe.wait_ge(xm_ready, b + 1)
                        pe.transpose(psT, XM[:, 0, :], ident[:, :]).then_inc(xm_turned, 1)
                        pe.wait_ge(diag_ready, b + 1)
                        pe.matmul(psM, ones[:, :], diag, start=True, stop=True).then_inc(rep_ready, 1)
                        pe.wait_ge(inv_ready, b + 1)
                        pe.matmul(lo[:, 0:HALF], zeros, iota_n[:, 0:HALF], start=True, stop=False)
                        pe.matmul(hi[:, 0:HALF], zeros, iota_n[:, 0:HALF], start=True, stop=False)
                        with pe.Fori(0, NCH) as c:
                            v = b * NCH + c
                            pe.wait_ge(r_ready, v + 1)
                            pe.wait_ge(oh_ready, v * CT + CT)
                            for t in range(CT):
                                pe.matmul(lo[:, 0:HALF], R[:, t, :], onehot[:, t, 0:HALF], start=False, stop=False)
                                last = pe.matmul(hi[:, 0:HALF], R[:, t, :], onehot[:, t, HALF:NP], start=False,
                                                 stop=False)
                            last.then_inc(w_ready, 1)
                        pe.matmul(lo[:, 0:HALF], zeros, iota_n[:, 0:HALF], start=False, stop=True)
                        pe.matmul(hi[:, 0:HALF], zeros, iota_n[:, 0:HALF], start=False, stop=True)\
                          .then_inc(w_closed, 1)
                        pe.wait_ge(p_ready, b + 1)
                        pe.wait_ge(pt_ready, b + 1)
                        for t in range(NT):
                            to = psP[t // 4][:, (t % 4) * P:(t % 4 + 1) * P]
                            last = pe.transpose(to, PR[:, t * P:(t + 1) * P], ident[:, :])
                        last.then_inc(p_turned, 1)
                    pe.wait_ge(pt_ready, j * BPT + (BPT + 1))
                    pe.wait_ge(o_moved, j + 1)
                    for h in range(H):
                        r = slice(DH * (h % 2), DH * (h % 2 + 1))
                        for t in range(NT):
                            last = pe.matmul(psO[r, (h // 2) * P:(h // 2 + 1) * P], vs[:, t, h * DH:(h + 1) * DH],
                                             PT[:, t, h, :], start=t == 0, stop=t == NT - 1)
                    last.then_inc(o_ready, 1)


_INS = ['x', 'src', 'dst', 'edge_attr_8', 'edge_attr_8_n2', 'L0_gnn_Wqkv', 'L0_gnn_bqkv', 'L0_gnn_Wo', 'L0_gnn_bo',
        'L0_gnn_ln1_g', 'L0_gnn_ln1_b', 'L0_gnn_W1', 'L0_gnn_b1', 'L0_gnn_W2', 'L0_gnn_b2', 'L0_gnn_ln2_g',
        'L0_gnn_ln2_b', 'L0_ffn_gate_w', 'L0_ffn_biases', 'L0_ffn_w1', 'L0_ffn_w3', 'L0_ffn_w2', 'L0_ffn_sw1',
        'L0_ffn_sw3', 'L0_ffn_sw2']


def kernel(**inputs):
    import numpy as _np
    import concourse.bacc as _bacc
    from concourse import mybir as _mybir
    from concourse.bass_utils import run_bass_kernel_spmd as _run

    nc = _bacc.Bacc("TRN2", target_bir_lowering=False, num_devices=1)
    arrays, args = {}, []
    for name in _INS:
        a = _np.ascontiguousarray(inputs[name])
        arrays[f"in_{name}"] = a
        args.append(nc.dram_tensor(f"in_{name}", a.shape, _mybir.dt.from_np(a.dtype), kind="ExternalInput").ap())
    out = nc.dram_tensor("out", (N, D), F32, kind="ExternalOutput").ap()
    program(nc, *args, out)
    r = _run(nc, [arrays], core_ids=[0])
    return r.results[0]["out"]
```

```python
from contextlib import ExitStack

import concourse.bass as bass
from concourse import mybir

P = 128
F32 = mybir.dt.float32
I32 = mybir.dt.int32
U32 = mybir.dt.uint32
F32R = mybir.dt.float32r
ALU = mybir.AluOpType
ACT = mybir.ActivationFunctionType
AX = mybir.AxisListType

N = 625
D = 512
DC = D // P
H = 8
DH = D // H
NE = 20000
FF = 4 * D
HID = 1024
HC = HID // P
EX = 8
NT = -(-N // P)
NP = NT * P
HALF = NP // 2
LAST = N - (NT - 1) * P
EPS = 1e-5
BN = P // H
NB = NP // BN
BPT = P // BN
CT = 5
CHUNK = CT * P
EP, EJ = 125, NE // 125
REC = 2 + H
BIG = 1e30
TINY = 2.0 ** -64
STAGES = 6
UW = 256
UM = UW // P
UNITS = HID // UW
SLOT = 4096
CB = 2
CAP = CB * P


def node_tiles(ap):
    full = ap[0:(NT - 1) * P, :].rearrange("(t p) n -> p t n", p=P)
    return full, ap[(NT - 1) * P:N, :]


def wait_past(eng, sem, value):
    if not isinstance(value, int) or value > 0:
        eng.wait_ge(sem, value)


def program(nc, x, src, dst, edge_attr_8, edge_attr_8_n2, Wqkv, bqkv, Wo, bo, ln1_g, ln1_b, W1, b1, W2, b2,
            ln2_g, ln2_b, gate_w, biases, w1, w3, w2, sw1, sw3, sw2, out):
    with ExitStack() as ctx:
        def sb(name, shape, dt=F32):
            return ctx.enter_context(nc.sbuf_tensor(name, shape, dt))

        semaphores = {}

        def sem(name):
            if name not in semaphores:
                semaphores[name] = ctx.enter_context(nc.semaphore(name))
            return semaphores[name]

        w_hi = sb("weights_hi", [P, 4 * SLOT])
        xs = sb("xs", [P, NT, D])
        hT = sb("hT", [P, DC, NP])
        vs = sb("vs", [P, NT, D])
        iota_n = sb("iota_n", [P, NP])
        ident = sb("ident", [P, P])
        ones = sb("ones", [P, P])
        below = sb("below", [P, P])
        small = sb("small", [P, 64])
        gate_sb = sb("gate", [P, 80])
        tab_f = sb("tab_f", [1, 3 * NB + 1])
        tab = sb("tab", [1, 2 * NB + 1], I32)
        most = sb("most", [1, 1], I32)
        psum = [ctx.enter_context(nc.psum_tensor(f"ps{i}", [P, 512], F32)) for i in range(8)]
        logits_d = nc.dram_tensor("logits_scratch", [NB, H, BN, NP], F32, kind="Internal").ap()
        rec_d = nc.dram_tensor("record_scratch", [NE + CHUNK, REC], F32, kind="Internal").ap()
        rows_d = nc.dram_tensor("slot_rows", [EX * CAP, D], F32, kind="Internal").ap()
        y_d = nc.dram_tensor("slot_results", [EX * CAP, D], F32, kind="Internal").ap()
        w_in = [sem(f"w_in{i}") for i in range(2)]

        def memory(stage, name, shape):
            return stage.enter_context(nc.sbuf_tensor(name, shape, F32))

        def two_slots(stage, name, n=2 * SLOT):
            return (memory(stage, f"weights_lo_{name}", [P, n]), memory(stage, f"work_{name}", [P, 12 * NP]))

        def all_slots(w_lo):
            return [w[:, i * SLOT:(i + 1) * SLOT] for w, n in ((w_lo, 2), (w_hi, 4)) for i in range(n)]

        with ExitStack() as graph_layer:
            wo = memory(graph_layer, "wo", [P, DC, D])
            with ExitStack() as attention_part:
                big = memory(attention_part, "big", [P, 16, NP])
                with ExitStack() as stage:
                    w_lo, work = two_slots(stage, "before", DC * 3 * D + 4 * EJ + D)
                    projections(nc, sem, src, dst, edge_attr_8, edge_attr_8_n2, x, Wqkv, bqkv, Wo, W1, W2, ln1_g, ln1_b,
                                rec_d, rows_d, logits_d, wo, w_lo, w_hi, big, xs, hT, vs, work, small, tab_f, tab,
                                iota_n, ident, ones, below, psum)
                attention(nc, sem, rec_d, logits_d, big, hT, vs, iota_n, ident, ones, tab, small, psum)
                attention_any(nc, sem, rec_d, logits_d, big, hT, vs, iota_n, ident, ones, tab, small, psum)
            work = memory(graph_layer, "work_ff", [P, 12 * NP])
            feed_forward(nc, sem, x, bo, ln2_g, ln2_b, b1, b2, wo, w_hi, xs, hT, vs, work, small, ident, psum)
        with ExitStack() as stage:
            w_lo, work = memory(stage, "weights_lo_shared", [P, 2 * SLOT]), memory(stage, "gate_work", [P, 1300])
            routing(nc, sem, w_in, gate_w, biases, w1, w3, w2, sw1, sw3, sw2, rows_d, all_slots(w_lo), xs, hT,
                    vs, work, gate_sb, iota_n, below, ones, most, small, ident, psum)
        experts_routed(nc, sem, w_in, w1, w3, w2, rows_d, y_d, out, all_slots(w_hi), xs, hT, vs, gate_sb, most, ident,
                       psum)
        with ExitStack() as stage:
            big = memory(stage, "big_all", [P, 16, NP])
            w_lo, work = two_slots(stage, "all")
            experts_all(nc, sem, w_in, w1, w3, w2, out, all_slots(w_lo), big, xs, hT, work, gate_sb, most, psum)


class Order:

    def __init__(self, eng, sem, base=0):
        self.eng, self.sem, self.base, self.n = eng, sem, base, 0

    def done(self, ins):
        ins.then_inc(self.sem, 1)
        self.n += 1

    def wait(self):
        self.eng.wait_ge(self.sem, self.base + self.n)

    def link(self, ins):
        self.done(ins)
        self.wait()


def projections(nc, sem, src, dst, edge_attr_8, edge_attr_8_n2, x, Wqkv, bqkv, Wo, W1, W2, ln1_g, ln1_b, rec_d,
                rows_d, logits_d, wo, w_lo, w_hi, big, xs, hT, vs, work, small, tab_f, tab, iota_n, ident, ones, below, psum):
    free = big.rearrange("p a n -> p (a n)")[0:EP, 8 * NP:16 * NP]
    ints = free[:, 0:2 * EJ].bitcast(I32).rearrange("p (a j) -> p a j", a=2)
    blk_i = free[:, 2 * EJ:3 * EJ].bitcast(I32)
    blk = free[:, 3 * EJ:4 * EJ]
    near = free[:, 4 * EJ:(4 + H) * EJ]
    path = free[:, (4 + H) * EJ:(4 + 2 * H) * EJ]
    rec = free[:, (4 + 2 * H) * EJ:(4 + 2 * H + REC) * EJ].rearrange("p (j c) -> p j c", c=REC)
    eq = w_hi[0:EP, 0:EJ * NB].rearrange("p (j b) -> p j b", b=NB)
    pos = w_hi[0:EP, EJ * NB:2 * EJ * NB].rearrange("p (j b) -> p j b", b=NB)
    rest_lo = w_lo[:, DC * 3 * D:]
    e_up = rest_lo[0:EP, 0:EJ]
    e_down = rest_lo[0:EP, EJ:2 * EJ]
    ends = rest_lo[0:EP, 2 * EJ:2 * EJ + 2 * NB]
    pad = rest_lo[:, 3 * EJ:3 * EJ + CT * REC]
    zeros = rest_lo[:, 4 * EJ:4 * EJ + D]
    ends_t = small[0:2 * NB, 60:61]
    loaded, consts, edge_own, edge_turned, stored, tabled, poolown, eq_used = map(
        sem, ("edge_loaded", "edge_consts", "edge_own", "edge_turned", "edge_stored", "edge_tabled", "edge_poolown",
              "eq_used"))
    wqkv = w_lo[:, 0:DC * 3 * D].rearrange("p (c n) -> p c n", c=DC)
    w1 = w_hi[:, 0:DC * FF].rearrange("p (c n) -> p c n", c=DC)
    w2 = w_hi[:, 2 * SLOT:2 * SLOT + DC * FF].rearrange("p (c n) -> p c n", n=D)
    g1 = work[:, 0:D]
    s1 = work[:, D:2 * D]
    bv = work[:, 2 * D:3 * D]
    hrow = [work[:, (3 + i) * D:(4 + i) * D] for i in range(2)]
    stage = [work[:, (6 + i) * NP:(7 + i) * NP] for i in range(STAGES)]
    eps = small[:, 0:1]
    bqk_row = work[0:2 * DC, 5 * D:5 * D + P]
    bqk = small[:, 1:9]
    std = small[:, 10:15]
    rstd = small[:, 15:20]
    mv = small[:, 20:30].rearrange("p (t c) -> p t c", c=2)
    stats = small[:, 30:60].rearrange("p (t c) -> p t c", c=6)
    pairs = [(h, t) for t in range(NT) for h in range(H)]
    (x_in, vec_in, wqkv_in, later_in, zeroed, own, stds, rows, turned, moved, qk_ps, qk_sb, v_ps, v_sb, s_ps, s_act,
     s_dve, bqk_ready) = map(sem, (
        "x_in", "vec_in", "wqkv_in", "later_in", "tail_zeroed", "ln_own", "ln_stds", "h_rows", "h_turned", "h_moved",
        "qk_ps", "qk_sb", "v_ps", "v_sb", "s_ps", "s_act", "s_dve", "bqk_ready"))
    s_out = [sem(f"s_out{i}") for i in range(STAGES)]
    bqk_turned = sem("bqk_turned")
    scale = float(D) ** -0.5

    with nc.Block() as block:
        @block.sync
        def _(sp):
            full, rest = node_tiles(x)
            sp.wait_ge(zeroed, 1)
            sp.dma_start(xs[:, 0:NT - 1, :], full).then_inc(x_in, 16)
            sp.dma_start(xs[0:LAST, NT - 1, :], rest).then_inc(x_in, 16)
            sp.dma_start(bqk_row, bqkv[0:2 * D].rearrange("(m p) -> m p", p=P)).then_inc(vec_in, 16)
            for to, vec in ((g1, ln1_g), (s1, ln1_b), (bv, bqkv[2 * D:3 * D])):
                sp.dma_start(to, vec.rearrange("(a n) -> a n", a=1).broadcast_to([P, D])).then_inc(vec_in, 16)
            sp.dma_start(wqkv, Wqkv.rearrange("(c p) n -> p c n", p=P)).then_inc(wqkv_in, 16)
            sp.dma_start(ints[:, 0, :], src.rearrange("(p j) -> p j", j=EJ)).then_inc(loaded, 16)
            sp.dma_start(ints[:, 1, :], dst.rearrange("(p j) -> p j", j=EJ)).then_inc(loaded, 16)
            sp.dma_start(near, edge_attr_8.rearrange("(p j) h -> p (j h)", j=EJ)).then_inc(loaded, 16)
            sp.dma_start(path, edge_attr_8_n2.rearrange("(p j) h -> p (j h)", j=EJ)).then_inc(loaded, 16)
            sp.dma_start(wo[:, :, :], Wo.rearrange("(c p) n -> p c n", p=P)).then_inc(later_in, 16)
            sp.wait_ge(consts, 9)
            sp.dma_start(rec_d[NE:NE + CHUNK, :].rearrange("(p t) c -> p (t c)", t=CT), pad).then_inc(stored, 16)
            sp.dma_start(rows_d.rearrange("(a p) n -> p a n", p=P),
                         zeros.unsqueeze(1).broadcast_to([P, EX * CB, D])).then_inc(stored, 16)
            sp.wait_ge(edge_own, 3)
            sp.dma_start(rec_d[0:NE, :].rearrange("(p j) c -> p (j c)", j=EJ),
                         rec.rearrange("p j c -> p (j c)")).then_inc(stored, 16)
            sp.wait_ge(eq_used, 1)
            sp.dma_start(w1, W1.rearrange("(c p) n -> p c n", p=P)).then_inc(later_in, 16)
            sp.dma_start(w2, W2.rearrange("(c p) n -> p c n", p=P)).then_inc(later_in, 16)
            for i, (h, t) in enumerate(pairs):
                done = s_act if i % 2 == 0 else s_dve
                sp.wait_ge(done, i // 2 + 1)
                sp.dma_start(logits_d[t * BPT:(t + 1) * BPT, h, :, :].rearrange("b l s -> b l s"),
                             stage[i % STAGES]).then_inc(s_out[i % STAGES], 16)
            for k in range(STAGES):
                sp.wait_ge(s_out[k], 16 * len(pairs[k::STAGES]))
            sp.wait_ge(later_in, 48)
            sp.wait_ge(stored, 48)

        @block.gpsimd
        def _(pool):
            exact = dict(allow_small_or_imprecise_dtypes=True)
            pool.memset(xs[:, NT - 1, :], 0.0).then_inc(zeroed, 1)
            pool.memset(ident[:, :], 0.0).then_inc(poolown, 1)
            pool.memset(pad, 0.0).then_inc(poolown, 1)
            pool.memset(below[:, :], 1.0).then_inc(poolown, 1)
            pool.wait_ge(poolown, 3)
            pool.affine_select(out=ident[:, :], in_=ident[:, :], compare_op=ALU.not_equal, fill=1.0, base=0,
                               pattern=[[-1, P]], channel_multiplier=1).then_inc(consts, 1)
            pool.iota(iota_n[:, :], [[1, NP]], base=0, channel_multiplier=0, **exact).then_inc(consts, 1)
            pool.iota(e_up, [[1, EJ]], base=1, channel_multiplier=EJ, **exact).then_inc(consts, 1)
            pool.iota(e_down, [[-1, EJ]], base=NE, channel_multiplier=-EJ, **exact).then_inc(consts, 1)
            pool.memset(ones[:, :], 1.0).then_inc(consts, 1)
            pool.memset(pad.rearrange("p (t c) -> p t c", c=REC)[:, :, 1:2], -1.0).then_inc(consts, 2)
            pool.memset(zeros, 0.0).then_inc(consts, 1)
            pool.affine_select(out=below[:, :], in_=below[:, :], compare_op=ALU.is_gt, fill=0.0, base=0,
                               pattern=[[1, P]], channel_multiplier=-1).then_inc(consts, 1)

        @block.vector
        def _(dve):
            o = Order(dve, own)
            dve.memset(eps, EPS).then_inc(own, 1)
            o.n += 1
            dve.wait_ge(x_in, 32)
            for norm in range(2):
                for t in range(NT):
                    o.done(dve.bn_stats(stats[:, t, :], xs[:, t, :]))
                o.wait()
                for t in range(NT):
                    o.done(dve.bn_aggr(mv[:, t, :], stats[:, t, :]))
                o.wait()
                dve.wait_ge(stds, norm + 1)
                o.link(dve.reciprocal(rstd, std))
                if norm == 0:
                    for t in range(NT):
                        o.done(dve.tensor_scalar(xs[:, t, :], xs[:, t, :], mv[:, t, 0:1], rstd[:, t:t + 1],
                                                 ALU.subtract, ALU.mult))
                    o.wait()
            dve.wait_ge(vec_in, 64)
            dve.wait_ge(bqk_turned, 1)
            dve.tensor_scalar(bqk[:, 0:DC], psum[7][:, 0:DC], scale, None, ALU.mult).then_inc(bqk_ready, 1)
            dve.tensor_copy(bqk[:, DC:2 * DC], psum[7][:, DC:2 * DC]).then_inc(bqk_ready, 1)
            for t in range(NT):
                r = hrow[t % 2]
                if t >= 2:
                    dve.wait_ge(turned, t - 1)
                o.link(dve.scalar_tensor_tensor(out=r, in0=xs[:, t, :], scalar=mv[:, t, 0:1], in1=g1,
                                                op0=ALU.subtract, op1=ALU.mult))
                dve.scalar_tensor_tensor(out=r, in0=r, scalar=rstd[:, t:t + 1], in1=s1, op0=ALU.mult,
                                         op1=ALU.add).then_inc(rows, 1)
            oe = Order(dve, edge_own)
            dve.wait_ge(loaded, 64)
            oe.done(dve.tensor_copy(rec[:, :, 0], ints[:, 0, :]))
            oe.done(dve.tensor_copy(rec[:, :, 1], ints[:, 1, :]))
            oe.done(dve.tensor_tensor(rec[:, :, 2:REC], near.rearrange("p (j h) -> p j h", h=H),
                                      path.rearrange("p (j h) -> p j h", h=H), ALU.add))
            oe.link(dve.tensor_scalar(blk_i, ints[:, 1, :], BN.bit_length() - 1, None, ALU.arith_shift_right))
            oe.link(dve.tensor_copy(blk, blk_i))
            dve.wait_ge(consts, 9)
            oe.link(dve.tensor_tensor(eq, blk.unsqueeze(2).broadcast_to([EP, EJ, NB]),
                                      iota_n[0:EP, 0:NB].unsqueeze(1).broadcast_to([EP, EJ, NB]), ALU.is_equal))
            for k, e in enumerate((e_up, e_down)):
                oe.link(dve.tensor_tensor(pos, eq, e.unsqueeze(2).broadcast_to([EP, EJ, NB]), ALU.mult))
                oe.link(dve.tensor_reduce(ends[:, k * NB:(k + 1) * NB], pos.rearrange("p j b -> p b j"), AX.X,
                                          ALU.max))
            dve.sem_inc(eq_used, 1)
            for t in range(NT):
                dve.wait_ge(v_ps, t + 1)
                dve.tensor_tensor(vs[:, t, :], psum[4 + t % 2][:, :], bv, ALU.add).then_inc(v_sb, 1)
            dve.wait_ge(edge_turned, 1)
            oe.link(dve.tensor_reduce(ends_t, psum[6][0:2 * NB, 0:EP], AX.X, ALU.max))
            dve.wait_ge(edge_turned, 2)
            oe.link(dve.tensor_scalar(tab_f[0:1, 0:NB], psum[7][0:1, NB:2 * NB], -1.0, float(NE), ALU.mult, ALU.add))
            oe.link(dve.tensor_copy(tab_f[0:1, NB:2 * NB], psum[7][0:1, 0:NB]))
            oe.link(dve.tensor_tensor(tab_f[0:1, 2 * NB + 1:3 * NB + 1], tab_f[0:1, NB:2 * NB], tab_f[0:1, 0:NB],
                                      ALU.subtract))
            oe.link(dve.tensor_reduce(tab_f[0:1, 2 * NB:2 * NB + 1], tab_f[0:1, 2 * NB + 1:3 * NB + 1], AX.X, ALU.max))
            dve.tensor_copy(tab[0:1, :], tab_f[0:1, 0:2 * NB + 1]).then_inc(tabled, 1)
            for i in range(1, len(pairs), 2):
                dve.wait_ge(s_ps, i + 1)
                if i >= STAGES:
                    dve.wait_ge(s_out[i % STAGES], 16 * (i // STAGES))
                a, b = (psum[2 * (i % 4)], psum[2 * (i % 4) + 1])
                dve.tensor_copy(stage[i % STAGES][:, 0:HALF], a[:, 0:HALF])
                dve.tensor_copy(stage[i % STAGES][:, HALF:NP], b[:, 0:HALF]).then_inc(s_dve, 1)

        @block.scalar
        def _(act):
            for norm in range(2):
                act.wait_ge(own, 1 + 10 + 16 * norm)
                act.activation(std, mv[:, :, 1], ACT.Sqrt, bias=eps).then_inc(stds, 1)
            for t in range(NT):
                act.wait_ge(turned, t + 1)
                act.activation(hT[:, :, t * P:(t + 1) * P], psum[t % 2][:, :].rearrange("p (c n) -> p c n", c=DC),
                               ACT.Copy).then_inc(moved, 1)
            act.wait_ge(bqk_ready, 2)
            for m in range(2 * DC):
                for half in range(2):
                    i = 2 * m + half
                    act.wait_ge(qk_ps, i + 1)
                    act.activation(big[:, m, half * HALF:(half + 1) * HALF], psum[i % 4][:, 0:HALF], ACT.Identity,
                                   bias=bqk[:, m:m + 1], scale=scale if m < DC else 1.0).then_inc(qk_sb, 1)
            for i in range(0, len(pairs), 2):
                act.wait_ge(s_ps, i + 1)
                if i >= STAGES:
                    act.wait_ge(s_out[i % STAGES], 16 * (i // STAGES))
                a, b = (psum[2 * (i % 4)], psum[2 * (i % 4) + 1])
                act.activation(stage[i % STAGES][:, 0:HALF], a[:, 0:HALF], ACT.Copy)
                act.activation(stage[i % STAGES][:, HALF:NP], b[:, 0:HALF], ACT.Copy).then_inc(s_act, 1)

        @block.tensor
        def _(pe):
            pe.wait_ge(consts, 9)
            pe.wait_ge(vec_in, 64)
            pe.transpose(psum[7][:, 0:2 * DC], bqk_row, ident[0:2 * DC, 0:2 * DC]).then_inc(bqk_turned, 1)
            for t in range(NT):
                pe.wait_ge(rows, t + 1)
                if t >= 2:
                    pe.wait_ge(moved, t - 1)
                for c in range(DC):
                    last = pe.transpose(psum[t % 2][:, c * P:(c + 1) * P], hrow[t % 2][:, c * P:(c + 1) * P],
                                        ident[:, :])
                last.then_inc(turned, 1)
            pe.wait_ge(moved, NT)
            pe.wait_ge(wqkv_in, 16)
            for m in range(2 * DC):
                for half in range(2):
                    i = 2 * m + half
                    if i >= 4:
                        pe.wait_ge(qk_sb, i - 3)
                    for c in range(DC):
                        last = pe.matmul(psum[i % 4][:, 0:HALF], wqkv[:, c, m * P:(m + 1) * P],
                                         hT[:, c, half * HALF:(half + 1) * HALF], start=c == 0, stop=c == DC - 1)
                    last.then_inc(qk_ps, 1)
            for t in range(NT):
                if t >= 2:
                    pe.wait_ge(v_sb, t - 1)
                for c in range(DC):
                    last = pe.matmul(psum[4 + t % 2][:, :], hT[:, c, t * P:(t + 1) * P], wqkv[:, c, 2 * D:3 * D],
                                     start=c == 0, stop=c == DC - 1)
                last.then_inc(v_ps, 1)
            pe.wait_ge(edge_own, 10)
            pe.transpose(psum[6][0:2 * NB, 0:EP], ends, ident[0:EP, 0:EP]).then_inc(edge_turned, 1)
            pe.wait_ge(edge_own, 11)
            pe.matmul(psum[7][0:1, 0:2 * NB], ends_t, ident[0:2 * NB, 0:2 * NB], start=True,
                      stop=True).then_inc(edge_turned, 1)
            pe.wait_ge(qk_sb, 4 * DC)
            pe.wait_ge(v_sb, NT)
            for i, (h, t) in enumerate(pairs):
                r = slice(DH * (h % 2), DH * (h % 2 + 1))
                if i == 3:
                    pe.wait_ge(edge_own, 13)
                if i >= 4:
                    pe.wait_ge(s_act if i % 2 == 0 else s_dve, i // 2 - 1)
                for half in range(2):
                    last = pe.matmul(psum[2 * (i % 4) + half][:, 0:HALF],
                                     big[r, DC + h // 2, t * P:(t + 1) * P],
                                     big[r, h // 2, half * HALF:(half + 1) * HALF], start=True, stop=True)
                last.then_inc(s_ps, 1)


def attention(nc, sem, rec_d, logits_d, big, hT, vs, iota_n, ident, ones, tab, small, psum):
    with ExitStack() as stage:
        def sb(name, shape, dt=F32):
            t = stage.enter_context(nc.sbuf_tensor(name, shape, dt))
            return t[(slice(None),) * len(shape)]

        X = [sb(f"biases{i}", [P, CT, P]) for i in range(2)]
        R = sb("bias_exp", [P, CT, P])
        Rhi, Rlo = ([sb(f"bias_exp_{name}{i}", [P, CT, P], F32R) for i in range(2)] for name in ("hi", "lo"))
        onehot = [sb(f"onehot{i}", [P, CT, NP], F32R) for i in range(2)]
        S = [sb(f"logits{i}", [P, NP]) for i in range(2)]
        L = sb("exponents", [P, NP])
        PR = sb("weights", [P, NP])
        XM = sb("largest", [P, 2, P])
        rec = [sb(f"records{i}", [P, CT, REC]) for i in range(2)]
        miss = [sb(f"miss{i}", [P, CT, BN]) for i in range(2)]
        minus_big = sb("minus_big", [P, 1])
        diag = sb("diag", [P, P])
        attention_blocks(nc, sem, rec_d, logits_d, big, hT, vs, iota_n, ident, ones, tab, small, psum,
                         X, R, Rhi, Rlo, onehot, S, L, PR, XM, rec, miss, minus_big, diag)


def attention_blocks(nc, sem, rec_d, logits_d, big, hT, vs, iota_n, ident, ones, tab, small, psum,
                     X, R, Rhi, Rlo, onehot, S, L, PR, XM, rec, miss, minus_big, diag):
    PT = big[:, 8:16, :].rearrange("p a n -> p (a n)").rearrange("p (t h d) -> p t h d", t=NT, h=H)
    tiny = small[:, 0:1]
    guard, nguard, total, inv, worst = (small[:, k:k + 1] for k in range(1, 6))
    psT, psM = psum[0][:, 0:P], psum[0][:, P:2 * P]
    psW = [(psum[1], psum[2]), (psum[3], psum[4])]
    psP = (psum[5], psum[6])
    psO = psum[7]

    (consts, poolown, x_ready, xm_ready, xm_turned, own, diag_ready, rep_ready, d_done, r_ready, oh_ready,
     l_ready, g_ready, e_ready, inv_ready, p_ready, p_turned, pt_ready, o_ready, o_moved, w_ready, rhi_ready, rlo_ready, last_oh_ready) = map(sem, (
         "at_consts", "at_poolown", "x_ready", "xm_ready", "xm_turned", "at_own", "diag_ready", "rep_ready", "d_done",
         "r_ready", "oh_ready", "l_ready", "g_ready", "e_ready", "inv_ready", "p_ready",
         "p_turned", "pt_ready", "o_ready", "o_moved", "w_ready", "rhi_ready",
         "rlo_ready", "last_oh_ready"))
    worst_ready = sem("worst_ready")
    rec_in = [sem(f"rec_in{i}") for i in range(2)]
    s_in = [sem(f"s_in{i}") for i in range(2)]
    half = BPT // 2

    with nc.Block() as block:
        @block.sync
        def _(sp):
            longest = sp.value_load(tab[0:1, 2 * NB:2 * NB + 1], min_val=-NE, max_val=NE)
            with sp.If(longest < CHUNK + 1):
                def number(v):
                    return v if isinstance(v, int) else sp.snap(v)

                def records(b, k, at):
                    sp.dma_start(rec[k % 2].rearrange("p t c -> p (t c)"),
                                 rec_d.rearrange("e c -> (e c)")[bass.ds(at, CHUNK * REC)]
                                 .rearrange("(p n) -> p n", p=P)).then_inc(rec_in[k % 2], 16)

                def record_at(b):
                    return sp.snap(sp.value_load(tab[0:1, bass.ds(b, 1)], min_val=0, max_val=NE) * REC)

                def tile(j, last=False):
                    for k in range(BPT):
                        b = j * BPT + k
                        further = not (last and k >= BPT - 2)
                        if further:
                            at = record_at(b + 2)
                            used, hot_used = number(b + 1), number((b + 1) * (CT - 1))
                        row, free = number(b * (P * NP)), number(b - 1)
                        if further:
                            sp.wait_ge(oh_ready, hot_used)
                            sp.wait_ge(x_ready, used)
                            sp.wait_ge(last_oh_ready, used)
                            records(b + 2, k, at)
                        wait_past(sp, e_ready, free)
                        sp.dma_start(S[k % 2], logits_d.rearrange("b h l s -> (b h l s)")[bass.ds(row, P * NP)]
                                     .rearrange("(p n) -> p n", p=P)).then_inc(s_in[k % 2], 16)

                for k in range(2):
                    records(k, k, record_at(k))
                tile(0)
                with sp.Fori(1, NT - 1) as j:
                    tile(j)
                tile(NT - 1, True)

        @block.gpsimd
        def _(pool):
            longest = pool.value_load(tab[0:1, 2 * NB:2 * NB + 1], min_val=-NE, max_val=NE)
            with pool.If(longest < CHUNK + 1):
                pool.memset(minus_big, -BIG).then_inc(consts, 1)
                pool.memset(tiny, TINY).then_inc(consts, 1)
                pool.wait_ge(consts, 2)

                def biases(b, k, came):
                    m = miss[k % 2]
                    wait_past(pool, w_ready, b - 2)
                    wait_past(pool, rec_in[k % 2], came)
                    pool.tensor_tensor(m, rec[k % 2][:, :, 1:2].broadcast_to([P, CT, BN]),
                                       iota_n[:, bass.ds(b * BN, BN)].unsqueeze(1).broadcast_to([P, CT, BN]),
                                       ALU.subtract).then_inc(poolown, 1)
                    wait_past(pool, poolown, 3 * b + 1)
                    pool.tensor_tensor(m, m, m, ALU.mult).then_inc(poolown, 1)
                    wait_past(pool, poolown, 3 * b + 2)
                    pool.tensor_tensor(m, m, minus_big.unsqueeze(1).broadcast_to([P, CT, BN]), ALU.mult)\
                        .then_inc(poolown, 1)
                    wait_past(pool, poolown, 3 * b + 3)
                    wait_past(pool, r_ready, b - 1)
                    pool.tensor_tensor(X[k % 2].rearrange("p t (h d) -> p t h d", h=H),
                                       rec[k % 2][:, :, 2:REC].unsqueeze(3).broadcast_to([P, CT, H, BN]),
                                       m.unsqueeze(2).broadcast_to([P, CT, H, BN]), ALU.add).then_inc(x_ready, 1)

                def last_onehot(b, k):
                    pool.tensor_scalar(onehot[k % 2][:, CT - 1, :], iota_n[:, :], rec[k % 2][:, CT - 1, 0:1], None,
                                       ALU.is_equal).then_inc(last_oh_ready, 1)

                def low_part(b, k):
                    wait_past(pool, rhi_ready, b + 1)
                    pool.tensor_tensor(Rlo[k % 2], R, Rhi[k % 2], ALU.subtract).then_inc(rlo_ready, 1)

                def tile(j, last=False):
                    for k in range(BPT):
                        b = j * BPT + k
                        if not (last and k >= BPT - 2):
                            biases(b + 2, k, 16 * half * j + 16 * (k // 2 + 2))
                        if not (last and k == BPT - 1):
                            if last:
                                pool.wait_ge(w_ready, b)
                            last_onehot(b + 1, k + 1)
                            low_part(b + 1, k + 1)

                biases(0, 0, 16)
                last_onehot(0, 0)
                biases(1, 1, 16)
                low_part(0, 0)
                tile(0)
                with pool.Fori(1, NT - 1) as j:
                    tile(j)
                tile(NT - 1, True)

        @block.vector
        def _(dve):
            longest = dve.value_load(tab[0:1, 2 * NB:2 * NB + 1], min_val=-NE, max_val=NE)
            with dve.If(longest < CHUNK + 1):
                dve.wait_ge(consts, 2)

                def onehots(b, k, tiles, came):
                    wait_past(dve, rec_in[k % 2], came)
                    for t in tiles:
                        wait_past(dve, w_ready, b - 1)
                        dve.tensor_scalar(onehot[k % 2][:, t, :], iota_n[:, :], rec[k % 2][:, t, 0:1], None,
                                          ALU.is_equal).then_inc(oh_ready, 1)

                def largest(b, k):
                    wait_past(dve, x_ready, b + 1)
                    dve.tensor_reduce(XM[:, k % 2, :], X[k % 2].rearrange("p t m -> p m t"), AX.X, ALU.max)\
                       .then_inc(xm_ready, 1)

                def diagonal(b, k):
                    wait_past(dve, xm_turned, b + 1)
                    dve.tensor_reduce(worst, psT, AX.X, ALU.max).then_inc(worst_ready, 1)
                    wait_past(dve, worst_ready, b + 1)
                    dve.tensor_scalar(diag, ident[:, :], worst, -BIG / 10, ALU.mult, ALU.max).then_inc(diag_ready, 1)

                def lower(b, k):
                    wait_past(dve, rep_ready, b + 1)
                    dve.tensor_tensor(X[k % 2], X[k % 2], psM.unsqueeze(1).broadcast_to([P, CT, P]), ALU.subtract)\
                       .then_inc(d_done, 1)

                def weights(b, k):
                    lo, hi = psW[k % 2]
                    wait_past(dve, e_ready, b + 1)
                    wait_past(dve, p_turned, b)
                    dve.tensor_tensor_reduce(PR[:, 0:HALF], lo[:, 0:HALF], L[:, 0:HALF], 1.0, 1e-37, ALU.mult, ALU.add,
                                             total).then_inc(own, 1)
                    wait_past(dve, own, 2 * b + 1)
                    dve.tensor_tensor_reduce(PR[:, HALF:NP], hi[:, 0:HALF], L[:, HALF:NP], 1.0, total, ALU.mult,
                                             ALU.add, guard).then_inc(own, 1)
                    wait_past(dve, own, 2 * b + 2)
                    dve.reciprocal(inv, guard).then_inc(inv_ready, 1)

                def guards(b, k, came, further, came_on):
                    wait_past(dve, l_ready, b + 1)
                    wait_past(dve, s_in[k % 2], came)
                    if further:
                        onehots(b + 2, k, (1,), came_on)
                    dve.tensor_tensor_reduce(L, L, S[k % 2], -1.0, 3e38, ALU.add, ALU.min, nguard).then_inc(g_ready, 1)

                def collect(j, at):
                    wait_past(dve, o_ready, j + 1)
                    dve.tensor_copy(hT[:, :, bass.ds(at, P)], psO[:, :].rearrange("p (c d) -> p c d", c=DC))\
                       .then_inc(o_moved, 1)

                def tile(j, last=False):
                    for k in range(BPT):
                        b = j * BPT + k
                        came_on = 16 * half * j + 16 * (k // 2 + 2)
                        further = not (last and k >= BPT - 2)
                        if not (last and k == BPT - 1):
                            lower(b + 1, k + 1)
                        if not (isinstance(b, int) and b == 0):
                            weights(b - 1, k + 1)
                        if further:
                            largest(b + 2, k)
                            onehots(b + 2, k, (0,), came_on)
                        guards(b, k, 16 * half * j + 16 * (k // 2 + 1), further, came_on)
                        if further:
                            onehots(b + 2, k, (2,), came_on)
                            diagonal(b + 2, k)
                            onehots(b + 2, k, (3,), came_on)
                        if k == 2 and not (isinstance(j, int) and j == 0):
                            collect(j - 1, j * P - P)

                largest(0, 0)
                diagonal(0, 0)
                onehots(0, 0, (0, 1, 2, 3), 16)
                lower(0, 0)
                largest(1, 1)
                diagonal(1, 1)
                onehots(1, 1, (0, 1, 2, 3), 16)
                tile(0)
                with dve.Fori(1, NT - 1) as j:
                    tile(j)
                tile(NT - 1, True)
                weights(NB - 1, 1)
                collect(NT - 1, (NT - 1) * P)

        @block.scalar
        def _(act):
            longest = act.value_load(tab[0:1, 2 * NB:2 * NB + 1], min_val=-NE, max_val=NE)
            with act.If(longest < CHUNK + 1):
                act.preload_act_table_set("natural_log_exp_and_others")
                act.wait_ge(consts, 2)

                def weigh(b, k):
                    wait_past(act, d_done, b + 1)
                    wait_past(act, rlo_ready, b)
                    act.activation(R, X[k % 2], ACT.Exp).then_inc(r_ready, 1)
                    wait_past(act, r_ready, b + 1)
                    wait_past(act, w_ready, b - 1)
                    act.activation(Rhi[k % 2], R, ACT.Copy).then_inc(rhi_ready, 1)

                def logs(b, k):
                    wait_past(act, w_ready, b + 1)
                    wait_past(act, inv_ready, b)
                    lo, hi = psW[k % 2]
                    act.activation(L[:, 0:HALF], lo[:, 0:HALF], ACT.Ln, bias=tiny)
                    act.activation(L[:, HALF:NP], hi[:, 0:HALF], ACT.Ln, bias=tiny).then_inc(l_ready, 1)

                def exps(b, k):
                    wait_past(act, g_ready, b + 1)
                    act.activation(L, S[k % 2], ACT.Exp, bias=nguard).then_inc(e_ready, 1)

                def norm(b):
                    wait_past(act, inv_ready, b + 1)
                    act.activation(PR, PR, ACT.Copy, scale=inv).then_inc(p_ready, 1)

                def keep(b, k, used):
                    wait_past(act, p_turned, b + 1)
                    wait_past(act, o_ready, used)
                    lo = psP[0][:, :].rearrange("s (t h d) -> s t h d", t=4, h=H)
                    for t in range(4):
                        act.activation(PT[:, t, :, k * BN:(k + 1) * BN], lo[:, t], ACT.Copy)
                    act.activation(PT[:, 4, :, k * BN:(k + 1) * BN], psP[1][:, 0:P].rearrange("s (h d) -> s h d", h=H),
                                   ACT.Copy).then_inc(pt_ready, 1)

                def tile(j, last=False):
                    for k in range(BPT):
                        b = j * BPT + k
                        first = isinstance(b, int) and b == 0
                        if not first:
                            exps(b - 1, k + 1)
                        if not (last and k == BPT - 1):
                            weigh(b + 1, k + 1)
                        logs(b, k)
                        if not first:
                            norm(b - 1)
                            keep(b - 1, (k - 1) % BPT, j if k else j - 1)

                weigh(0, 0)
                tile(0)
                with act.Fori(1, NT - 1) as j:
                    tile(j)
                tile(NT - 1, True)
                exps(NB - 1, 1)
                norm(NB - 1)
                keep(NB - 1, BPT - 1, NT - 1)

        @block.tensor
        def _(pe):
            longest = pe.value_load(tab[0:1, 2 * NB:2 * NB + 1], min_val=-NE, max_val=NE)
            with pe.If(longest < CHUNK + 1):
                def turn_largest(b, k):
                    wait_past(pe, xm_ready, b + 1)
                    wait_past(pe, d_done, b)
                    pe.transpose(psT, XM[:, k % 2, :], ident[:, :]).then_inc(xm_turned, 1)

                def spread(b):
                    wait_past(pe, diag_ready, b + 1)
                    pe.matmul(psM, ones[:, :], diag, start=True, stop=True).then_inc(rep_ready, 1)

                def sums(b, k, part):
                    lo, hi = psW[k % 2]
                    r = (Rhi, Rlo)[part][k % 2]
                    if part == 0:
                        wait_past(pe, inv_ready, b - 1)
                        wait_past(pe, oh_ready, (CT - 1) * (b + 1))
                        wait_past(pe, last_oh_ready, b + 1)
                    wait_past(pe, rlo_ready if part else rhi_ready, b + 1)
                    for t in range(CT):
                        for bank, half_ in ((lo, 0), (hi, HALF)):
                            last = pe.matmul(bank[:, 0:HALF], r[:, t, :], onehot[k % 2][:, t, half_:half_ + HALF],
                                             start=t == 0 and part == 0, stop=t == CT - 1 and part == 1)
                    if part:
                        last.then_inc(w_ready, 1)

                def turn(b):
                    wait_past(pe, p_ready, b + 1)
                    wait_past(pe, pt_ready, b)
                    for t in range(NT):
                        to = psP[t // 4][:, (t % 4) * P:(t % 4 + 1) * P]
                        last = pe.transpose(to, PR[:, t * P:(t + 1) * P], ident[:, :])
                    last.then_inc(p_turned, 1)

                def weighted_sums(j):
                    wait_past(pe, pt_ready, BPT * (j + 1))
                    wait_past(pe, o_moved, j)
                    for h in range(H):
                        r = slice(DH * (h % 2), DH * (h % 2 + 1))
                        for t in range(NT):
                            last = pe.matmul(psO[r, (h // 2) * P:(h // 2 + 1) * P], vs[:, t, h * DH:(h + 1) * DH],
                                             PT[:, t, h, :], start=t == 0, stop=t == NT - 1)
                    last.then_inc(o_ready, 1)

                def tile(j, last=False):
                    for k in range(BPT):
                        b = j * BPT + k
                        further = not (last and k >= BPT - 2)
                        sums(b, k, 0)
                        if not (last and k == BPT - 1):
                            spread(b + 1)
                        sums(b, k, 1)
                        if further:
                            turn_largest(b + 2, k)
                        if k == 1 and not (isinstance(j, int) and j == 0):
                            weighted_sums(j - 1)
                        if not (isinstance(b, int) and b == 0):
                            turn(b - 1)

                turn_largest(0, 0)
                spread(0)
                turn_largest(1, 1)
                tile(0)
                with pe.Fori(1, NT - 1) as j:
                    tile(j)
                tile(NT - 1, True)
                turn(NB - 1)
                weighted_sums(NT - 1)


def feed_forward(nc, sem, x, bo, ln2_g, ln2_b, b1, b2, wo, w_hi, xs, hT, vs, work, small, ident, psum):
    with ExitStack() as stage:
        def sb(name, shape, dt=F32R):
            t = stage.enter_context(nc.sbuf_tensor(name, shape, dt))
            return t[(slice(None),) * len(shape)]

        parts = ("hi", "lo")
        rows_T = [sb(f"ff_rows_{part}", [P, DC, NP]) for part in parts]
        w1s = [[sb(f"ff_w1_{part}{i}", [P, DC, P]) for part in parts] for i in range(2)]
        w2s = [[sb(f"ff_w2_{part}{i}", [P, D]) for part in parts] for i in range(4)]
        hid = [[sb(f"ff_hidden_{part}{i}", [P, NP]) for part in parts] for i in range(2)]
        h32 = [sb(f"ff_hidden{i}", [P, NP], F32) for i in range(2)]
        feed_forward_units(nc, sem, x, bo, ln2_g, ln2_b, b1, b2, wo, w_hi, xs, hT, vs, work, small, ident, psum,
                           rows_T, w1s, w2s, hid, h32)


def feed_forward_units(nc, sem, x, bo, ln2_g, ln2_b, b1, b2, wo, w_hi, xs, hT, vs, work, small, ident, psum,
                       rows_T, w1s, w2s, hid, h32):
    w1 = w_hi[:, 0:DC * FF].rearrange("p (c n) -> p c n", c=DC)
    w2 = w_hi[:, 2 * SLOT:2 * SLOT + DC * FF].rearrange("p (c n) -> p c n", n=D)
    g2, s2, bo_r, b2_r = (work[:, i * D:(i + 1) * D] for i in range(4))
    xin = work[:, 5 * D:10 * D].rearrange("p (t n) -> p t n", t=NT)
    hrow = [work[:, (10 + i) * D:(11 + i) * D] for i in range(2)]
    b1_row = work[0:FF // P, 12 * D:12 * D + P]
    b1c = vs[:, 0, 0:FF // P]
    eps = small[:, 0:1]
    std = small[:, 10:15]
    rstd = small[:, 15:20]
    mv = small[:, 20:30].rearrange("p (t c) -> p t c", c=2)
    stats = small[:, 30:60].rearrange("p (t c) -> p t c", c=6)
    MC = FF // P
    up_bank = psum[NT:8]
    h1_ready, mv_ready = sem("h1_ready"), sem("mv_ready")
    (vec_in, x_in, zeroed, own, stds, rows, turned, moved, rows_lo, o_ps, b1_turned, b1_ready, split_hi, split_lo, u_ps,
     u_sb, h_hi, h_lo, y_ps, y_sb, eps_set) = map(sem, (
         "ff_vec_in", "ff_x_in", "ff_zeroed", "ff_own", "ff_stds", "ff_rows", "ff_turned", "ff_moved", "ff_rows_lo",
         "o_ps", "b1_turned", "b1_ready", "ff_split_hi", "ff_split_lo", "u_ps", "u_sb", "ff_h_hi", "ff_h_lo", "y_ps",
         "y_sb", "ff_eps"))

    with nc.Block() as block:
        @block.sync
        def _(sp):
            for to, vec in ((g2, ln2_g), (s2, ln2_b), (bo_r, bo), (b2_r, b2)):
                sp.dma_start(to, vec.rearrange("(a n) -> a n", a=1).broadcast_to([P, D])).then_inc(vec_in, 16)
            sp.dma_start(b1_row, b1.rearrange("(m p) -> m p", p=P)).then_inc(vec_in, 16)
            full, rest = node_tiles(x)
            sp.wait_ge(zeroed, 1)
            sp.dma_start(xin[:, 0:NT - 1, :], full).then_inc(x_in, 16)
            sp.dma_start(xin[0:LAST, NT - 1, :], rest).then_inc(x_in, 16)

        @block.gpsimd
        def _(pool):
            pool.memset(xin[:, NT - 1, :], 0.0).then_inc(zeroed, 1)

        @block.vector
        def _(dve):
            def weights_lo(m):
                dve.wait_ge(split_hi, 2 * m + 1)
                dve.tensor_tensor(w1s[m % 2][1], w1[:, :, m * P:(m + 1) * P], w1s[m % 2][0], ALU.subtract)\
                   .then_inc(split_lo, 1)
                dve.wait_ge(split_hi, 2 * m + 2)
                dve.tensor_tensor(w2s[m % 4][1], w2[:, m, :], w2s[m % 4][0], ALU.subtract).then_inc(split_lo, 1)

            o = Order(dve, own)
            dve.memset(eps, EPS).then_inc(eps_set, 1)
            weights_lo(0)
            def low_rows(t):
                dve.wait_ge(moved, t + 1)
                dve.tensor_tensor(rows_T[1][:, :, t * P:(t + 1) * P],
                                  psum[2 + t % 2][:, :].rearrange("p (c n) -> p c n", c=DC),
                                  rows_T[0][:, :, t * P:(t + 1) * P], ALU.subtract).then_inc(rows_lo, 1)

            def row(t):
                r = hrow[t % 2]
                dve.wait_ge(stds, t + 1)
                o.link(dve.reciprocal(rstd[:, t:t + 1], std[:, t:t + 1]))
                if t >= 2:
                    dve.wait_ge(turned, t - 1)
                o.link(dve.scalar_tensor_tensor(out=r, in0=xs[:, t, :], scalar=mv[:, t, 0:1], in1=g2,
                                                op0=ALU.subtract, op1=ALU.mult))
                dve.scalar_tensor_tensor(out=r, in0=r, scalar=rstd[:, t:t + 1], in1=s2, op0=ALU.mult,
                                         op1=ALU.add).then_inc(rows, 1)

            dve.wait_ge(vec_in, 80)
            for t in range(NT):
                o.done(dve.tensor_tensor(xs[:, t, :], xs[:, t, :], bo_r, ALU.add))
            o.wait()
            for t in range(NT):
                dve.wait_ge(o_ps, t + 1)
                dve.tensor_tensor(xs[:, t, :], xs[:, t, :], psum[t % 2][:, :], ALU.add).then_inc(h1_ready, 1)
                dve.wait_ge(h1_ready, t + 1)
                o.link(dve.bn_stats(stats[:, t, :], xs[:, t, :]))
                dve.bn_aggr(mv[:, t, :], stats[:, t, :]).then_inc(mv_ready, 1)
                if t:
                    row(t - 1)
                if t > 1:
                    low_rows(t - 2)
            row(NT - 1)
            low_rows(NT - 2)
            low_rows(NT - 1)
            dve.wait_ge(b1_turned, 1)
            dve.tensor_copy(b1c, psum[7][:, 0:MC]).then_inc(b1_ready, 1)
            for m in range(MC):
                if m + 1 < MC:
                    weights_lo(m + 1)
                dve.wait_ge(h_hi, m + 1)
                dve.tensor_tensor(hid[m % 2][1], h32[m % 2], hid[m % 2][0], ALU.subtract).then_inc(h_lo, 1)
                if 2 <= m < 2 + NT:
                    t = m - 2
                    dve.wait_ge(x_in, 32)
                    o.link(dve.tensor_tensor(xin[:, t, :], xin[:, t, :], b2_r, ALU.add))
                    o.link(dve.tensor_tensor(xs[:, t, :], xs[:, t, :], xin[:, t, :], ALU.add))
            for t in range(NT):
                dve.wait_ge(y_ps, t + 1)
                dve.tensor_tensor(xs[:, t, :], xs[:, t, :], psum[t][:, :], ALU.add).then_inc(y_sb, 1)

        @block.scalar
        def _(act):
            def weights_hi(m):
                if m >= 2:
                    act.wait_ge(u_ps, 2 * (m - 1))
                act.activation(w1s[m % 2][0], w1[:, :, m * P:(m + 1) * P], ACT.Copy).then_inc(split_hi, 1)
                act.activation(w2s[m % 4][0], w2[:, m, :], ACT.Copy).then_inc(split_hi, 1)

            weights_hi(0)
            act.wait_ge(eps_set, 1)
            for t in range(NT + 1):
                if t < NT:
                    act.wait_ge(mv_ready, t + 1)
                    act.activation(std[:, t:t + 1], mv[:, t, 1:2], ACT.Sqrt, bias=eps).then_inc(stds, 1)
                if t:
                    act.wait_ge(turned, t)
                    act.activation(rows_T[0][:, :, (t - 1) * P:t * P],
                                   psum[2 + (t - 1) % 2][:, :].rearrange("p (c n) -> p c n", c=DC), ACT.Copy)\
                       .then_inc(moved, 1)
            act.wait_ge(b1_ready, 1)
            for m in range(MC):
                if m + 1 < MC:
                    weights_hi(m + 1)
                for half in range(2):
                    i = 2 * m + half
                    act.wait_ge(u_ps, i + 1)
                    if m >= 2:
                        act.wait_ge(h_lo, m - 1)
                    act.activation(h32[m % 2][:, half * HALF:(half + 1) * HALF], up_bank[i % 3][:, 0:HALF], ACT.Gelu,
                                   bias=b1c[:, m:m + 1]).then_inc(u_sb, 1)
                act.wait_ge(u_sb, 2 * m + 2)
                act.activation(hid[m % 2][0], h32[m % 2], ACT.Copy).then_inc(h_hi, 1)

        @block.tensor
        def _(pe):
            passes = ((0, 0), (0, 1), (1, 0))

            def turn(t):
                pe.wait_ge(rows, t + 1)
                if t >= 2:
                    pe.wait_ge(rows_lo, t - 1)
                for c in range(DC):
                    last = pe.transpose(psum[2 + t % 2][:, c * P:(c + 1) * P], hrow[t % 2][:, c * P:(c + 1) * P],
                                        ident[:, :])
                last.then_inc(turned, 1)

            for t in range(NT):
                if t >= 2:
                    pe.wait_ge(h1_ready, t - 1)
                for c in range(DC):
                    last = pe.matmul(psum[t % 2][:, :], hT[:, c, t * P:(t + 1) * P], wo[:, c, :], start=c == 0,
                                     stop=c == DC - 1)
                last.then_inc(o_ps, 1)
                if t >= 2:
                    turn(t - 2)
            pe.wait_ge(vec_in, 80)
            pe.transpose(psum[7][:, 0:MC], b1_row, ident[0:MC, 0:MC]).then_inc(b1_turned, 1)
            turn(NT - 2)
            turn(NT - 1)
            pe.wait_ge(rows_lo, NT)
            pe.wait_ge(b1_ready, 1)

            def down(m):
                pe.wait_ge(h_lo, m + 1)
                pe.wait_ge(split_lo, 2 * m + 2)
                for t in range(NT):
                    for i, (hp, wp) in enumerate(passes):
                        last = pe.matmul(psum[t][:, :], hid[m % 2][hp][:, t * P:(t + 1) * P], w2s[m % 4][wp],
                                         start=m == 0 and i == 0, stop=m == MC - 1 and i == 2)
                    if m == MC - 1:
                        last.then_inc(y_ps, 1)

            for m in range(MC):
                pe.wait_ge(split_lo, 2 * m + 1)
                for half in range(2):
                    k = 2 * m + half
                    if k >= 3:
                        pe.wait_ge(u_sb, k - 2)
                    for i, (wp, xp) in enumerate(passes):
                        for c in range(DC):
                            last = pe.matmul(up_bank[k % 3][:, 0:HALF], w1s[m % 2][wp][:, c, :],
                                             rows_T[xp][:, c, half * HALF:(half + 1) * HALF], start=i == 0 and c == 0,
                                             stop=i == 2 and c == DC - 1)
                    last.then_inc(u_ps, 1)
                if m:
                    down(m - 1)
            down(MC - 1)


def routing(nc, sem, w_in, gate_w, biases, w1, w3, w2, sw1, sw3, sw2, rows_d, slots, xs, hT, vs, work, gate_sb, iota_n,
            below, ones, most, small, ident, psum):
    with ExitStack() as stage:
        def sb(name, shape, dt=F32R):
            t = stage.enter_context(nc.sbuf_tensor(name, shape, dt))
            return t[(slice(None),) * len(shape)]

        parts = ("hi", "lo")
        rows_T = [sb(f"sh_rows_{part}", [P, DC, NP]) for part in parts]
        w1s, w3s = ([[sb(f"sh_{w}_{part}{i}", [P, DC, P]) for part in parts] for i in range(2)] for w in ("w1", "w3"))
        w2s = [[sb(f"sh_w2_{part}{i}", [P, D]) for part in parts] for i in range(4)]
        hid = [[sb(f"sh_hidden_{part}{i}", [P, NP]) for part in parts] for i in range(2)]
        h32 = [sb(f"sh_hidden{i}", [P, NP], F32) for i in range(2)]
        gated = [sb(f"sh_gated{i}", [P, HALF], F32) for i in range(2)]
        routing_units(nc, sem, w_in, gate_w, biases, w1, w3, w2, sw1, sw3, sw2, rows_d, slots, xs, hT, vs, work,
                      gate_sb, iota_n, below, ones, most, small, ident, psum, rows_T, w1s, w3s, w2s, hid, h32, gated)


def routing_units(nc, sem, w_in, gate_w, biases, w1, w3, w2, sw1, sw3, sw2, rows_d, slots, xs, hT, vs, work, gate_sb,
                  iota_n, below, ones, most, small, ident, psum, rows_T, w1s, w3s, w2s, hid, h32, gated):
    gate_row = work[0:EX, 0:D]
    bias_r = work[:, D:D + EX]
    gate_t = work[:, D + 8:D + 8 + DC * EX].rearrange("p (c e) -> p c e", c=DC)
    names = gate_views(gate_sb)
    gates, prob, slot_i = names["gates"], names["prob"], names["slot_i"]
    sc, sbias, top, topb, pick0, pick1, cum, tot, base, picked = (
        work[:, D + 40 + 40 * i:D + 80 + 40 * i].rearrange("p (t e) -> p t e", t=NT) for i in range(10))
    idx = work[:, D + 600:D + 640].bitcast(U32).rearrange("p (t e) -> p t e", t=NT)
    idx_f = work[:, D + 640:D + 680].rearrange("p (t e) -> p t e", t=NT)
    psums = work[:, D + 680:D + 685]
    first_slot = work[:, D + 688:D + 696]
    slot_f = work[:, D + 700:D + 710].rearrange("p (k t) -> p k t", k=2)
    count = work[:, D + 712:D + 720]
    most_f = work[:, D + 720:D + 721]
    weighed = work[:, D + 740:D + 780].rearrange("p (t e) -> p t e", t=NT)
    eps = small[:, 0:1]
    std = small[:, 10:15]
    rstd = small[:, 15:20]
    mv = small[:, 20:30].rearrange("p (t c) -> p t c", c=2)
    stats = small[:, 30:60].rearrange("p (t c) -> p t c", c=6)
    (vec_in, own, stds, rows, turned, moved, gate_turned, sc_ps, best, exp_out, a_ps, a_sb, b_sb, y_ps, y_sb,
     picks_ready, cum_ps, slots_ready, scattered) = map(sem, (
         "ro_vec_in", "ro_own", "ro_stds", "ro_rows", "ro_turned", "ro_moved", "gate_turned", "sc_ps", "best",
         "ro_exp_out", "sh_a_ps", "sh_a_sb", "sh_b_sb", "sh_y_ps", "sh_y_sb", "picks_ready", "cum_ps",
         "slots_ready", "scattered"))
    shared_in = [sem(f"shared_in{i}") for i in range(UNITS)]
    counts_taken = sem("counts_taken")
    rows_hi, rows_lo, split_hi, split_lo, h_hi, h_lo = map(sem, ("sh_rows_hi", "sh_rows_lo", "sh_split_hi",
                                                                 "sh_split_lo", "sh_h_hi", "sh_h_lo"))
    shared = expert_parts(slots, 0, sw1, sw3, sw2)

    def unit(n, a, m):
        return a[:, m, :] if n == 2 else a[:, :, m * P:(m + 1) * P]

    def split(n, m):
        return w2s[m % 4] if n == 2 else (w1s, w3s)[n][m % 2]

    up_bank = psum[NT:8]
    gate_ps, score_ps = psum[7][:, HALF:HALF + DC * EX], psum[NT - 1][:, 0:NT * EX]
    cum_bank, tot_bank = (psum[7][:, HALF + i * NT * EX:HALF + (i + 1) * NT * EX] for i in range(2))

    with nc.Block() as block:
        @block.sync
        def _(sp):
            sp.dma_start(gate_row, gate_w).then_inc(vec_in, 16)
            sp.dma_start(bias_r, biases.rearrange("(a n) -> a n", a=1).broadcast_to([P, EX])).then_inc(vec_in, 16)
            for u in range(UNITS):
                for n, (to, frm) in enumerate(shared):
                    cut = (slice(None), slice(u * UM, (u + 1) * UM)) if n == 2 else \
                        (slice(None), slice(None), slice(u * UW, (u + 1) * UW))
                    sp.dma_start(to[cut], frm[cut]).then_inc(shared_in[u], 16)
            for to, frm in expert_parts(slots, 3, w1[0], w3[0], w2[0]):
                sp.dma_start(to, frm).then_inc(w_in[0], 16)

        @block.gpsimd
        def _(pool):
            pool.wait_ge(slots_ready, 1)
            fullest = pool.value_load(most[0:1, 0:1], min_val=0, max_val=NP)
            with pool.If(fullest < CAP + 1):
                for t in range(NT):
                    n = P if t < NT - 1 else LAST
                    for k in range(2):
                        pool.indirect_dma_start(
                            out=rows_d, out_offset=bass.IndirectOffsetOnAxis(ap=slot_i[0:n, k, t:t + 1], axis=0),
                            in_=vs[0:n, t, :], in_offset=None).then_inc(scattered, 16)
                pool.wait_ge(scattered, 16 * 2 * NT)

        @block.vector
        def _(dve):
            o = Order(dve, own)
            for t in range(NT):
                o.done(dve.bn_stats(stats[:, t, :], xs[:, t, :]))
            o.wait()
            for t in range(NT):
                o.done(dve.bn_aggr(mv[:, t, :], stats[:, t, :]))
            dve.wait_ge(stds, 1)
            o.link(dve.reciprocal(rstd, std))
            for t in range(NT):
                dve.tensor_scalar(vs[:, t, :], xs[:, t, :], mv[:, t, 0:1], rstd[:, t:t + 1], ALU.subtract,
                                  ALU.mult).then_inc(rows, 1)
            dve.wait_ge(gate_turned, 1)
            o.link(dve.tensor_copy(gate_t, gate_ps.rearrange("p (c e) -> p c e", c=DC)))
            for t in range(NT):
                dve.wait_ge(rows_hi, t + 1)
                cut = slice(t * P, (t + 1) * P)
                dve.tensor_tensor(rows_T[1][:, :, cut], hT[:, :, cut], rows_T[0][:, :, cut], ALU.subtract)\
                   .then_inc(rows_lo, 1)

            def weights_lo(m, n):
                dve.wait_ge(split_hi, 3 * m + n + 1)
                dve.tensor_tensor(split(n, m)[1], unit(n, shared[n][0], m), split(n, m)[0], ALU.subtract)\
                   .then_inc(split_lo, 1)

            def hidden(m, half):
                i = 2 * m + half
                dve.wait_ge(a_sb, i + 1)
                dve.wait_ge(a_ps, 2 * i + 2)
                if m >= 2:
                    dve.wait_ge(h_lo, m - 1)
                dve.tensor_tensor(h32[m % 2][:, half * HALF:(half + 1) * HALF], gated[i % 2],
                                  up_bank[(2 * i + 1) % 3][:, 0:HALF], ALU.mult).then_inc(b_sb, 1)

            def chunk(m):
                for n in range(3):
                    if m + 1 < HC:
                        weights_lo(m + 1, n)
                    if n < 2:
                        hidden(m, n)
                dve.wait_ge(h_hi, m + 1)
                dve.tensor_tensor(hid[m % 2][1], h32[m % 2], hid[m % 2][0], ALU.subtract).then_inc(h_lo, 1)

            for n in range(3):
                weights_lo(0, n)
            chunk(0)
            dve.wait_ge(sc_ps, 1)
            o.link(dve.tensor_copy(sc, score_ps.rearrange("p (t e) -> p t e", t=NT)))
            o.link(dve.tensor_tensor(sbias, sc, bias_r.unsqueeze(1).broadcast_to([P, NT, EX]), ALU.add))
            for t in range(NT):
                o.done(dve.max(top[:, t, :], sc[:, t, :]))
                o.done(dve.max(topb[:, t, :], sbias[:, t, :]))
            o.wait()
            for t in range(NT):
                o.done(dve.max_index(idx[:, t, :], topb[:, t, :], sbias[:, t, :]))
            o.wait()
            dve.tensor_copy(idx_f, idx).then_inc(best, 1)
            dve.wait_ge(best, 1)

            chunk(1)
            for k, pick in enumerate((pick0, pick1)):
                o.done(dve.tensor_tensor(pick, iota_n[:, 0:EX].unsqueeze(1).broadcast_to([P, NT, EX]),
                                         idx_f[:, :, k:k + 1].broadcast_to([P, NT, EX]), ALU.is_equal))
            o.wait()
            dve.tensor_tensor(picked, pick0, pick1, ALU.add).then_inc(picks_ready, 1)
            dve.wait_ge(picks_ready, 1)
            chunk(2)
            dve.wait_ge(exp_out, 1)
            o.link(dve.tensor_scalar(prob, prob, 1.0, None, ALU.add))
            o.link(dve.reciprocal(prob, prob))
            o.link(dve.tensor_reduce(psums, prob, AX.X, ALU.add))
            o.link(dve.reciprocal(psums, psums))
            o.link(dve.tensor_tensor(prob, prob, psums.unsqueeze(2).broadcast_to([P, NT, 2]), ALU.mult))
            dve.wait_ge(cum_ps, 1)
            o.done(dve.memset(base[:, 0, :], 0.0))
            o.done(dve.tensor_scalar(first_slot, iota_n[:, 0:EX], float(CAP), None, ALU.mult))
            o.done(dve.tensor_copy(cum, cum_bank.rearrange("p (t e) -> p t e", t=NT)))
            o.done(dve.tensor_copy(tot, tot_bank.rearrange("p (t e) -> p t e", t=NT)))
            o.wait()
            dve.sem_inc(counts_taken, 1)
            chunk(3)
            for t in range(1, NT):
                o.link(dve.tensor_tensor(base[:, t, :], base[:, t - 1, :], tot[:, t - 1, :], ALU.add))
            chunk(4)
            o.link(dve.tensor_tensor(count, base[:, NT - 1, :], tot[:, NT - 1, :], ALU.add))
            o.link(dve.tensor_reduce(most_f, count, AX.X, ALU.max))
            o.done(dve.tensor_copy(most[0:1, 0:1], most_f[0:1, :]))
            o.link(dve.tensor_tensor(cum, cum, base, ALU.add))
            o.link(dve.tensor_tensor(cum, cum, first_slot.unsqueeze(1).broadcast_to([P, NT, EX]), ALU.add))
            for k, pick in enumerate((pick0, pick1)):
                o.link(dve.tensor_tensor(weighed, pick, cum, ALU.mult))
                o.link(dve.tensor_reduce(slot_f[:, k, :], weighed, AX.X, ALU.add))
            dve.tensor_copy(slot_i, slot_f).then_inc(slots_ready, 1)
            chunk(5)
            o.link(dve.tensor_tensor(weighed, pick0, prob[:, :, 0:1].broadcast_to([P, NT, EX]), ALU.mult))
            o.link(dve.tensor_tensor(gates, pick1, prob[:, :, 1:2].broadcast_to([P, NT, EX]), ALU.mult))
            o.done(dve.tensor_tensor(gates, gates, weighed, ALU.add))
            chunk(6)
            chunk(7)
            for t in range(NT):
                dve.wait_ge(y_ps, t + 1)
                dve.tensor_tensor(xs[:, t, :], xs[:, t, :], psum[t][:, :], ALU.add).then_inc(y_sb, 1)

        @block.scalar
        def _(act):
            act.wait_ge(own, 2 * NT)
            act.activation(std, mv[:, :, 1], ACT.Sqrt, bias=eps).then_inc(stds, 1)
            for t in range(NT):
                cut = slice(t * P, (t + 1) * P)
                act.wait_ge(turned, t + 1)
                act.activation(hT[:, :, cut], psum[2 + t % 2][:, :].rearrange("p (c n) -> p c n", c=DC),
                               ACT.Copy).then_inc(moved, 1)
                act.wait_ge(moved, t + 1)
                act.activation(rows_T[0][:, :, cut], hT[:, :, cut], ACT.Copy).then_inc(rows_hi, 1)

            def weights_hi(m, n):
                if n == 0:
                    act.wait_ge(shared_in[m // UM], 48)
                    if m >= 2:
                        act.wait_ge(a_ps, 4 * (m - 1))
                act.activation(split(n, m)[0], unit(n, shared[n][0], m), ACT.Copy).then_inc(split_hi, 1)

            for n in range(3):
                weights_hi(0, n)
            for m in range(HC):
                for n in range(3):
                    if m + 1 < HC:
                        weights_hi(m + 1, n)
                    if n < 2:
                        i = 2 * m + n
                        act.wait_ge(a_ps, 2 * i + 1)
                        if i >= 2:
                            act.wait_ge(b_sb, i - 1)
                        act.activation(gated[i % 2], up_bank[2 * i % 3][:, 0:HALF], ACT.Silu).then_inc(a_sb, 1)
                act.wait_ge(b_sb, 2 * m + 2)
                act.activation(hid[m % 2][0], h32[m % 2], ACT.Copy).then_inc(h_hi, 1)
                if m == 1:
                    act.wait_ge(best, 1)
                    act.activation(prob, top[:, :, 0:2], ACT.Exp, scale=-1.0).then_inc(exp_out, 1)

        @block.tensor
        def _(pe):
            pe.wait_ge(vec_in, 32)
            for c in range(DC):
                last = pe.transpose(gate_ps[:, c * EX:(c + 1) * EX], gate_row[:, c * P:(c + 1) * P],
                                    ident[0:EX, 0:EX])
            last.then_inc(gate_turned, 1)
            for t in range(NT):
                pe.wait_ge(rows, t + 1)
                if t >= 2:
                    pe.wait_ge(moved, t - 1)
                for c in range(DC):
                    last = pe.transpose(psum[2 + t % 2][:, c * P:(c + 1) * P], vs[:, t, c * P:(c + 1) * P],
                                        ident[:, :])
                last.then_inc(turned, 1)
            passes = ((0, 0), (0, 1), (1, 0))
            pe.wait_ge(rows_lo, NT)

            def up(m):
                for half in range(2):
                    for n in range(2):
                        k = 4 * m + 2 * half + n
                        if k == 14:
                            pe.wait_ge(counts_taken, 1)
                        if k >= 3:
                            pe.wait_ge(b_sb if (k - 3) % 2 else a_sb, (k - 3) // 2 + 1)
                        if half == 0:
                            pe.wait_ge(split_lo, 3 * m + n + 1)
                        for i, (wp, xp) in enumerate(passes):
                            for c in range(DC):
                                last = pe.matmul(up_bank[k % 3][:, 0:HALF], split(n, m)[wp][:, c, :],
                                                 rows_T[xp][:, c, half * HALF:(half + 1) * HALF],
                                                 start=i == 0 and c == 0, stop=i == 2 and c == DC - 1)
                        last.then_inc(a_ps, 1)

            def down(m):
                pe.wait_ge(h_lo, m + 1)
                pe.wait_ge(split_lo, 3 * m + 3)
                for t in range(NT):
                    for i, (hp, wp) in enumerate(passes):
                        last = pe.matmul(psum[t][:, :], hid[m % 2][hp][:, t * P:(t + 1) * P], split(2, m)[wp],
                                         start=m == 0 and i == 0, stop=m == HC - 1 and i == 2)
                    if m == HC - 1:
                        last.then_inc(y_ps, 1)

            pe.wait_ge(own, 2 * NT + 2)
            up(0)
            for t in range(NT):
                for c in range(DC):
                    last = pe.matmul(score_ps[:, t * EX:(t + 1) * EX], hT[:, c, t * P:(t + 1) * P], gate_t[:, c, :],
                                     start=c == 0, stop=c == DC - 1)
            last.then_inc(sc_ps, 1)
            for m in range(1, HC):
                up(m)
                if m == 1:
                    pe.wait_ge(own, 2 * NT + 3)
                down(m - 1)
                if m == 2:
                    pe.wait_ge(picks_ready, 1)
                    pe.wait_ge(b_sb, 2 * m + 2)
                    for lhs, bank in ((below, cum_bank), (ones, tot_bank)):
                        for t in range(NT):
                            n = P if t < NT - 1 else LAST
                            last = pe.matmul(bank[:, t * EX:(t + 1) * EX], lhs[0:n, :], picked[0:n, t, :], start=True,
                                             stop=True)
                    last.then_inc(cum_ps, 1)
            down(HC - 1)


def gate_views(gate_sb):
    return dict(gates=gate_sb[:, 0:NT * EX].rearrange("p (t e) -> p t e", t=NT),
                prob=gate_sb[:, 40:50].rearrange("p (t k) -> p t k", t=NT),
                slot_i=gate_sb[:, 60:70].bitcast(I32).rearrange("p (k t) -> p k t", k=2))


def expert_parts(slots, s, a, b, c):
    return ((slots[s].rearrange("p (c n) -> p c n", c=DC), a.rearrange("(c p) n -> p c n", p=P)),
            (slots[s + 1].rearrange("p (c n) -> p c n", c=DC), b.rearrange("(c p) n -> p c n", p=P)),
            (slots[s + 2].rearrange("p (c n) -> p c n", n=D), c.rearrange("(c p) n -> p c n", p=P)))


def one_expert(w, e):
    return w[bass.ds(e, 1), :, :].rearrange("a k n -> (a k) n")


def experts_routed(nc, sem, w_in, w1, w3, w2, rows_d, y_d, out, slots, xs, hT, vs, gate_sb, most, ident, psum):
    with ExitStack() as stage:
        def sb(name, shape, dt=F32):
            t = stage.enter_context(nc.sbuf_tensor(name, shape, dt))
            return t[(slice(None),) * len(shape)]

        parts = ("hi", "lo")
        w1s, w3s = ([[sb(f"{w}_{part}{i}", [P, DC, UW], F32R) for part in parts] for i in range(2)]
                    for w in ("w1", "w3"))
        w2s = [[sb(f"w2_{part}{i}", [P, UM, D], F32R) for part in parts] for i in range(4)]
        xT = [[sb(f"xT_{part}{i}", [P, DC, CAP], F32R) for part in parts] for i in range(2)]
        hid = [[sb(f"hidden_{part}{i}", [P, UM, CAP], F32R) for part in parts] for i in range(2)]
        h32 = [sb(f"hidden{i}", [P, UM, CAP]) for i in range(2)]
        gated = [sb(f"gated{i}", [P, CAP]) for i in range(UM)]
        y_st = [sb(f"y_stage{i}", [P, D]) for i in range(CB)]
        routed_units(nc, sem, w_in, w1, w3, w2, rows_d, y_d, out, slots, xs, hT, vs, gate_sb, most, ident, psum,
                     w1s, w3s, w2s, xT, hid, h32, gated, y_st)


def routed_units(nc, sem, w_in, w1, w3, w2, rows_d, y_d, out, slots, xs, hT, vs, gate_sb, most, ident, psum,
                 w1s, w3s, w2s, xT, hid, h32, gated, y_st):
    names = gate_views(gate_sb)
    prob, slot_i = names["prob"], names["slot_i"]
    got = (hT.rearrange("p c n -> p (c n)").rearrange("p (t n) -> p t n", t=NT), vs)
    xrow = [vs[:, 2 * k:2 * k + CB, :] for k in range(2)]
    raw1, raw3, raw2 = (p[0] for p in expert_parts(slots, 3, w1[0], w3[0], w2[0]))
    raw = [(raw1[:, :, u * UW:(u + 1) * UW], raw3[:, :, u * UW:(u + 1) * UW], raw2[:, u * UM:(u + 1) * UM, :])
           for u in range(UNITS)]
    (x_turned, x_hi, x_lo, w_hi_ready, w_lo_ready, a_ps, a_sb, b_sb, h_hi, h_lo, y_ps, y_sb, sums,
     stored) = map(sem, (
         "xe_turned", "xe_hi", "xe_lo", "w_hi_ready", "w_lo_ready", "re_a_ps", "re_a_sb", "re_b_sb",
         "h_hi", "h_lo", "re_y_ps", "re_y_sb", "re_sums", "re_stored"))
    x_in = [sem(f"xe_in{i}") for i in range(2)]
    raw_in = [sem(f"raw_in{i}") for i in range(UNITS)]
    y_out = [sem(f"y_out{i}") for i in range(CB)]
    got_in = [sem(f"got_in{i}") for i in range(NT)]
    PAIRS = EX // 2

    def wait_raw(eng, e, u):
        if isinstance(e, int) and e == 0:
            eng.wait_ge(w_in[0], 48)
        else:
            eng.wait_ge(raw_in[u], e * 48)

    with nc.Block() as block:
        @block.sync
        def _(sp):
            fullest = sp.value_load(most[0:1, 0:1], min_val=0, max_val=NP)
            with sp.If(fullest < CAP + 1):
                def number(v):
                    return v if isinstance(v, int) else sp.snap(v)

                def x_rows(first, k):
                    sp.dma_start(xrow[k], rows_d[bass.ds(first, CAP), :].rearrange("(b p) n -> p b n", p=P))\
                      .then_inc(x_in[k], 16)

                def store(first, blk):
                    sp.dma_start(y_d[bass.ds(first, P), :], y_st[blk]).then_inc(y_out[blk], 16)

                def expert(e, k, last):
                    next_e, x_first = number(e + 1), number((e + 2) * CAP)
                    split = [number((e * UNITS + u) * 3 + 3) for u in range(UNITS)]
                    y_first = [number((e - 1) * CAP + blk * P) for blk in range(CB)]
                    y_made = [number((e - 1) * CB + (blk + 1)) for blk in range(CB)]
                    if not last:
                        wait_past(sp, x_turned, e + 1)
                        x_rows(x_first, k)
                    for u in range(UNITS):
                        if not (last and k == 1):
                            wait_past(sp, w_lo_ready, split[u])
                            for to, frm in zip(raw[u], (
                                    one_expert(w1, next_e)[:, u * UW:(u + 1) * UW].rearrange("(c p) n -> p c n", p=P),
                                    one_expert(w3, next_e)[:, u * UW:(u + 1) * UW].rearrange("(c p) n -> p c n", p=P),
                                    one_expert(w2, next_e)[u * UW:(u + 1) * UW, :]
                                    .rearrange("(c p) n -> p c n", p=P))):
                                sp.dma_start(to, frm).then_inc(raw_in[u], 16)
                        if u == 2 and not (isinstance(e, int) and e == 0):
                            for blk in range(CB):
                                wait_past(sp, y_sb, y_made[blk])
                                store(y_first[blk], blk)

                def pair(j, last=False):
                    for k in range(2):
                        expert(j * 2 + k, k, last)

                x_rows(0, 0)
                x_rows(CAP, 1)
                pair(0)
                with sp.Fori(1, PAIRS - 1) as j:
                    pair(j)
                pair(PAIRS - 1, True)
                for blk in range(CB):
                    sp.wait_ge(y_sb, (EX - 1) * CB + (blk + 1))
                    store((EX - 1) * CAP + blk * P, blk)
                for t in range(NT):
                    n = P if t < NT - 1 else LAST
                    sp.wait_ge(sums, 2 * t + 2)
                    sp.dma_start(out[t * P:t * P + n, :], xs[0:n, t, :]).then_inc(stored, 16)
                sp.wait_ge(stored, 16 * NT)

        @block.gpsimd
        def _(pool):
            fullest = pool.value_load(most[0:1, 0:1], min_val=0, max_val=NP)
            with pool.If(fullest < CAP + 1):
                for blk in range(CB):
                    pool.wait_ge(y_out[blk], 16 * EX)
                for t in range(NT):
                    n = P if t < NT - 1 else LAST
                    for k in range(2):
                        pool.indirect_dma_start(
                            out=got[k][0:n, t, :], out_offset=None, in_=y_d,
                            in_offset=bass.IndirectOffsetOnAxis(ap=slot_i[0:n, k, t:t + 1], axis=0))\
                            .then_inc(got_in[t], 16)

        @block.vector
        def _(dve):
            fullest = dve.value_load(most[0:1, 0:1], min_val=0, max_val=NP)
            with dve.If(fullest < CAP + 1):
                def weights_lo(v, u, n):
                    to = ((w1s, w3s)[n][u % 2] if n < 2 else w2s[u])
                    wait_past(dve, w_hi_ready, v * 3 + (n + 1))
                    dve.tensor_tensor(to[1], raw[u][n], to[0], ALU.subtract).then_inc(w_lo_ready, 1)

                def rows_lo(e, k):
                    wait_past(dve, x_hi, e + 1)
                    for blk in range(CB):
                        last = dve.tensor_tensor(xT[k][1][:, :, blk * P:(blk + 1) * P],
                                                 psum[6 + blk][:, :].rearrange("p (c n) -> p c n", c=DC),
                                                 xT[k][0][:, :, blk * P:(blk + 1) * P], ALU.subtract)
                    last.then_inc(x_lo, 1)

                def hidden(v, u, m):
                    wait_past(dve, a_sb, v * UM + (m + 1))
                    wait_past(dve, a_ps, v * UM + (m + 1))
                    wait_past(dve, h_lo, v - 1)
                    dve.tensor_tensor(h32[u % 2][:, m, :], gated[m], psum[2 * m + 1][:, 0:CAP], ALU.mult)\
                       .then_inc(b_sb, 1)

                def results(e):
                    for blk in range(CB):
                        wait_past(dve, y_ps, e * CB + (blk + 1))
                        wait_past(dve, y_out[blk], e * 16)
                        dve.tensor_copy(y_st[blk], psum[4 + blk][:, :]).then_inc(y_sb, 1)

                def pair(j, last=False):
                    for k in range(2):
                        e = j * 2 + k
                        for u in range(UNITS):
                            v = e * UNITS + u
                            more = not (last and k == 1 and u == UNITS - 1)
                            for n in range(3):
                                if more:
                                    weights_lo(v + 1, (u + 1) % UNITS, n)
                                if (u, n) == (1, 0) and not (isinstance(e, int) and e == 0):
                                    results(e - 1)
                                if n < UM:
                                    hidden(v, u, n)
                            wait_past(dve, h_hi, v + 1)
                            dve.tensor_tensor(hid[u % 2][1], h32[u % 2], hid[u % 2][0], ALU.subtract)\
                               .then_inc(h_lo, 1)
                            if u == 2 and not (last and k == 1):
                                rows_lo(e + 1, 1 - k)

                rows_lo(0, 0)
                for n in range(3):
                    weights_lo(0, 0, n)
                pair(0)
                with dve.Fori(1, PAIRS - 1) as j:
                    pair(j)
                pair(PAIRS - 1, True)
                results(EX - 1)
                for t in range(NT):
                    n = P if t < NT - 1 else LAST
                    dve.wait_ge(got_in[t], 32)
                    for k in range(2):
                        if k:
                            dve.wait_ge(sums, 2 * t + 1)
                        dve.scalar_tensor_tensor(out=xs[0:n, t, :], in0=got[k][0:n, t, :],
                                                 scalar=prob[0:n, t, k:k + 1], in1=xs[0:n, t, :], op0=ALU.mult,
                                                 op1=ALU.add).then_inc(sums, 1)

        @block.scalar
        def _(act):
            fullest = act.value_load(most[0:1, 0:1], min_val=0, max_val=NP)
            with act.If(fullest < CAP + 1):
                def weights_hi(v, e, u, n):
                    to = ((w1s, w3s)[n][u % 2] if n < 2 else w2s[u])
                    if n == 0:
                        wait_raw(act, e, u)
                        wait_past(act, a_ps, (v - 1) * UM)
                    act.activation(to[0], raw[u][n], ACT.Copy).then_inc(w_hi_ready, 1)

                def rows_hi(e, k):
                    wait_past(act, x_turned, e + 1)
                    for blk in range(CB):
                        last = act.activation(xT[k][0][:, :, blk * P:(blk + 1) * P],
                                              psum[6 + blk][:, :].rearrange("p (c n) -> p c n", c=DC), ACT.Copy)
                    last.then_inc(x_hi, 1)

                def gate(v, m):
                    wait_past(act, a_ps, v * UM + (m + 1))
                    wait_past(act, b_sb, v * UM + (m + 1 - UM))
                    act.activation(gated[m], psum[2 * m][:, 0:CAP], ACT.Silu).then_inc(a_sb, 1)

                def pair(j, last=False):
                    for k in range(2):
                        e = j * 2 + k
                        for u in range(UNITS):
                            v = e * UNITS + u
                            more = not (last and k == 1 and u == UNITS - 1)
                            for n in range(3):
                                if more:
                                    weights_hi(v + 1, e + (u + 1) // UNITS, (u + 1) % UNITS, n)
                                if n < UM:
                                    gate(v, n)
                            wait_past(act, b_sb, v * UM + UM)
                            act.activation(hid[u % 2][0], h32[u % 2], ACT.Copy).then_inc(h_hi, 1)
                            if u == 2 and not (last and k == 1):
                                rows_hi(e + 1, 1 - k)

                rows_hi(0, 0)
                for n in range(3):
                    weights_hi(0, 0, 0, n)
                pair(0)
                with act.Fori(1, PAIRS - 1) as j:
                    pair(j)
                pair(PAIRS - 1, True)

        @block.tensor
        def _(pe):
            fullest = pe.value_load(most[0:1, 0:1], min_val=0, max_val=NP)
            with pe.If(fullest < CAP + 1):
                passes = ((0, 0), (0, 1), (1, 0))

                def turn(e, k, j):
                    wait_past(pe, x_in[k], j * 16 + 16)
                    wait_past(pe, x_lo, e)
                    for blk in range(CB):
                        for c in range(DC):
                            last = pe.transpose(psum[6 + blk][:, c * P:(c + 1) * P],
                                                xrow[k][:, blk, c * P:(c + 1) * P], ident[:, :])
                    last.then_inc(x_turned, 1)

                def up(v, e, k, u):
                    if u == 0:
                        wait_past(pe, x_lo, e + 1)
                    for m in range(UM):
                        wait_past(pe, b_sb, v * UM + (m + 1 - UM))
                        for n, w in enumerate((w1s, w3s)):
                            if m == 0:
                                wait_past(pe, w_lo_ready, v * 3 + (n + 1))
                            for i, (wp, xp) in enumerate(passes):
                                for c in range(DC):
                                    last = pe.matmul(psum[2 * m + n][:, 0:CAP], w[u % 2][wp][:, c, m * P:(m + 1) * P],
                                                     xT[k][xp][:, c, :], start=i == 0 and c == 0,
                                                     stop=i == 2 and c == DC - 1)
                        last.then_inc(a_ps, 1)

                def down(v, e, u):
                    wait_past(pe, h_lo, v + 1)
                    wait_past(pe, w_lo_ready, v * 3 + 3)
                    for blk in range(CB):
                        if u == 0:
                            wait_past(pe, y_sb, e * CB + (blk + 1 - CB))
                        for m in range(UM):
                            for i, (hp, wp) in enumerate(passes):
                                last = pe.matmul(psum[4 + blk][:, :], hid[u % 2][hp][:, m, blk * P:(blk + 1) * P],
                                                 w2s[u][wp][:, m, :], start=u == 0 and m == 0 and i == 0,
                                                 stop=u == UNITS - 1 and m == UM - 1 and i == 2)
                        if u == UNITS - 1:
                            last.then_inc(y_ps, 1)

                def pair(j, last=False):
                    for k in range(2):
                        e = j * 2 + k
                        for u in range(UNITS):
                            v = e * UNITS + u
                            up(v, e, k, u)
                            if u == 2 and not (last and k == 1):
                                turn(e + 1, 1 - k, j + k)
                            if u:
                                down(v - 1, e, u - 1)
                            elif not (isinstance(e, int) and e == 0):
                                down(v - 1, e - 1, UNITS - 1)

                turn(0, 0, 0)
                pair(0)
                with pe.Fori(1, PAIRS - 1) as j:
                    pair(j)
                pair(PAIRS - 1, True)
                down(EX * UNITS - 1, EX - 1, UNITS - 1)


def experts_all(nc, sem, w_in, w1, w3, w2, out, slots, big, xs, hT, work, gate_sb, most, psum):
    gates = gate_views(gate_sb)["gates"]
    gated = [work[:, 6 * D + i * HALF:6 * D + (i + 1) * HALF] for i in range(2)]
    (a_ps, a_sb, b_sb, y_ps, y_sb, stored) = map(sem, (
        "re_a_ps", "re_a_sb", "re_b_sb", "re_y_ps", "re_y_sb", "re_stored"))

    with nc.Block() as block:
        @block.sync
        def _(sp):
            fullest = sp.value_load(most[0:1, 0:1], min_val=0, max_val=NP)
            with sp.If(fullest > CAP):
                for to, frm in expert_parts(slots, 0, w1[1], w3[1], w2[1]):
                    sp.dma_start(to, frm).then_inc(w_in[1], 16)
                with sp.Fori(0, EX // 2 - 1) as j:
                    for k in range(2):
                        e = j * 2 + k
                        next_e = sp.snap(e + 2)
                        used = sp.snap(e * NT + NT)
                        sp.wait_ge(y_ps, used)
                        for to, frm in expert_parts(slots, 3 - 3 * k, one_expert(w1, next_e), one_expert(w3, next_e),
                                                    one_expert(w2, next_e)):
                            sp.dma_start(to, frm).then_inc(w_in[k], 16)
                full, rest = node_tiles(out)
                sp.wait_ge(y_sb, NT * EX)
                sp.dma_start(full, xs[:, 0:NT - 1, :]).then_inc(stored, 16)
                sp.dma_start(rest, xs[0:LAST, NT - 1, :]).then_inc(stored, 16)
                sp.wait_ge(stored, 32)

        @block.vector
        def _(dve):
            fullest = dve.value_load(most[0:1, 0:1], min_val=0, max_val=NP)
            with dve.If(fullest > CAP):
                def expert(e, k):
                    for m in range(HC):
                        for half in range(2):
                            i = 2 * m + half
                            wait_past(dve, a_sb, e * (2 * HC) + (i + 1))
                            wait_past(dve, a_ps, e * (2 * HC) + (i + 1))
                            dve.tensor_tensor(big[:, HC * k + m, half * HALF:(half + 1) * HALF], gated[i % 2],
                                              psum[2 * (i % 2) + 1][:, 0:HALF], ALU.mult).then_inc(b_sb, 1)
                    for t in range(NT):
                        wait_past(dve, y_ps, e * NT + (t + 1))
                        wait_past(dve, y_sb, e * NT + (t + 1 - NT))
                        dve.scalar_tensor_tensor(out=xs[:, t, :], in0=psum[4 + t % 2][:, :],
                                                 scalar=gates[:, t, bass.ds(e, 1)], in1=xs[:, t, :],
                                                 op0=ALU.mult, op1=ALU.add).then_inc(y_sb, 1)

                for k in range(2):
                    expert(k, k)
                with dve.Fori(1, EX // 2) as j:
                    for k in range(2):
                        expert(j * 2 + k, k)

        @block.scalar
        def _(act):
            fullest = act.value_load(most[0:1, 0:1], min_val=0, max_val=NP)
            with act.If(fullest > CAP):
                def expert(e):
                    for i in range(2 * HC):
                        wait_past(act, a_ps, e * (2 * HC) + (i + 1))
                        wait_past(act, b_sb, e * (2 * HC) + (i - 1))
                        act.activation(gated[i % 2], psum[2 * (i % 2)][:, 0:HALF], ACT.Silu).then_inc(a_sb, 1)

                for k in range(2):
                    expert(k)
                with act.Fori(1, EX // 2) as j:
                    for k in range(2):
                        expert(j * 2 + k)

        @block.tensor
        def _(pe):
            fullest = pe.value_load(most[0:1, 0:1], min_val=0, max_val=NP)
            with pe.If(fullest > CAP):
                def expert(e, k, j):
                    a, b, c3 = (p[0] for p in expert_parts(slots, 3 - 3 * k, w1[0], w3[0], w2[0]))
                    wait_past(pe, w_in[k], j * 48 + 48)
                    for m in range(HC):
                        for half in range(2):
                            i = 2 * m + half
                            wait_past(pe, b_sb, e * (2 * HC) + (i - 1))
                            for w, bank in ((a, 2 * (i % 2)), (b, 2 * (i % 2) + 1)):
                                for c in range(DC):
                                    last = pe.matmul(psum[bank][:, 0:HALF], w[:, c, m * P:(m + 1) * P],
                                                     hT[:, c, half * HALF:(half + 1) * HALF], start=c == 0,
                                                     stop=c == DC - 1)
                            last.then_inc(a_ps, 1)
                    wait_past(pe, b_sb, e * (2 * HC) + 2 * HC)
                    for t in range(NT):
                        wait_past(pe, y_sb, e * NT + (t - 1))
                        for m in range(HC):
                            last = pe.matmul(psum[4 + t % 2][:, :], big[:, HC * k + m, t * P:(t + 1) * P],
                                             c3[:, m, :], start=m == 0, stop=m == HC - 1)
                        last.then_inc(y_ps, 1)

                for k in range(2):
                    expert(k, k, 0)
                with pe.Fori(1, EX // 2) as j:
                    for k in range(2):
                        expert(j * 2 + k, k, j)


def attention_any(nc, sem, rec_d, logits_d, big, hT, vs, iota_n, ident, ones, tab, small, psum):
    with ExitStack() as stage:
        def sb(name, shape):
            t = stage.enter_context(nc.sbuf_tensor(name, shape, F32))
            return t[(slice(None),) * len(shape)]

        attention_chunks(nc, sem, rec_d, logits_d, big, hT, vs, iota_n, ident, ones, tab, small, psum,
                         sb("any_biases", [P, CT, P]), sb("any_bias_exp", [P, CT, P]), sb("any_onehot", [P, CT, NP]),
                         sb("any_logits", [P, NP]), sb("any_exponents", [P, NP]), sb("any_weights", [P, NP]),
                         sb("any_largest", [P, 2, P]), sb("any_records", [P, CT, REC]), sb("any_miss", [P, CT, BN]),
                         sb("any_minus_big", [P, 1]), sb("any_diag", [P, P]), sb("any_zeros", [P, P]))


def attention_chunks(nc, sem, rec_d, logits_d, big, hT, vs, iota_n, ident, ones, tab, small, psum,
                     X, R, onehot, S, L, PR, XM, rec, miss, minus_big, diag, zeros):
    NCH = -(-NE // CHUNK)
    PT = big[:, 8:16, :].rearrange("p a n -> p (a n)").rearrange("p (t h d) -> p t h d", t=NT, h=H)
    tiny = small[:, 0:1]
    guard, nguard, total, inv, worst = (small[:, k:k + 1] for k in range(1, 6))
    psT, psM = psum[0][:, 0:P], psum[0][:, P:2 * P]
    lo, hi = psum[1], psum[2]
    psP = (psum[5], psum[6])
    psO = psum[7]
    names = ("consts poolown rec_in x_made chunk_used xm_ready xm_turned own worst_ready diag_ready rep_ready "
             "d_done oh_ready r_ready w_ready s_in l_ready g_ready e_ready p_made inv_ready p_ready p_turned pt_ready "
             "o_ready o_moved w_closed").split()
    (consts, poolown, rec_in, x_made, chunk_used, xm_ready, xm_turned, own, worst_ready, diag_ready,
     rep_ready, d_done, oh_ready, r_ready, w_ready, s_in, l_ready, g_ready, e_ready, p_made, inv_ready, p_ready,
     p_turned, pt_ready, o_ready, o_moved, w_closed) = (
         sem("any_" + n if n in ("rec_in", "x_made", "chunk_used", "s_in", "w_closed") else
             f"at_{n}" if n in ("consts", "poolown", "own") else n) for n in names)

    with nc.Block() as block:
        @block.sync
        def _(sp):
            longest = sp.value_load(tab[0:1, 2 * NB:2 * NB + 1], min_val=-NE, max_val=NE)
            with sp.If(longest > CHUNK):
                with sp.Fori(0, NB) as b:
                    row = sp.snap(b * (P * NP))
                    blocks_done = sp.snap(b + 1)
                    sp.wait_ge(e_ready, blocks_done)
                    sp.dma_start(S, logits_d.rearrange("b h l s -> (b h l s)")[bass.ds(row, P * NP)]
                                 .rearrange("(p n) -> p n", p=P)).then_inc(s_in, 16)
                    for sweep in range(2):
                        with sp.Fori(0, NCH) as c:
                            at = sp.snap(c * (CHUNK * REC))
                            used = sp.snap(b * (2 * NCH) + (c + (sweep * NCH + 1)))
                            sp.wait_ge(chunk_used, used)
                            sp.dma_start(rec.rearrange("p t c -> p (t c)"),
                                         rec_d.rearrange("e c -> (e c)")[bass.ds(at, CHUNK * REC)]
                                         .rearrange("(p n) -> p n", p=P)).then_inc(rec_in, 16)

        @block.gpsimd
        def _(pool):
            longest = pool.value_load(tab[0:1, 2 * NB:2 * NB + 1], min_val=-NE, max_val=NE)
            with pool.If(longest > CHUNK):
                pool.memset(minus_big, -BIG).then_inc(consts, 1)
                pool.memset(zeros, 0.0).then_inc(consts, 1)
                pool.memset(tiny, TINY).then_inc(consts, 1)
                pool.wait_ge(consts, 3)
                with pool.Fori(0, NB) as b:
                    for sweep in range(2):
                        with pool.Fori(0, NCH) as c:
                            v = b * (2 * NCH) + (c + sweep * NCH)
                            pool.wait_ge(rec_in, v * 16 + 16)
                            pool.tensor_tensor(miss, rec[:, :, 1:2].broadcast_to([P, CT, BN]),
                                               iota_n[:, bass.ds(b * BN, BN)].unsqueeze(1).broadcast_to([P, CT, BN]),
                                               ALU.subtract).then_inc(poolown, 1)
                            pool.wait_ge(poolown, v * 3 + 1)
                            pool.tensor_tensor(miss, miss, miss, ALU.mult).then_inc(poolown, 1)
                            pool.wait_ge(poolown, v * 3 + 2)
                            pool.tensor_tensor(miss, miss, minus_big.unsqueeze(1).broadcast_to([P, CT, BN]),
                                               ALU.mult).then_inc(poolown, 1)
                            pool.wait_ge(poolown, v * 3 + 3)
                            pool.tensor_tensor(X.rearrange("p t (h d) -> p t h d", h=H),
                                               rec[:, :, 2:REC].unsqueeze(3).broadcast_to([P, CT, H, BN]),
                                               miss.unsqueeze(2).broadcast_to([P, CT, H, BN]), ALU.add)\
                                .then_inc(x_made, 1)

        @block.vector
        def _(dve):
            longest = dve.value_load(tab[0:1, 2 * NB:2 * NB + 1], min_val=-NE, max_val=NE)
            with dve.If(longest > CHUNK):
                for s in (chunk_used, inv_ready):
                    dve.sem_inc(s, 1)
                dve.wait_ge(consts, 3)
                with dve.Fori(0, NB) as b:
                    dve.wait_ge(xm_turned, b + 1)
                    dve.memset(XM[:, 0, :], -BIG).then_inc(own, 1)
                    with dve.Fori(0, NCH) as c:
                        v = b * (2 * NCH) + c
                        u = b * (2 * NCH + 4) + c * 2
                        dve.wait_ge(x_made, v + 1)
                        dve.wait_ge(own, u + 1)
                        dve.tensor_reduce(XM[:, 1, :], X.rearrange("p t m -> p m t"), AX.X, ALU.max).then_inc(own, 1)
                        dve.wait_ge(own, u + 2)
                        dve.tensor_tensor(XM[:, 0, :], XM[:, 0, :], XM[:, 1, :], ALU.max).then_inc(own, 1)
                        dve.wait_ge(own, u + 3)
                        dve.sem_inc(chunk_used, 1)
                    dve.sem_inc(xm_ready, 1)
                    dve.wait_ge(xm_turned, b + 2)
                    dve.tensor_reduce(worst, psT, AX.X, ALU.max).then_inc(worst_ready, 1)
                    dve.wait_ge(worst_ready, b + 1)
                    dve.tensor_scalar(diag, ident[:, :], worst, -BIG / 10, ALU.mult, ALU.max).then_inc(diag_ready, 1)
                    with dve.Fori(0, NCH) as c:
                        v = b * (2 * NCH) + (c + NCH)
                        dve.wait_ge(rep_ready, b + 1)
                        dve.wait_ge(x_made, v + 1)
                        dve.tensor_tensor(X, X, psM.unsqueeze(1).broadcast_to([P, CT, P]), ALU.subtract)\
                           .then_inc(d_done, 1)
                        dve.wait_ge(w_ready, b * NCH + (c + 1))
                        for t in range(CT):
                            dve.tensor_scalar(onehot[:, t, :], iota_n[:, :], rec[:, t, 0:1], None, ALU.is_equal)\
                               .then_inc(oh_ready, 1)
                        dve.wait_ge(w_ready, b * NCH + (c + 2))
                        dve.sem_inc(chunk_used, 1)
                    dve.wait_ge(l_ready, b + 1)
                    dve.wait_ge(s_in, b * 16 + 16)
                    dve.tensor_tensor(L, L, S, ALU.add).then_inc(own, 1)
                    dve.wait_ge(own, b * (2 * NCH + 4) + (2 * NCH + 2))
                    dve.tensor_reduce(nguard, L, AX.X, ALU.max, negate=True).then_inc(g_ready, 1)
                    dve.wait_ge(e_ready, b + 2)
                    dve.wait_ge(p_turned, b + 1)
                    dve.tensor_tensor_reduce(PR[:, 0:HALF], lo[:, 0:HALF], L[:, 0:HALF], 1.0, 0.0, ALU.mult, ALU.add,
                                             total).then_inc(own, 1)
                    dve.wait_ge(own, b * (2 * NCH + 4) + (2 * NCH + 3))
                    dve.tensor_tensor_reduce(PR[:, HALF:NP], hi[:, 0:HALF], L[:, HALF:NP], 1.0, total, ALU.mult,
                                             ALU.add, guard).then_inc(own, 1)
                    dve.wait_ge(own, b * (2 * NCH + 4) + (2 * NCH + 4))
                    dve.tensor_scalar(total, guard, 1e-37, None, ALU.max).then_inc(p_made, 1)
                    dve.wait_ge(p_made, b + 1)
                    dve.reciprocal(inv, total).then_inc(inv_ready, 1)

        @block.scalar
        def _(act):
            longest = act.value_load(tab[0:1, 2 * NB:2 * NB + 1], min_val=-NE, max_val=NE)
            with act.If(longest > CHUNK):
                for s in (e_ready, pt_ready, o_moved):
                    act.sem_inc(s, 1)
                act.preload_act_table_set("natural_log_exp_and_others")
                act.wait_ge(consts, 3)
                with act.Fori(0, NT) as j:
                    with act.Fori(0, BPT) as k:
                        b = j * BPT + k
                        with act.Fori(0, NCH) as c:
                            act.wait_ge(d_done, b * NCH + (c + 1))
                            act.wait_ge(w_ready, b * NCH + (c + 1))
                            act.activation(R, X, ACT.Exp).then_inc(r_ready, 1)
                        act.wait_ge(w_closed, b + 1)
                        act.wait_ge(inv_ready, b + 1)
                        act.activation(L[:, 0:HALF], lo[:, 0:HALF], ACT.Ln, bias=tiny)
                        act.activation(L[:, HALF:NP], hi[:, 0:HALF], ACT.Ln, bias=tiny).then_inc(l_ready, 1)
                        act.wait_ge(g_ready, b + 1)
                        act.activation(L, S, ACT.Exp, bias=nguard).then_inc(e_ready, 1)
                        act.wait_ge(inv_ready, b + 2)
                        act.activation(PR, PR, ACT.Copy, scale=inv).then_inc(p_ready, 1)
                        act.wait_ge(p_turned, b + 2)
                        act.wait_ge(o_ready, j + 1)
                        first = psP[0][:, :].rearrange("s (t h d) -> s t h d", t=4, h=H)
                        for t in range(4):
                            act.activation(PT[:, t, :, bass.ds(k * BN, BN)], first[:, t], ACT.Copy)
                        act.activation(PT[:, 4, :, bass.ds(k * BN, BN)],
                                       psP[1][:, 0:P].rearrange("s (h d) -> s h d", h=H), ACT.Copy)\
                           .then_inc(pt_ready, 1)
                    act.wait_ge(o_ready, j + 2)
                    act.activation(hT[:, :, bass.ds(j * P, P)], psO[:, :].rearrange("p (c d) -> p c d", c=DC),
                                   ACT.Copy).then_inc(o_moved, 1)

        @block.tensor
        def _(pe):
            longest = pe.value_load(tab[0:1, 2 * NB:2 * NB + 1], min_val=-NE, max_val=NE)
            with pe.If(longest > CHUNK):
                for s in (w_ready, xm_turned, p_turned, o_ready):
                    pe.sem_inc(s, 1)
                pe.wait_ge(consts, 3)
                with pe.Fori(0, NT) as j:
                    with pe.Fori(0, BPT) as k:
                        b = j * BPT + k
                        pe.wait_ge(xm_ready, b + 1)
                        pe.transpose(psT, XM[:, 0, :], ident[:, :]).then_inc(xm_turned, 1)
                        pe.wait_ge(diag_ready, b + 1)
                        pe.matmul(psM, ones[:, :], diag, start=True, stop=True).then_inc(rep_ready, 1)
                        pe.wait_ge(inv_ready, b + 1)
                        pe.matmul(lo[:, 0:HALF], zeros, iota_n[:, 0:HALF], start=True, stop=False)
                        pe.matmul(hi[:, 0:HALF], zeros, iota_n[:, 0:HALF], start=True, stop=False)
                        with pe.Fori(0, NCH) as c:
                            v = b * NCH + c
                            pe.wait_ge(r_ready, v + 1)
                            pe.wait_ge(oh_ready, v * CT + CT)
                            for t in range(CT):
                                pe.matmul(lo[:, 0:HALF], R[:, t, :], onehot[:, t, 0:HALF], start=False, stop=False)
                                last = pe.matmul(hi[:, 0:HALF], R[:, t, :], onehot[:, t, HALF:NP], start=False,
                                                 stop=False)
                            last.then_inc(w_ready, 1)
                        pe.matmul(lo[:, 0:HALF], zeros, iota_n[:, 0:HALF], start=False, stop=True)
                        pe.matmul(hi[:, 0:HALF], zeros, iota_n[:, 0:HALF], start=False, stop=True)\
                          .then_inc(w_closed, 1)
                        pe.wait_ge(p_ready, b + 1)
                        pe.wait_ge(pt_ready, b + 1)
                        for t in range(NT):
                            to = psP[t // 4][:, (t % 4) * P:(t % 4 + 1) * P]
                            last = pe.transpose(to, PR[:, t * P:(t + 1) * P], ident[:, :])
                        last.then_inc(p_turned, 1)
                    pe.wait_ge(pt_ready, j * BPT + (BPT + 1))
                    pe.wait_ge(o_moved, j + 1)
                    for h in range(H):
                        r = slice(DH * (h % 2), DH * (h % 2 + 1))
                        for t in range(NT):
                            last = pe.matmul(psO[r, (h // 2) * P:(h // 2 + 1) * P], vs[:, t, h * DH:(h + 1) * DH],
                                             PT[:, t, h, :], start=t == 0, stop=t == NT - 1)
                    last.then_inc(o_ready, 1)


_INS = ['x', 'src', 'dst', 'edge_attr_8', 'edge_attr_8_n2', 'L0_gnn_Wqkv', 'L0_gnn_bqkv', 'L0_gnn_Wo', 'L0_gnn_bo',
        'L0_gnn_ln1_g', 'L0_gnn_ln1_b', 'L0_gnn_W1', 'L0_gnn_b1', 'L0_gnn_W2', 'L0_gnn_b2', 'L0_gnn_ln2_g',
        'L0_gnn_ln2_b', 'L0_ffn_gate_w', 'L0_ffn_biases', 'L0_ffn_w1', 'L0_ffn_w3', 'L0_ffn_w2', 'L0_ffn_sw1',
        'L0_ffn_sw3', 'L0_ffn_sw2']


def kernel(**inputs):
    import numpy as _np
    import concourse.bacc as _bacc
    from concourse import mybir as _mybir
    from concourse.bass_utils import run_bass_kernel_spmd as _run

    nc = _bacc.Bacc("TRN2", target_bir_lowering=False, num_devices=1)
    arrays, args = {}, []
    for name in _INS:
        a = _np.ascontiguousarray(inputs[name])
        arrays[f"in_{name}"] = a
        args.append(nc.dram_tensor(f"in_{name}", a.shape, _mybir.dt.from_np(a.dtype), kind="ExternalInput").ap())
    out = nc.dram_tensor("out", (N, D), F32, kind="ExternalOutput").ap()
    program(nc, *args, out)
    r = _run(nc, [arrays], core_ids=[0])
    return r.results[0]["out"]
```
